# Optimizing a Trainium2 kernel written in Bass

```python
import numpy as np
import jax
import jax.numpy as jnp

def _softmax(x, axis=-1):
    return jax.nn.softmax(x, axis=axis)

def _gelu(x):
    return jax.nn.gelu(x, approximate=True)

def _silu(x):
    return jax.nn.silu(x)

def _sigmoid(x):
    return jax.nn.sigmoid(x)

def _layernorm(x, axis=-1, eps=1e-05):
    m = jnp.mean(x, axis=axis, keepdims=True)
    v = jnp.var(x, axis=axis, keepdims=True)
    return (x - m) / jnp.sqrt(v + eps)

def _scatter_add(tgt, idx, src, axis=0):
    return tgt.at[idx].add(src)

def _segment_sum(src, seg, n):
    return jax.ops.segment_sum(src, seg, n)
kernel_name = 'mk_gps_d1_gnn_r8_dbdb60'

def setup_inputs(seed: int=0):
    np.random.seed(seed)
    _w = jnp.asarray

    def _rec_inputs():
        import jax
        import jax.numpy as jnp
        _gk = jax.random.key(seed)
        x = -6.415e-05 + 1 * jax.random.normal(jax.random.fold_in(_gk, 1), (1250, 1024), jnp.float32)
        src = jax.random.randint(jax.random.fold_in(_gk, 2), (20000,), 0, 1250, jnp.int32)
        dst = jnp.minimum((1250 * jax.random.uniform(jax.random.fold_in(_gk, 3), (20000,)) ** 2.0).astype(jnp.int32), 9999)
        _o = jnp.argsort(dst, stable=True)
        src = src[_o]
        dst = dst[_o]
        return (x, src, dst)
    x, src, dst = _rec_inputs()

    def _L0_gnn_setup():
        import jax, jax.numpy as jnp
        import numpy as np
        NEG_SLOPE = 0.1
        EPS = 1e-05
        key = jax.random.key(seed)
        k1, k2, k3, k4, k5 = jax.random.split(key, 5)
        N, E, DIN, DOUT = (1250, 20000, 1024, 1024)
        x = jax.random.normal(k1, (N, DIN), dtype=jnp.float32)
        W = jax.random.normal(k2, (DIN, DOUT), dtype=jnp.float32) * 0.02
        a = jax.random.normal(k3, (1, 2 * DOUT), dtype=jnp.float32) * 0.02
        src = jax.random.randint(k4, (E,), 0, N, dtype=jnp.int64)
        dst = jax.random.randint(k5, (E,), 0, N, dtype=jnp.int64)
        return {'x': x, 'W': W, 'a': a, 'src': src, 'dst': dst}
    _L0_gnn_all = _L0_gnn_setup()
    _L0_gnn_in = {k: v for k, v in _L0_gnn_all.items() if k in ('W', 'a')}
    del _L0_gnn_all

    def _L0_mix_setup():
        import jax, jax.numpy as jnp
        import numpy as np
        B, N, D = (4, 512, 1024)
        key = jax.random.key(seed)
        kx, kql, kqr, kk, kv = jax.random.split(key, 5)
        std = 1.0 / D
        return {'x': jax.random.normal(kx, (B, N, D), dtype=jnp.float32), 'w_query_left': jax.random.normal(kql, (D, D), dtype=jnp.float32) * std, 'w_query_right': jax.random.normal(kqr, (D, D), dtype=jnp.float32) * std, 'w_key': jax.random.normal(kk, (D, D), dtype=jnp.float32) * std, 'w_value': jax.random.normal(kv, (D, D), dtype=jnp.float32) * std}
    _L0_mix_all = _L0_mix_setup()
    _L0_mix_in = {k: v for k, v in _L0_mix_all.items() if k in ('w_query_left', 'w_query_right', 'w_key', 'w_value')}
    del _L0_mix_all

    def _L0_ffn_setup():
        import jax, jax.numpy as jnp
        import numpy as np
        B, S, D, E, K = (4, 256, 1024, 8, 2)
        EPS, W_THRES, TEMP = (0.0001, 0.1, 1.0)
        key = jax.random.key(seed)
        k1, k2, k3, k4, k5 = jax.random.split(key, 5)
        x = jax.random.normal(k1, (B, S, D), dtype=jnp.float32)
        gate_W = jax.random.normal(k2, (D, E), dtype=jnp.float32) * 0.02
        gate_b = jnp.zeros((E,), dtype=jnp.float32)
        expert_W = jax.random.normal(k3, (E, D, D), dtype=jnp.float32) * 0.02
        expert_b = jnp.zeros((E, D), dtype=jnp.float32)
        return {'x': x, 'gate_W': gate_W, 'gate_b': gate_b, 'expert_W': expert_W, 'expert_b': expert_b}
    _L0_ffn_all = _L0_ffn_setup()
    _L0_ffn_in = {k: v for k, v in _L0_ffn_all.items() if k in ('gate_W', 'gate_b', 'expert_W', 'expert_b')}
    del _L0_ffn_all
    return {'x': x, 'src': src, 'dst': dst, 'L0_gnn_W': _L0_gnn_in['W'], 'L0_gnn_a': _L0_gnn_in['a'], 'L0_mix_w_query_left': _L0_mix_in['w_query_left'], 'L0_mix_w_query_right': _L0_mix_in['w_query_right'], 'L0_mix_w_key': _L0_mix_in['w_key'], 'L0_mix_w_value': _L0_mix_in['w_value'], 'L0_ffn_gate_W': _L0_ffn_in['gate_W'], 'L0_ffn_gate_b': _L0_ffn_in['gate_b'], 'L0_ffn_expert_W': _L0_ffn_in['expert_W'], 'L0_ffn_expert_b': _L0_ffn_in['expert_b']}

def reference(x, src, dst, L0_gnn_W, L0_gnn_a, L0_mix_w_query_left, L0_mix_w_query_right, L0_mix_w_key, L0_mix_w_value, L0_ffn_gate_W, L0_ffn_gate_b, L0_ffn_expert_W, L0_ffn_expert_b):
    import jax
    import jax.numpy as jnp

    def _L0_gnn_ref(x, W, a, src, dst):
        import jax, jax.numpy as jnp
        import numpy as np
        NEG_SLOPE = 0.1
        EPS = 1e-05
        N = x.shape[0]
        d = W.shape[1]
        h = x @ W
        a_l, a_r = (a[0, :d], a[0, d:])
        al = h @ a_l
        ar = h @ a_r
        e = jnp.exp(-jax.nn.leaky_relu(al[src] + ar[dst], negative_slope=NEG_SLOPE))
        rowsum = jax.ops.segment_sum(e, src, num_segments=N)
        h_prime = jax.ops.segment_sum(e[:, None] * h[dst], src, num_segments=N)
        h_prime = h_prime / (rowsum[:, None] + EPS)
        return jax.nn.elu(h_prime)

    def _L0_mix_ref(x, w_query_left, w_query_right, w_key, w_value):
        import jax, jax.numpy as jnp
        import numpy as np
        B, N, D = (4, 512, 1024)
        query_left = jnp.einsum('bnd,de->bne', x, w_query_left)
        query_right = jnp.einsum('bnd,de->bne', x, w_query_right)
        key = jnp.einsum('bnd,de->bne', x, w_key)
        value = jnp.einsum('bnd,de->bne', x, w_value)
        query = query_left * query_right
        kv_attn = jnp.einsum('bnd,bne->bde', key, value)
        linear_attn = jnp.einsum('bnd,bde->bne', query, kv_attn)
        return linear_attn

    def _L0_ffn_ref(x, gate_W, gate_b, expert_W, expert_b):
        import jax, jax.numpy as jnp
        import numpy as np
        B, S, D, E, K = (4, 256, 1024, 8, 2)
        EPS, W_THRES, TEMP = (0.0001, 0.1, 1.0)
        scores = jnp.maximum((x @ gate_W + gate_b) / TEMP, EPS)
        p = jax.nn.softmax(scores, axis=-1)
        _, topk_idx = jax.lax.top_k(p, K)
        topk_mask = jax.nn.one_hot(topk_idx, E, dtype=p.dtype).sum(-2) > 0
        w = jnp.maximum(p, W_THRES)
        w_gather = jnp.take_along_axis(w, topk_idx, axis=-1)
        total = jax.lax.stop_gradient(w_gather.sum(-1, keepdims=True))
        w = w / total
        comb = jnp.where(topk_mask, w, jnp.zeros_like(w))
        y = jnp.einsum('bsd,edf->bsef', x, expert_W) + expert_b
        out = jnp.einsum('bsef,bse->bsf', y, comb) / K
        return out
    xn = _layernorm(x, axis=-1)
    x = x + _L0_gnn_ref(xn, L0_gnn_W, L0_gnn_a, src, dst) + _L0_mix_ref(xn[None], L0_mix_w_query_left, L0_mix_w_query_right, L0_mix_w_key, L0_mix_w_value)[0]
    x = x + _L0_ffn_ref(_layernorm(x, axis=-1)[None], L0_ffn_gate_W, L0_ffn_gate_b, L0_ffn_expert_W, L0_ffn_expert_b)[0]
    return x

_drawn_inputs = setup_inputs


def setup_inputs(seed=0):
    import zlib

    import numpy as np

    out = dict(_drawn_inputs(seed))
    spreads = {'L0_ffn_gate_b': (0.0, 0.592), 'L0_ffn_expert_b': (0.0, 0.8)}
    factors = {'L0_mix_w_query_left': 8.0,
     'L0_mix_w_query_right': 8.0,
     'L0_mix_w_key': 8.0,
     'L0_mix_w_value': 8.0,
     'L0_gnn_a': 8.0}
    for name, (base, spread) in spreads.items():
        noise = np.random.default_rng([zlib.crc32(name.encode()), seed]).standard_normal(out[name].shape)
        drawn = base * np.exp(spread * noise) if base else spread * noise
        out[name] = jnp.asarray(drawn.astype(out[name].dtype))
    for name, factor in factors.items():
        out[name] = (out[name] * factor).astype(out[name].dtype)
    return out
```

```python
from contextlib import ExitStack

import concourse.bass as bass
from concourse import mybir


def gps_layer(nc, x, src, dst, gnn_W, gnn_a, w_ql, w_qr, w_key, w_value, gate_W, gate_b, expert_W, expert_b, out):
    f32, f32r = mybir.dt.float32, mybir.dt.float32r
    f16, i32 = mybir.dt.float16, mybir.dt.int32
    ALU, ACT, AX = mybir.AluOpType, mybir.ActivationFunctionType, mybir.AxisListType

    P = 128
    N, D = x.shape
    E = src.shape[0]
    NE = expert_b.shape[0]
    NT = (N + P - 1) // P
    KB = D // P
    HALF = 512
    NH = D // HALF
    MB = HALF // P
    ROWS = [min(P, N - t * P) for t in range(NT)]
    EP = 125
    EC = E // EP
    assert EP * EC == E and EC % 4 == 0
    NEG_SLOPE, GNN_EPS, LN_EPS, GATE_EPS, W_THRES, TOPK = 0.1, 1e-5, 1e-5, 1e-4, 0.1, 2
    F32_MAX = 3.4028234e38
    SCOLS = [(c, min(HALF, N - c)) for c in range(0, N, HALF)]

    base = (nc.sbuf_base + 31) // 32 * 32
    RING, BIG, ACC, RAW, QT, SMALL = 0, 16384, 36864, 47104, 49152, 52224

    ctx = ExitStack()
    with ctx:
        def at(name, word, shape, dt=f32):
            return nc.alloc_sbuf_tensor_at(name, shape, dt, offset=base + 4 * word)

        small_at = [SMALL]

        def small(name, shape, dt=f32):
            words = 1
            for s in shape[1:]:
                words *= s
            t = at(name, small_at[0], shape, dt)
            small_at[0] += (words + 7) // 8 * 8
            assert base + 4 * small_at[0] <= nc.sbuf_usable_end
            return t

        def sem(name):
            return ctx.enter_context(nc.semaphore(name))

        w_hi = [at(f"w_hi{s}", RING + 8192 * s, [P, KB, HALF], f32r) for s in range(2)]
        w_lo = [at(f"w_lo{s}", RING + 8192 * s + 4096, [P, KB, HALF], f32r) for s in range(2)]
        w_raw = at("w_raw", RAW, [P, 2, 2, HALF])
        acc = at("acc", ACC, [P, NT, D])
        xn_hi = at("xn_hi", BIG, [P, NT, D], f32r)
        xn_lo = at("xn_lo", BIG + 10240, [P, NT, D], f32r)
        UPPER = [sum(KB - i for i in range(m)) * P for m in range(KB)]
        NUP = UPPER[-1] + P
        LOWER = {}
        for m in range(KB):
            for n in range(m + 1, KB):
                LOWER[(n, m)] = len(LOWER) * P
        NLOW = len(LOWER) * P
        gu_hi = at("gu_hi", ACC, [P, NUP], f32r)
        gu_lo = at("gu_lo", ACC + NUP, [P, NUP], f32r)
        gl_hi = at("gl_hi", BIG, [P, NLOW], f32r)
        gl_lo = at("gl_lo", BIG + NLOW, [P, NLOW], f32r)
        T0 = BIG + 2 * NLOW
        t_hi = at("t_hi", T0, [P, KB, HALF], f32r)
        t_lo = at("t_lo", T0 + 4096, [P, KB, HALF], f32r)
        kv_out = at("kv_out", T0 + 8192, [P, 4, HALF])
        xt_hi = at("xt_hi", BIG, [P, KB, N], f32r)
        xt_lo = at("xt_lo", BIG + KB * N, [P, KB, N], f32r)
        qt_hi = at("qt_hi", QT, [P, 3, MB, P], f32r)
        qt_lo = at("qt_lo", QT + 1536, [P, 3, MB, P], f32r)
        a_bc = at("a_bc", QT, [P, 2 * D])
        a_junk = at("a_junk", QT + 2 * D, [P, D])
        h_hi = at("h_hi", BIG, [P, NT, D], f32r)
        h_lo = at("h_lo", BIG + 10240, [P, NT, D], f32r)
        cnt = at("cnt", RING, [P, NT, N])
        al_bc = at("al_bc", RING + 12504, [P, NT * P])
        hot_s = at("hot_s", QT, [P, 4, N], f16)
        hot_d = at("hot_d", QT + 2504, [P, 4, 2 * P], f16)
        nodes16 = at("nodes16", RAW, [P, NT * P], f16)
        src_i = at("src_i", RAW + 640, [P, EC], i32)
        dst_i = at("dst_i", RAW + 800, [P, EC], i32)
        src_f = at("src_f", RAW + 960, [P, EC])
        dst_f = at("dst_f", RAW + 1120, [P, EC])
        att = at("att", ACC, [P, 2, NT, P])
        att_hi = at("att_hi", ACC + 2560, [P, 2, NT, P], f32r)
        att_lo = at("att_lo", ACC + 5120, [P, 2, NT, P], f32r)
        hp = at("hp", ACC + 7680, [P, 2, D])
        mix_in = at("mix_in", RAW, [P, 2, D])
        x_in = at("x_in", QT, [P, 2, D])
        hneg = at("hneg", QT + 2 * D, [P, D])
        xn2 = at("xn2", QT, [P, 2, D])
        eb = at("eb", QT + 2 * D, [P, D])

        ident = small("ident", [P, P])
        ones = small("ones", [P, P])
        ones_r = small("ones_r", [P, 2], f32r)
        stats = small("stats", [P, 2, 6])
        mv = small("mv", [P, 2])
        mean = small("mean", [P, NT])
        rstd = small("rstd", [P, NT])
        nt1 = small("nt1", [P, 1])
        nt2 = small("nt2", [P, 1])
        al = small("al", [P, NT])
        ar = small("ar", [P, NT])
        rsum = small("rsum", [P, NT])
        gw = small("gw", [P, KB, NE])
        gw_hi = small("gw_hi", [P, KB, NE], f32r)
        gw_lo = small("gw_lo", [P, KB, NE], f32r)
        gb = small("gb", [P, NE])
        rank = small("rank", [P, NE])
        sc = small("sc", [P, NT, NE])
        g_p = at("g_p", RAW, [P, NT, NE])
        g_key = at("g_key", RAW + 80, [P, NT, NE])
        g_mask = at("g_mask", RAW + 160, [P, NT, NE])
        g_s2 = at("g_s2", RAW + 240, [P, NT, NE])
        g_m = at("g_m", RAW + 320, [P, NT])
        g_t = at("g_t", RAW + 336, [P, NT])
        comb = small("comb", [P, NT, NE])
        combT = at("combT", BIG + 2 * KB * N, [P, 2, P])

        ps = ctx.enter_context(nc.psum_tensor("ps", [P, 8, HALF], f32))

        kv_d = nc.dram_tensor("kv_d", (D, D), f32).ap()
        mix_d = nc.dram_tensor("mix_d", (N, D), f32).ap()
        x2_d = nc.dram_tensor("x2_d", (N, D), f32).ap()

        def half(w, h):
            return w.rearrange("(k p) n -> p k n", p=P)[:, :, h * HALF:(h + 1) * HALF]

        CH = [half(w_value, 0), half(w_key, 0), half(w_key, 1), half(w_value, 1), half(w_key, 0), half(w_key, 1),
              half(w_ql, 0), half(w_qr, 0), half(w_ql, 1), half(w_qr, 1), half(kv_d, 0), half(kv_d, 1),
              half(gnn_W, 0), half(gnn_W, 1)]
        C_KV, C_W, C_EXP = 10, 12, 14
        for e in range(NE):
            for h in range(NH):
                CH.append(half(expert_W[e], h))
        UNITS = 4

        owner, first = [], {}

        def phase(name, owners):
            first[name] = len(owner)
            owner.extend(owners)

        G_PIECES = []
        for m in range(KB):
            lo, width = m * P, D - m * P
            cut = [width] if width <= HALF else [HALF, width - HALF]
            for w in cut:
                G_PIECES.append((m, lo, w))
                lo += w
        phase("G", ["dve"] * len(G_PIECES))
        LOW_KEYS = list(LOWER)
        LOW_BANKS = [LOW_KEYS[i:i + 4] for i in range(0, len(LOW_KEYS), 4)]
        phase("LOW", ["act", "dve"] * len(LOW_BANKS))
        phase("T0", ["dve"] * KB)
        phase("KV0", ["dve"] * KB)
        phase("T1", ["dve"] * KB)
        phase("KV1", ["dve"] * KB)
        phase("XT", ["dve"] * (2 * NT))
        for h in range(NH):
            phase(f"QL{h}", ["act"] * NT)
            phase(f"QR{h}", ["dve"] * NT)
        phase("QTMIX", ["dve"] * (4 * NT))
        phase("H0", ["act"] * NT)
        phase("H1", ["act"] * NT)
        phase("AL", ["act"] * len(SCOLS))
        phase("GNN", ["dve", "act", "act"] * NT)
        phase("X2T", ["dve"] * (2 * NT))
        phase("GATE", ["dve"])
        phase("BIAS", ["act", "dve", "dve"] * NT)
        phase("EXP", ["dve"] * (NE * NH * NT))

        def released(n):
            return (s_free_act if owner[n] == "act" else s_free_dve), owner[:n + 1].count(owner[n])

        def qt_job(t, i):
            return first["QTMIX"] + (0 if t == 0 else 4 * t - 2) + i

        def mix_job(t, h):
            return first["QTMIX"] + (4 + 4 * t if t < NT - 1 else 4 * NT - 2) + h

        s_x = [sem(f"s_xt{t}") for t in range(NT)]
        s_raw = [sem(f"s_raw{i}") for i in range(2)]
        s_const, s_edges, s_a, s_gw, s_eb = (sem(n) for n in ("s_const", "s_edges", "s_a", "s_gw", "s_eb"))
        s_xn, s_xhi, s_xlo = sem("s_xn"), sem("s_xhi"), sem("s_xlo")
        s_whi, s_wlo = sem("s_whi"), sem("s_wlo")
        s_full, s_free_act, s_free_dve = sem("s_full"), sem("s_free_act"), sem("s_free_dve")
        s_hi = sem("s_hi")
        s_kvs = [sem(f"s_kvs{i}") for i in range(4)]
        s_xn2 = sem("s_xn2")
        s_mixs = sem("s_mixs")
        s_al, s_hhi, s_hlo = sem("s_al"), sem("s_hhi"), sem("s_hlo")
        s_diag = sem("s_diag")
        s_hot, s_hot_used, s_cnt_free = sem("s_hot"), sem("s_hot_used"), sem("s_cnt_free")
        s_z, s_e, s_att, s_atthi, s_attlo = sem("s_z"), sem("s_e"), sem("s_att"), sem("s_atthi"), sem("s_attlo")
        s_mx = [sem(f"s_mx{i}") for i in range(2)]
        s_rsum, s_neg, s_eneg, s_x2 = sem("s_rsum"), sem("s_neg"), sem("s_eneg"), sem("s_x2")
        s_x2s = [sem(f"s_x2s{i}") for i in range(2)]
        s_x2l = [sem(f"s_x2l{t}") for t in range(NT)]
        s_var, s_sd, s_gwhi, s_gwlo = sem("s_var"), sem("s_sd"), sem("s_gwhi"), sem("s_gwlo")
        s_gate, s_gexp, s_comb, s_combT = sem("s_gate"), sem("s_gexp"), sem("s_comb"), sem("s_combT")
        s_out = sem("s_out")
        s_chain = sem("s_chain")
        s_pool = sem("s_pool")

        block = ctx.enter_context(nc.Block())

        ring_free = {2: first["T0"] + KB, 3: first["KV0"] + 4, 4: first["KV0"] + KB, 5: first["T1"] + KB,
                     6: first["KV1"] + 4, 7: first["KV1"] + KB}
        for i in range(4):
            name = ["QL0", "QR0", "QL1", "QR1"][i]
            ring_free[8 + i] = first[name] + NT
        ring_free[12] = ring_free[13] = first["QTMIX"] + 4 * NT
        ring_free[14] = ring_free[15] = first["GNN"] + 3 * NT
        for c in range(16, len(CH)):
            ring_free[c] = first["EXP"] + (c - 15) * NT

        @block.sync
        def _(sp):
            def load_unit(u):
                c, r = divmod(u, UNITS)
                if u >= 2:
                    sp.wait_ge(s_wlo, u - 1)
                sp.dma_start(w_raw[:, u % 2], CH[c][:, 2 * r:2 * r + 2, :]).then_inc(s_raw[u % 2], 16)

            for t in range(NT):
                sp.dma_start(acc[0:ROWS[t], t, :], x[t * P:t * P + ROWS[t], :]).then_inc(s_x[t], 16)
            u = 0
            while u < 2 * UNITS + 2:
                load_unit(u)
                u += 1
            for h in range(NH):
                for m in range(KB):
                    sp.wait_ge(s_free_dve, released(first[f"KV{h}"] + m)[1])
                    sp.dma_start(kv_d[m * P:(m + 1) * P, h * HALF:(h + 1) * HALF], kv_out[:, m % 4]).then_inc(s_kvs[m % 4], 16)
                    load_unit(u)
                    u += 1
                if h == 0:
                    for _ in range(UNITS):
                        load_unit(u)
                        u += 1
                    sp.wait_ge(s_full, first["T1"] + KB)
                    for t in range(NT):
                        sp.dma_start(acc[0:ROWS[t], t, :], x[t * P:t * P + ROWS[t], :]).then_inc(s_x[t], 16)
            while u < UNITS * C_KV:
                load_unit(u)
                u += 1
            for s in s_kvs:
                sp.wait_ge(s, 16 * 2 * NH)
            while u < UNITS * C_W + 2:
                load_unit(u)
                u += 1
            for t in range(NT):
                sp.wait_ge(s_free_dve, released(mix_job(t, 1))[1])
                sp.dma_start(mix_d[t * P:t * P + ROWS[t], :], acc[0:ROWS[t], t, :]).then_inc(s_mixs, 16)
            sp.wait_ge(s_full, first["H0"])
            sp.dma_start(a_bc[:, :], gnn_a.partition_broadcast(P)).then_inc(s_a, 16)
            while u < UNITS * C_EXP:
                load_unit(u)
                u += 1
            sp.wait_ge(s_wlo, u)
            sp.dma_start(src_i[0:EP, :], src.rearrange("(p c) -> p c", c=EC)).then_inc(s_edges, 16)
            sp.dma_start(dst_i[0:EP, :], dst.rearrange("(p c) -> p c", c=EC)).then_inc(s_edges, 16)
            sp.wait_ge(s_mixs, 16 * NT)
            sp.wait_ge(s_hot_used, (NT // 2) * EC)
            for t in range(NT + 1):
                if t < NT:
                    if t >= 2:
                        sp.wait_ge(s_x2s[t % 2], 16 * (t // 2))
                    sp.dma_start(mix_in[0:ROWS[t], t % 2, :], mix_d[t * P:t * P + ROWS[t], :]).then_inc(s_mx[t % 2], 16)
                    sp.dma_start(x_in[0:ROWS[t], t % 2, :], x[t * P:t * P + ROWS[t], :]).then_inc(s_mx[t % 2], 16)
                if t >= 1:
                    i = t - 1
                    sp.wait_ge(s_x2, i + 1)
                    sp.dma_start(x2_d[i * P:i * P + ROWS[i], :], x_in[0:ROWS[i], i % 2, :]).then_inc(s_x2s[i % 2], 16)
            for i in range(2):
                sp.wait_ge(s_x2s[i], 16 * (NT // 2))
            for t in range(NT):
                sp.dma_start(acc[0:ROWS[t], t, :], x2_d[t * P:t * P + ROWS[t], :]).then_inc(s_x2l[t], 16)
            sp.dma_start(gw[:, :, :], gate_W.rearrange("(k p) e -> p k e", p=P)).then_inc(s_gw, 16)
            sp.dma_start(gb[:, :], gate_b.rearrange("(o e) -> o e", o=1).partition_broadcast(P)).then_inc(s_gw, 16)
            sp.dma_start(eb[0:NE, :], expert_b).then_inc(s_eb, 16)
            sp.wait_ge(s_comb, 1)
            while u < UNITS * len(CH):
                load_unit(u)
                u += 1
            for t in range(NT):
                sp.wait_ge(s_free_dve, released(first["EXP"] + (NE * NH - 1) * NT + t)[1])
                sp.dma_start(out[t * P:t * P + ROWS[t], :], acc[0:ROWS[t], t, :]).then_inc(s_out, 16)
            sp.wait_ge(s_out, 16 * NT)

        @block.gpsimd
        def _(pool):
            nc.gpsimd.memset(ident[:, :], 0.0).then_inc(s_pool, 1)
            nc.gpsimd.memset(ones[:, :], 1.0).then_inc(s_const, 1)
            pool.wait_ge(s_pool, 1)
            nc.gpsimd.affine_select(out=ident[:, :], in_=ident[:, :], compare_op=ALU.not_equal, fill=1.0,
                                    base=0, pattern=[[-1, P]], channel_multiplier=1).then_inc(s_const, 1)
            nc.gpsimd.iota(rank[:, :], [[-1, NE]], base=NE, channel_multiplier=0,
                           allow_small_or_imprecise_dtypes=True).then_inc(s_const, 1)
            pool.wait_ge(s_wlo, UNITS * C_EXP)
            nc.gpsimd.iota(nodes16[:, :], [[1, NT * P]], base=0, channel_multiplier=0,
                           allow_small_or_imprecise_dtypes=True).then_inc(s_const, 1)

        @block.scalar
        def _(act):
            def split_hi(u):
                c, r = divmod(u, UNITS)
                act.wait_ge(s_raw[u % 2], 16 * (u // 2 + 1))
                if c >= 2 and r == 0 and c in ring_free:
                    act.wait_ge(s_full, ring_free[c])
                nc.scalar.copy(w_hi[c % 2][:, 2 * r:2 * r + 2, :], w_raw[:, u % 2]).then_inc(s_whi, 1)

            def evac(n, dst_ap, rows=P, cols=HALF):
                act.wait_ge(s_full, n + 1)
                i = nc.scalar.copy(dst_ap, ps[0:rows, n % 8, 0:cols])
                if owner[n] == "act":
                    i.then_inc(s_free_act, 1)
                else:
                    i.then_inc(s_hi, 1)

            act.wait_ge(s_const, 3)
            nc.scalar.copy(ones_r[:, :], ones[:, 0:2])
            for t in range(NT):
                act.wait_ge(s_var, t + 1)
                nc.scalar.activation(nt1[0:ROWS[t], :], mv[0:ROWS[t], 1:2], ACT.Sqrt).then_inc(s_sd, 1)
                act.wait_ge(s_xn, t + 1)
                nc.scalar.copy(xn_hi[0:ROWS[t], t, :], acc[0:ROWS[t], t, :]).then_inc(s_xhi, 1)
            u = 0
            for u in range(UNITS):
                split_hi(u)
            u = UNITS
            for i, (m, lo, w) in enumerate(G_PIECES):
                off = UPPER[m] + lo - m * P
                evac(first["G"] + i, gu_hi[:, off:off + w], cols=w)
                if i >= len(G_PIECES) - UNITS:
                    split_hi(u)
                    u += 1
            for i, keys in enumerate(LOW_BANKS):
                evac(first["LOW"] + 2 * i, gl_hi[:, LOWER[keys[0]]:LOWER[keys[0]] + len(keys) * P], cols=len(keys) * P)
            for h in range(NH):
                for m in range(KB):
                    if h == 1 and m == 0:
                        act.wait_ge(s_full, first["KV0"] + KB)
                    evac(first[f"T{h}"] + m, t_hi[:, m, :])
                    if h == 1 and 1 <= m <= UNITS:
                        split_hi(u)
                        u += 1
                for m in range(KB):
                    n = first[f"KV{h}"] + m
                    act.wait_ge(s_full, n + 1)
                    split_hi(u)
                    u += 1
            for m in range(4):
                act.wait_ge(s_kvs[m], 16 * 2 * NH)
            for t in range(NT):
                for g in range(2):
                    w = ROWS[t]
                    n = first["XT"] + 2 * t + g
                    act.wait_ge(s_full, n + 1)
                    nc.scalar.copy(xt_hi[:, MB * g:MB * g + MB, t * P:t * P + w],
                                   ps[:, n % 8, :].rearrange("p (b c) -> p b c", c=P)[:, :, 0:w]).then_inc(s_hi, 1)
            for h in range(NH):
                for t in range(NT):
                    evac(first[f"QL{h}"] + t, acc[0:ROWS[t], t, h * HALF:(h + 1) * HALF], rows=ROWS[t])
                    if t < UNITS:
                        split_hi(u)
                        u += 1
                for t in range(NT):
                    if t < UNITS:
                        act.wait_ge(s_full, first[f"QR{h}"] + t + 1)
                        split_hi(u)
                        u += 1
            for t in range(NT):
                for g in range(2):
                    n, q = qt_job(t, g), 2 * t + g
                    if q >= 3:
                        act.wait_ge(s_full, mix_job((q - 3) // 2, 1) + 1)
                    act.wait_ge(s_full, n + 1)
                    w = ROWS[t]
                    nc.scalar.copy(qt_hi[:, q % 3, :, 0:w],
                                   ps[:, n % 8, :].rearrange("p (b c) -> p b c", c=P)[:, :, 0:w]).then_inc(s_hi, 1)
                if t == 0:
                    for _ in range(UNITS):
                        split_hi(u)
                        u += 1
            for _ in range(UNITS):
                split_hi(u)
                u += 1
            for h in range(NH):
                for t in range(NT):
                    act.wait_ge(s_mixs, 16 * NT)
                    evac(first[f"H{h}"] + t, acc[0:ROWS[t], t, h * HALF:(h + 1) * HALF], rows=ROWS[t])
                    if h == 0 and t < UNITS:
                        split_hi(u)
                        u += 1
            for t in range(NT):
                act.wait_ge(s_free_act, released(first["H1"] + t)[1])
                nc.scalar.copy(h_hi[0:ROWS[t], t, :], acc[0:ROWS[t], t, :]).then_inc(s_hhi, 1)
            for i, (c, w) in enumerate(SCOLS):
                w = min(HALF, NT * P - c)
                evac(first["AL"] + i, al_bc[:, c:c + w], cols=w)
            for pp in range(NT // 2):
                act.wait_ge(s_hot_used, (pp + 1) * EC)
                for a in range(2):
                    for b, (c, w) in enumerate(SCOLS):
                        i = nc.scalar.copy(cnt[:, 2 * pp + a, c:c + w], ps[:, 3 * a + b, 0:w])
                i.then_inc(s_cnt_free, 1)
            for t in range(NT + 1):
                if t < NT:
                    w = ROWS[t]
                    act.wait_ge(s_z, t + 1)
                    nc.scalar.activation(att[:, t % 2], att[:, t % 2], ACT.Exp, scale=-1.0).then_inc(s_e, 1)
                    act.wait_ge(s_att, t + 1)
                    if t >= 2:
                        act.wait_ge(s_full, first["GNN"] + 3 * (t - 2) + 3)
                    nc.scalar.copy(att_hi[:, t % 2], att[:, t % 2]).then_inc(s_atthi, 1)
                if t >= 1:
                    i = t - 1
                    w = ROWS[i]
                    act.wait_ge(s_rsum, i + 1)
                    if i >= 2:
                        act.wait_ge(s_x2, i - 1)
                    for h in range(NH):
                        n = first["GNN"] + 3 * i + 1 + h
                        act.wait_ge(s_full, n + 1)
                        nc.scalar.activation(hp[0:w, i % 2, h * HALF:(h + 1) * HALF], ps[0:w, n % 8, :], ACT.Copy,
                                             scale=rsum[0:w, i:i + 1]).then_inc(s_free_act, 1)
                    act.wait_ge(s_neg, i + 1)
                    nc.scalar.activation(hneg[0:w, :], hneg[0:w, :], ACT.Exp).then_inc(s_eneg, 1)
            act.wait_ge(s_gw, 32)
            nc.scalar.copy(gw_hi[:, :, :], gw[:, :, :]).then_inc(s_gwhi, 1)
            for t in range(NT):
                w = ROWS[t]
                act.wait_ge(s_var, NT + t + 1)
                nc.scalar.activation(nt1[0:w, :], mv[0:w, 1:2], ACT.Sqrt).then_inc(s_sd, 1)
                for g in range(2):
                    n = first["X2T"] + 2 * t + g
                    act.wait_ge(s_full, n + 1)
                    nc.scalar.copy(xt_hi[:, MB * g:MB * g + MB, t * P:t * P + w],
                                   ps[:, n % 8, :].rearrange("p (b c) -> p b c", c=P)[:, :, 0:w]).then_inc(s_hi, 1)
            act.wait_ge(s_gate, 1)
            nc.scalar.activation(g_p[:, :, :], g_p[:, :, :], ACT.Exp).then_inc(s_gexp, 1)
            for t in range(NT):
                n = first["BIAS"] + 3 * t
                if t >= 2:
                    act.wait_ge(s_full, n - 3)
                evac(n, combT[0:NE, t % 2, :], rows=NE, cols=P)
                if t < UNITS:
                    split_hi(u)
                    u += 1
            for c in range(NE * NH):
                for t in range(NT):
                    if t < UNITS and u < UNITS * len(CH):
                        act.wait_ge(s_full, first["EXP"] + c * NT + t + 1)
                        split_hi(u)
                        u += 1

        @block.vector
        def _(dve):
            chained = [0]

            def link(i):
                chained[0] += 1
                i.then_inc(s_chain, 1)
                dve.wait_ge(s_chain, chained[0])

            def split_lo(u):
                c, r = divmod(u, UNITS)
                dve.wait_ge(s_whi, u + 1)
                nc.vector.tensor_tensor(w_lo[c % 2][:, 2 * r:2 * r + 2, :], w_raw[:, u % 2],
                                        w_hi[c % 2][:, 2 * r:2 * r + 2, :].bitcast(f32), ALU.subtract).then_inc(s_wlo, 1)

            hi_count = [0]

            def evac_lo(n, dst_ap, src_ap, hi_ap):
                hi_count[0] += 1
                dve.wait_ge(s_hi, hi_count[0])
                nc.vector.tensor_tensor(dst_ap, src_ap, hi_ap.bitcast(f32), ALU.subtract).then_inc(s_free_dve, 1)

            var_count = [0]

            def norm_stats(t):
                w = ROWS[t]
                for g in range(2):
                    i = nc.vector.bn_stats(stats[0:w, g, :], acc[0:w, t, g * HALF:(g + 1) * HALF])
                link(i)
                link(nc.vector.bn_aggr(mv[0:w, :], stats[0:w, :, :].rearrange("p a b -> p (a b)")))
                link(nc.vector.tensor_copy(mean[0:w, t:t + 1], mv[0:w, 0:1]))
                nc.vector.tensor_scalar(mv[0:w, 1:2], mv[0:w, 1:2], LN_EPS, None, ALU.add).then_inc(s_var, 1)
                var_count[0] += 1
                dve.wait_ge(s_sd, var_count[0])
                link(nc.vector.reciprocal(nt2[0:w, :], nt1[0:w, :]))
                link(nc.vector.tensor_tensor(nt1[0:w, :], nt2[0:w, :], nt2[0:w, :], ALU.mult))
                link(nc.vector.tensor_tensor(nt1[0:w, :], nt1[0:w, :], mv[0:w, 1:2], ALU.mult))
                link(nc.vector.tensor_scalar(nt1[0:w, :], nt1[0:w, :], -0.5, 1.5, ALU.mult, ALU.add))
                link(nc.vector.tensor_tensor(rstd[0:w, t:t + 1], nt1[0:w, :], nt2[0:w, :], ALU.mult))

            for t in range(NT):
                w = ROWS[t]
                dve.wait_ge(s_x[t], 16)
                norm_stats(t)
                nc.vector.tensor_scalar(acc[0:w, t, :], acc[0:w, t, :], mean[0:w, t:t + 1], rstd[0:w, t:t + 1],
                                        ALU.subtract, ALU.mult).then_inc(s_xn, 1)
                dve.wait_ge(s_xhi, t + 1)
                nc.vector.tensor_tensor(xn_lo[0:w, t, :], acc[0:w, t, :], xn_hi[0:w, t, :].bitcast(f32),
                                        ALU.subtract).then_inc(s_xlo, 1)
            for u in range(UNITS):
                split_lo(u)
            u = UNITS
            for i, (m, lo, w) in enumerate(G_PIECES):
                off, n = UPPER[m] + lo - m * P, first["G"] + i
                evac_lo(n, gu_lo[:, off:off + w], ps[:, n % 8, 0:w], gu_hi[:, off:off + w])
                if i >= len(G_PIECES) - UNITS:
                    split_lo(u)
                    u += 1
            for i, keys in enumerate(LOW_BANKS):
                n, w = first["LOW"] + 2 * i + 1, len(keys) * P
                dve.wait_ge(s_full, n + 1)
                nc.vector.tensor_copy(gl_lo[:, LOWER[keys[0]]:LOWER[keys[0]] + w], ps[:, n % 8, 0:w]).then_inc(s_free_dve, 1)
            for h in range(NH):
                for m in range(KB):
                    n = first[f"T{h}"] + m
                    evac_lo(n, t_lo[:, m, :], ps[:, n % 8, :], t_hi[:, m, :])
                    if h == 1 and 1 <= m <= UNITS:
                        split_lo(u)
                        u += 1
                for m in range(KB):
                    n = first[f"KV{h}"] + m
                    dve.wait_ge(s_full, n + 1)
                    k = 2 * h + m // 4
                    if k >= 1:
                        dve.wait_ge(s_kvs[m % 4], 16 * k)
                    nc.vector.tensor_copy(kv_out[:, m % 4], ps[:, n % 8, :]).then_inc(s_free_dve, 1)
                    split_lo(u)
                    u += 1
                    if h == 1:
                        for t in ([m] if m < KB - 1 else range(m, NT)):
                            w = ROWS[t]
                            dve.wait_ge(s_x[t], 32)
                            nc.vector.tensor_scalar(acc[0:w, t, :], acc[0:w, t, :], mean[0:w, t:t + 1], rstd[0:w, t:t + 1],
                                                    ALU.subtract, ALU.mult).then_inc(s_xn2, 1)
            for m in range(4):
                dve.wait_ge(s_kvs[m], 16 * 2 * NH)
            for t in range(NT):
                for g in range(2):
                    w = ROWS[t]
                    n = first["XT"] + 2 * t + g
                    evac_lo(n, xt_lo[:, MB * g:MB * g + MB, t * P:t * P + w],
                            ps[:, n % 8, :].rearrange("p (b c) -> p b c", c=P)[:, :, 0:w],
                            xt_hi[:, MB * g:MB * g + MB, t * P:t * P + w])
            for h in range(NH):
                for t in range(NT):
                    if t < UNITS:
                        split_lo(u)
                        u += 1
                for t in range(NT):
                    n, w = first[f"QR{h}"] + t, ROWS[t]
                    dve.wait_ge(s_free_act, released(first[f"QL{h}"] + t)[1])
                    dve.wait_ge(s_full, n + 1)
                    a = acc[0:w, t, h * HALF:(h + 1) * HALF]
                    nc.vector.tensor_tensor(a, ps[0:w, n % 8, :], a, ALU.mult).then_inc(s_free_dve, 1)
                    if t < UNITS:
                        split_lo(u)
                        u += 1

            def mix_out(t):
                w = ROWS[t]
                for h in range(NH):
                    n = mix_job(t, h)
                    dve.wait_ge(s_full, n + 1)
                    nc.vector.tensor_copy(acc[0:w, t, h * HALF:(h + 1) * HALF], ps[0:w, n % 8, :]).then_inc(s_free_dve, 1)

            for t in range(NT):
                if t >= 2:
                    mix_out(t - 2)
                for g in range(2):
                    n, q, w = qt_job(t, g), 2 * t + g, ROWS[t]
                    evac_lo(n, qt_lo[:, q % 3, :, 0:w],
                            ps[:, n % 8, :].rearrange("p (b c) -> p b c", c=P)[:, :, 0:w], qt_hi[:, q % 3, :, 0:w])
                if t == 0:
                    for _ in range(UNITS):
                        split_lo(u)
                        u += 1
            mix_out(NT - 2)
            mix_out(NT - 1)
            for _ in range(UNITS):
                split_lo(u)
                u += 1
            for _ in range(UNITS):
                split_lo(u)
                u += 1
            i = nc.vector.memset(al[:, :], 0.0)
            link(nc.vector.memset(ar[:, :], 0.0))
            dve.wait_ge(s_a, 16)
            for t in range(NT):
                w = ROWS[t]
                dve.wait_ge(s_free_act, released(first["H1"] + t)[1])
                for v, a in ((al, a_bc[0:w, 0:D]), (ar, a_bc[0:w, D:2 * D])):
                    link(nc.vector.tensor_tensor_reduce(out=a_junk[0:w, :], in0=acc[0:w, t, :], in1=a, scale=1.0, scalar=0.0,
                                                        op0=ALU.mult, op1=ALU.add, accum_out=v[0:w, t:t + 1]))
            for t in range(NT):
                w = ROWS[t]
                dve.wait_ge(s_hhi, t + 1)
                i = nc.vector.tensor_tensor(h_lo[0:w, t, :], acc[0:w, t, :], h_hi[0:w, t, :].bitcast(f32), ALU.subtract)
                i.then_inc(s_hlo, 1)
            dve.wait_ge(s_hlo, NT)
            for t in range(NT):
                nc.vector.tensor_scalar(acc[:, 0, t * P:(t + 1) * P] if t < 8 else acc[:, 1, (t - 8) * P:(t - 7) * P],
                                        ident[:, :], al[:, t:t + 1], None, ALU.mult).then_inc(s_diag, 1)
            dve.wait_ge(s_edges, 32)
            link(nc.vector.tensor_copy(src_f[0:EP, :], src_i[0:EP, :]))
            link(nc.vector.tensor_copy(dst_f[0:EP, :], dst_i[0:EP, :]))
            dve.wait_ge(s_const, 4)

            def hot(pp, j, col, used):
                if used is not None:
                    dve.wait_ge(s_hot_used, used)
                nc.vector.tensor_scalar(hot_s[0:EP, j, :], nodes16[0:EP, 0:N], src_f[0:EP, bass.ds(col, 1)], None, ALU.is_equal)
                nc.vector.tensor_scalar(hot_d[0:EP, j, :], nodes16[0:EP, 2 * pp * P:2 * (pp + 1) * P],
                                        dst_f[0:EP, bass.ds(col, 1)], None, ALU.is_equal).then_inc(s_hot, 1)

            for pp in range(NT // 2):
                for j in range(4):
                    hot(pp, j, j, None if pp == 0 else pp * EC + j - 3)
                with dve.Fori(1, EC // 4) as q:
                    for j in range(4):
                        hot(pp, j, q * 4 + j, q * 4 + (pp * EC + j - 3))
            for t in range(NT + 1):
                if t < NT:
                    w = ROWS[t]
                    if t == 0:
                        dve.wait_ge(s_free_act, released(first["AL"] + len(SCOLS) - 1)[1])
                        dve.wait_ge(s_cnt_free, NT // 2)
                    z = att[:, t % 2]
                    if t >= 2:
                        dve.wait_ge(s_atthi, t - 1)
                    link(nc.vector.tensor_tensor(z, al_bc[:, t * P:(t + 1) * P].unsqueeze(1).to_broadcast([P, NT, P]),
                                                 ar[:, :].unsqueeze(2).to_broadcast([P, NT, P]), ALU.add))
                    nc.vector.scalar_tensor_tensor(z, z, NEG_SLOPE, z, ALU.mult, ALU.max).then_inc(s_z, 1)
                    dve.wait_ge(s_e, t + 1)
                    nc.vector.scalar_tensor_tensor(z[:, :, 0:w], z[:, :, 0:w], F32_MAX, cnt[:, :, t * P:t * P + w],
                                                   ALU.min, ALU.mult).then_inc(s_att, 1)
                    dve.wait_ge(s_atthi, t + 1)
                    nc.vector.tensor_tensor(att_lo[:, t % 2], z, att_hi[:, t % 2].bitcast(f32), ALU.subtract).then_inc(s_attlo, 1)
                if t >= 1:
                    i = t - 1
                    w = ROWS[i]
                    n = first["GNN"] + 3 * i
                    dve.wait_ge(s_full, n + 1)
                    r = rsum[0:w, i:i + 1]
                    nc.vector.tensor_scalar(r, ps[0:w, n % 8, 0:1], GNN_EPS, None, ALU.add).then_inc(s_free_dve, 1)
                    dve.wait_ge(s_free_dve, released(n)[1])
                    nc.vector.reciprocal(r, r).then_inc(s_rsum, 1)
                    hv = hp[0:w, i % 2, :]
                    dve.wait_ge(s_free_act, released(n + 2)[1])
                    if i >= 1:
                        dve.wait_ge(s_x2, i)
                    nc.vector.tensor_scalar(hneg[0:w, :], hv, 0.0, None, ALU.min).then_inc(s_neg, 1)
                    dve.wait_ge(s_eneg, i + 1)
                    link(nc.vector.scalar_tensor_tensor(hv, hv, 0.0, hneg[0:w, :], ALU.max, ALU.add))
                    dve.wait_ge(s_mx[i % 2], 32 * (i // 2 + 1))
                    link(nc.vector.scalar_tensor_tensor(hv, hv, -1.0, mix_in[0:w, i % 2, :], ALU.add, ALU.add))
                    nc.vector.tensor_tensor(x_in[0:w, i % 2, :], x_in[0:w, i % 2, :], hv, ALU.add).then_inc(s_x2, 1)
            dve.wait_ge(s_gwhi, 1)
            nc.vector.tensor_tensor(gw_lo[:, :, :], gw[:, :, :], gw_hi[:, :, :].bitcast(f32), ALU.subtract).then_inc(s_gwlo, 1)
            for t in range(NT):
                w = ROWS[t]
                dve.wait_ge(s_x2l[t], 16)
                norm_stats(t)
                if t >= 2:
                    dve.wait_ge(s_full, first["X2T"] + 2 * (t - 2) + 2)
                nc.vector.tensor_scalar(xn2[0:w, t % 2, :], acc[0:w, t, :], mean[0:w, t:t + 1], rstd[0:w, t:t + 1],
                                        ALU.subtract, ALU.mult).then_inc(s_xn2, 1)
                for g in range(2):
                    n = first["X2T"] + 2 * t + g
                    evac_lo(n, xt_lo[:, MB * g:MB * g + MB, t * P:t * P + w],
                            ps[:, n % 8, :].rearrange("p (b c) -> p b c", c=P)[:, :, 0:w],
                            xt_hi[:, MB * g:MB * g + MB, t * P:t * P + w])
            link(nc.vector.memset(sc[:, :, :], 0.0))
            n = first["GATE"]
            dve.wait_ge(s_full, n + 1)
            gps = ps[:, n % 8, 0:NT * NE].rearrange("p (t e) -> p t e", e=NE)

            def over_experts(v):
                return v.unsqueeze(2).to_broadcast([P, NT, NE])

            def over_tiles(v):
                return v.unsqueeze(1).to_broadcast([P, NT, NE])

            if ROWS[-1] == P:
                link(nc.vector.tensor_copy(sc[:, :, :], gps))
            else:
                nc.vector.tensor_copy(sc[:, 0:NT - 1, :], gps[:, 0:NT - 1, :])
                link(nc.vector.tensor_copy(sc[0:ROWS[-1], NT - 1, :], gps[0:ROWS[-1], NT - 1, :]))
            S = sc[:, :, :]
            link(nc.vector.tensor_tensor(S, S, over_tiles(gb[:, :]), ALU.add))
            nc.vector.tensor_scalar(S, S, GATE_EPS, None, ALU.max).then_inc(s_free_dve, 1)
            dve.wait_ge(s_free_dve, released(n)[1])
            link(nc.vector.tensor_reduce(g_m[:, :], S, AX.X, ALU.max))
            nc.vector.tensor_tensor(g_p[:, :, :], S, over_experts(g_m[:, :]), ALU.subtract).then_inc(s_gate, 1)
            link(nc.vector.tensor_tensor(g_key[:, :, :], S, over_experts(g_m[:, :]), ALU.is_ge))
            link(nc.vector.tensor_tensor(g_key[:, :, :], g_key[:, :, :], over_tiles(rank[:, :]), ALU.mult))
            link(nc.vector.tensor_reduce(g_t[:, :], g_key[:, :, :], AX.X, ALU.max))
            link(nc.vector.tensor_tensor(g_mask[:, :, :], g_key[:, :, :], over_experts(g_t[:, :]), ALU.is_equal))
            link(nc.vector.scalar_tensor_tensor(g_s2[:, :, :], g_mask[:, :, :], -1e30, S, ALU.mult, ALU.add))
            link(nc.vector.tensor_reduce(g_m[:, :], g_s2[:, :, :], AX.X, ALU.max))
            link(nc.vector.tensor_tensor(g_key[:, :, :], g_s2[:, :, :], over_experts(g_m[:, :]), ALU.is_ge))
            link(nc.vector.tensor_tensor(g_key[:, :, :], g_key[:, :, :], over_tiles(rank[:, :]), ALU.mult))
            link(nc.vector.tensor_reduce(g_t[:, :], g_key[:, :, :], AX.X, ALU.max))
            link(nc.vector.tensor_tensor(g_s2[:, :, :], g_key[:, :, :], over_experts(g_t[:, :]), ALU.is_equal))
            link(nc.vector.tensor_tensor(g_mask[:, :, :], g_mask[:, :, :], g_s2[:, :, :], ALU.add))
            dve.wait_ge(s_gexp, 1)
            link(nc.vector.tensor_reduce(g_t[:, :], g_p[:, :, :], AX.X, ALU.add))
            link(nc.vector.reciprocal(g_t[:, :], g_t[:, :]))
            link(nc.vector.tensor_tensor(g_p[:, :, :], g_p[:, :, :], over_experts(g_t[:, :]), ALU.mult))
            link(nc.vector.scalar_tensor_tensor(g_p[:, :, :], g_p[:, :, :], W_THRES, g_mask[:, :, :], ALU.max, ALU.mult))
            link(nc.vector.tensor_reduce(g_t[:, :], g_p[:, :, :], AX.X, ALU.add))
            link(nc.vector.reciprocal(g_t[:, :], g_t[:, :]))
            link(nc.vector.tensor_scalar(g_t[:, :], g_t[:, :], 1.0 / TOPK, None, ALU.mult))
            nc.vector.tensor_tensor(comb[:, :, :], g_p[:, :, :], over_experts(g_t[:, :]), ALU.mult).then_inc(s_comb, 1)
            dve.wait_ge(s_comb, 1)

            for t in range(NT):
                w = ROWS[t]
                for h in range(NH):
                    n = first["BIAS"] + 3 * t + 1 + h
                    dve.wait_ge(s_full, n + 1)
                    a = acc[0:w, t, h * HALF:(h + 1) * HALF]
                    nc.vector.tensor_tensor(a, ps[0:w, n % 8, :], a, ALU.add).then_inc(s_free_dve, 1)
                if t < UNITS:
                    split_lo(u)
                    u += 1
            for c in range(NE * NH):
                e, h = divmod(c, NH)
                for t in range(NT):
                    w = ROWS[t]
                    n = first["EXP"] + c * NT + t
                    dve.wait_ge(s_free_dve, released(n)[1] - NT)
                    dve.wait_ge(s_full, n + 1)
                    a = acc[0:w, t, h * HALF:(h + 1) * HALF]
                    i = nc.vector.scalar_tensor_tensor(a, ps[0:w, n % 8, :], comb[0:w, t, e:e + 1], a, ALU.mult, ALU.add)
                    i.then_inc(s_free_dve, 1)
                    if t < UNITS and u < UNITS * len(CH):
                        split_lo(u)
                        u += 1

        @block.tensor
        def _(pe):
            def bank_free(n):
                if n >= 8:
                    pe.wait_ge(*released(n - 8))

            def chunk_ready(c):
                pe.wait_ge(s_wlo, UNITS * (c + 1))

            def three(o, lh, ll, rh, rl, k, last_k):
                nc.tensor.matmul(o, lh, rh, start=(k == 0), stop=False)
                nc.tensor.matmul(o, lh, rl, start=False, stop=False)
                return nc.tensor.matmul(o, ll, rh, start=False, stop=(k == last_k))

            for i, (m, lo, w) in enumerate(G_PIECES):
                n = first["G"] + i
                bank_free(n)
                for t in range(NT):
                    if i == 0:
                        pe.wait_ge(s_xlo, t + 1)
                    r = ROWS[t]
                    a, b = (v[0:r, t, m * P:(m + 1) * P] for v in (xn_hi, xn_lo))
                    c, d = (v[0:r, t, lo:lo + w] for v in (xn_hi, xn_lo))
                    last = three(ps[:, n % 8, 0:w], a, b, c, d, t, NT - 1)
                last.then_inc(s_full, 1)
            pe.wait_ge(s_const, 3)
            for i, keys in enumerate(LOW_BANKS):
                for part, (g, n) in enumerate(((gu_hi, first["LOW"] + 2 * i), (gu_lo, first["LOW"] + 2 * i + 1))):
                    bank_free(n)
                    if i == 0:
                        pe.wait_ge(s_free_dve, released(first["G"] + len(G_PIECES) - 1)[1])
                    for j, (row, col) in enumerate(keys):
                        off = UPPER[col] + (row - col) * P
                        last = nc.tensor.transpose(ps[:, n % 8, j * P:(j + 1) * P], g[:, off:off + P].bitcast(f32), ident[:, :])
                    last.then_inc(s_full, 1)

            def gram(k, m, part):
                if k <= m:
                    off = UPPER[k] + (m - k) * P
                    return (gu_hi, gu_lo)[part][:, off:off + P]
                off = LOWER[(k, m)]
                return (gl_hi, gl_lo)[part][:, off:off + P]

            for h in range(NH):
                c = 3 * h
                chunk_ready(c)
                if h == 0:
                    pe.wait_ge(*released(first["T0"] - 1))
                    pe.wait_ge(*released(first["T0"] - 2))
                for m in range(KB):
                    n = first[f"T{h}"] + m
                    bank_free(n)
                    for k in range(KB):
                        last = three(ps[:, n % 8, :], gram(k, m, 0), gram(k, m, 1), w_hi[c % 2][:, k, :], w_lo[c % 2][:, k, :], k, KB - 1)
                    last.then_inc(s_full, 1)
                for m in range(KB):
                    c = 3 * h + 1 + m // MB
                    if m % MB == 0:
                        chunk_ready(c)
                    n = first[f"KV{h}"] + m
                    bank_free(n)
                    col = (m % MB) * P
                    for k in range(KB):
                        if m == 0:
                            pe.wait_ge(*released(first[f"T{h}"] + k))
                        last = three(ps[:, n % 8, :], w_hi[c % 2][:, k, col:col + P], w_lo[c % 2][:, k, col:col + P],
                                     t_hi[:, k, :], t_lo[:, k, :], k, KB - 1)
                    last.then_inc(s_full, 1)

            def transposes(n, tile, g, w):
                for b in range(MB):
                    last = nc.tensor.transpose(ps[:, n % 8, b * P:b * P + w], tile[0:w, (MB * g + b) * P:(MB * g + b + 1) * P],
                                               ident[0:w, 0:w])
                last.then_inc(s_full, 1)

            for t in range(NT):
                pe.wait_ge(s_xn2, t + 1)
                for g in range(2):
                    n = first["XT"] + 2 * t + g
                    bank_free(n)
                    transposes(n, acc[:, t, :], g, ROWS[t])

            def nodes_times_chunk(c, name, start_job):
                chunk_ready(c)
                for t in range(NT):
                    n, w = start_job + t, ROWS[t]
                    bank_free(n)
                    for k in range(KB):
                        last = three(ps[0:w, n % 8, :], xt_hi[:, k, t * P:t * P + w], xt_lo[:, k, t * P:t * P + w],
                                     w_hi[c % 2][:, k, :], w_lo[c % 2][:, k, :], k, KB - 1)
                    last.then_inc(s_full, 1)

            pe.wait_ge(*released(first["XT"] + 2 * NT - 1))
            for h in range(NH):
                nodes_times_chunk(6 + 2 * h, "ql", first[f"QL{h}"])
                nodes_times_chunk(7 + 2 * h, "qr", first[f"QR{h}"])

            def q_transposes(t):
                pe.wait_ge(*released(first["QR1"] + t))
                for g in range(2):
                    n = qt_job(t, g)
                    bank_free(n)
                    transposes(n, acc[:, t, :], g, ROWS[t])

            q_transposes(0)
            for t in range(NT):
                if t + 1 < NT:
                    q_transposes(t + 1)
                w = ROWS[t]
                for h in range(NH):
                    n = mix_job(t, h)
                    bank_free(n)
                    if t == 0:
                        chunk_ready(C_KV + h)
                    pe.wait_ge(*released(qt_job(t, 1)))
                    for k in range(KB):
                        s = (2 * t + k // MB) % 3
                        last = three(ps[0:w, n % 8, :], qt_hi[:, s, k % MB, 0:w], qt_lo[:, s, k % MB, 0:w],
                                     w_hi[h][:, k, :], w_lo[h][:, k, :], k, KB - 1)
                    last.then_inc(s_full, 1)
            for h in range(NH):
                nodes_times_chunk(C_W + h, "h", first[f"H{h}"])
            for i in range(len(SCOLS)):
                n = first["AL"] + i
                bank_free(n)
                tiles = range(4 * i, min(NT, 4 * i + 4))
                for t in tiles:
                    pe.wait_ge(s_diag, t + 1)
                    d = acc[:, 0, t * P:(t + 1) * P] if t < 8 else acc[:, 1, (t - 8) * P:(t - 7) * P]
                    last = nc.tensor.matmul(ps[:, n % 8, (t % 4) * P:(t % 4 + 1) * P], ones[:, :], d, start=True, stop=True)
                last.then_inc(s_full, 1)
            for n in range(first["AL"] - 5, first["AL"] + len(SCOLS)):
                pe.wait_ge(*released(n))

            def count_chunk(j, hot_no, start, stop):
                pe.wait_ge(s_hot, hot_no)
                for a in range(2):
                    for b, (c, w) in enumerate(SCOLS):
                        last = nc.tensor.matmul(ps[:, 3 * a + b, 0:w], hot_d[0:EP, j, a * P:(a + 1) * P],
                                                hot_s[0:EP, j, c:c + w], start=start, stop=stop)
                last.then_inc(s_hot_used, 1)
                return last

            for pp in range(NT // 2):
                if pp >= 1:
                    pe.wait_ge(s_cnt_free, pp)
                for j in range(4):
                    count_chunk(j, pp * EC + j + 1, j == 0, False)
                with pe.Fori(1, EC // 4 - 1) as q:
                    for j in range(4):
                        count_chunk(j, q * 4 + (pp * EC + j + 1), False, False)
                for j in range(4):
                    count_chunk(j, pp * EC + EC - 4 + j + 1, False, j == 3)
            pe.wait_ge(s_cnt_free, NT // 2)
            for t in range(NT):
                w = ROWS[t]
                pe.wait_ge(s_attlo, t + 1)
                if t == 0:
                    pe.wait_ge(s_hlo, NT)
                n = first["GNN"] + 3 * t
                bank_free(n)
                for d in range(NT):
                    r = ROWS[d]
                    nc.tensor.matmul(ps[0:w, n % 8, 0:2], att_hi[0:r, t % 2, d, 0:w], ones_r[0:r, :], start=(d == 0), stop=False)
                    last = nc.tensor.matmul(ps[0:w, n % 8, 0:2], att_lo[0:r, t % 2, d, 0:w], ones_r[0:r, :], start=False, stop=(d == NT - 1))
                last.then_inc(s_full, 1)
                for h in range(NH):
                    n = first["GNN"] + 3 * t + 1 + h
                    bank_free(n)
                    for d in range(NT):
                        r = ROWS[d]
                        last = three(ps[0:w, n % 8, :], att_hi[0:r, t % 2, d, 0:w], att_lo[0:r, t % 2, d, 0:w],
                                     h_hi[0:r, d, h * HALF:(h + 1) * HALF], h_lo[0:r, d, h * HALF:(h + 1) * HALF], d, NT - 1)
                    last.then_inc(s_full, 1)
            for t in range(NT):
                pe.wait_ge(s_xn2, NT + t + 1)
                for g in range(2):
                    n = first["X2T"] + 2 * t + g
                    bank_free(n)
                    transposes(n, xn2[:, t % 2, :], g, ROWS[t])
            pe.wait_ge(*released(first["X2T"] + 2 * NT - 1))
            pe.wait_ge(s_gwlo, 1)
            n = first["GATE"]
            bank_free(n)
            for t in range(NT):
                w = ROWS[t]
                for k in range(KB):
                    last = three(ps[0:w, n % 8, t * NE:(t + 1) * NE], xt_hi[:, k, t * P:t * P + w], xt_lo[:, k, t * P:t * P + w],
                                 gw_hi[:, k, :], gw_lo[:, k, :], k, KB - 1)
            last.then_inc(s_full, 1)
            pe.wait_ge(s_comb, 1)
            pe.wait_ge(s_eb, 16)
            for t in range(NT):
                w = ROWS[t]
                n = first["BIAS"] + 3 * t
                bank_free(n)
                nc.tensor.transpose(ps[0:NE, n % 8, 0:P], comb[:, t, :], ident[:, :]).then_inc(s_full, 1)
                pe.wait_ge(*released(n))
                for h in range(NH):
                    n = first["BIAS"] + 3 * t + 1 + h
                    bank_free(n)
                    nc.tensor.matmul(ps[0:w, n % 8, :], combT[0:NE, t % 2, 0:w], eb[0:NE, h * HALF:(h + 1) * HALF],
                                     start=True, stop=True).then_inc(s_full, 1)
            for c in range(NE * NH):
                nodes_times_chunk(C_EXP + c, "expert", first["EXP"] + c * NT)


_INS = ["x", "src", "dst", "L0_gnn_W", "L0_gnn_a", "L0_mix_w_query_left", "L0_mix_w_query_right", "L0_mix_w_key",
        "L0_mix_w_value", "L0_ffn_gate_W", "L0_ffn_gate_b", "L0_ffn_expert_W", "L0_ffn_expert_b"]


def kernel(**inputs):
    import numpy as np
    import concourse.bacc as bacc
    from concourse.bass_utils import run_bass_kernel_spmd

    nc = bacc.Bacc("TRN2", target_bir_lowering=False, num_devices=1)
    arrays, args = {}, []
    for name in _INS:
        a = np.ascontiguousarray(inputs[name])
        arrays["in_" + name] = a
        args.append(nc.dram_tensor("in_" + name, a.shape, mybir.dt.from_np(a.dtype), kind="ExternalInput").ap())
    y = nc.dram_tensor("out_0", inputs["x"].shape, mybir.dt.float32, kind="ExternalOutput").ap()
    gps_layer(nc, *args, y)
    r = run_bass_kernel_spmd(nc, [arrays], core_ids=[0])
    return r.results[0]["out_0"]
```

```python
from contextlib import ExitStack

import concourse.bass as bass
from concourse import mybir


def gps_layer(nc, x, src, dst, gnn_W, gnn_a, w_ql, w_qr, w_key, w_value, gate_W, gate_b, expert_W, expert_b, out):
    f32, f32r = mybir.dt.float32, mybir.dt.float32r
    f16, i32, i16 = mybir.dt.float16, mybir.dt.int32, mybir.dt.int16
    ALU, ACT, AX = mybir.AluOpType, mybir.ActivationFunctionType, mybir.AxisListType

    P = 128
    N, D = x.shape
    E = src.shape[0]
    NE = expert_b.shape[0]
    NT = (N + P - 1) // P
    KB = D // P
    HALF = 512
    NH = D // HALF
    MB = HALF // P
    ROWS = [min(P, N - t * P) for t in range(NT)]
    EP = 125
    EC = E // EP
    assert EP * EC == E
    NB = 7
    CK = 4
    GE = CK * P
    NG = (E + NT * (GE - 1)) // GE
    NG += NG % 2
    NC = NG * CK
    NW = (N + 3) // 4 * 4
    NEG_SLOPE, GNN_EPS, LN_EPS, GATE_EPS, W_THRES, TOPK = 0.1, 1e-5, 1e-5, 1e-4, 0.1, 2
    NBLK = (TOPK * N + NE * P) // P
    NSLOT = NBLK + 1
    F32_MAX = 3.4028234e38
    SCOLS = [(c, min(HALF, NW - c)) for c in range(0, NW, HALF)]

    base = (nc.sbuf_base + 31) // 32 * 32
    RING, BIG, ACC, RAW, QT, SMALL = 0, 16384, 36864, 47104, 49152, 52224

    ctx = ExitStack()
    with ctx:
        def at(name, word, shape, dt=f32):
            return nc.alloc_sbuf_tensor_at(name, shape, dt, offset=base + 4 * word)

        small_at = [SMALL]

        def small(name, shape, dt=f32):
            words = 1
            for s in shape[1:]:
                words *= s
            t = at(name, small_at[0], shape, dt)
            small_at[0] += (words + 7) // 8 * 8
            assert base + 4 * small_at[0] <= nc.sbuf_usable_end
            return t

        def sem(name):
            return ctx.enter_context(nc.semaphore(name))

        w_hi = [at(f"w_hi{s}", RING + 8192 * s, [P, KB, HALF], f32r) for s in range(2)]
        w_lo = [at(f"w_lo{s}", RING + 8192 * s + 4096, [P, KB, HALF], f32r) for s in range(2)]
        w_raw = at("w_raw", RAW, [P, 2, 2, HALF])
        acc = at("acc", ACC, [P, NT, D])
        xn_hi = at("xn_hi", BIG, [P, NT, D], f32r)
        xn_lo = at("xn_lo", BIG + 10240, [P, NT, D], f32r)
        UPPER = [sum(KB - i for i in range(m)) * P for m in range(KB)]
        NUP = UPPER[-1] + P
        LOWER = {}
        for m in range(KB):
            for n in range(m + 1, KB):
                LOWER[(n, m)] = len(LOWER) * P
        NLOW = len(LOWER) * P
        gu_hi = at("gu_hi", ACC, [P, NUP], f32r)
        gu_lo = at("gu_lo", ACC + NUP, [P, NUP], f32r)
        gl_hi = at("gl_hi", BIG, [P, NLOW], f32r)
        gl_lo = at("gl_lo", BIG + NLOW, [P, NLOW], f32r)
        T0 = BIG + 2 * NLOW
        t_hi = at("t_hi", T0, [P, KB, HALF], f32r)
        t_lo = at("t_lo", T0 + 4096, [P, KB, HALF], f32r)
        kv_out = at("kv_out", T0 + 8192, [P, 4, HALF])
        xt_hi = at("xt_hi", BIG, [P, KB, N], f32r)
        xt_lo = at("xt_lo", BIG + KB * N, [P, KB, N], f32r)
        qt_hi = at("qt_hi", QT, [P, 3, MB, P], f32r)
        qt_lo = at("qt_lo", QT + 1536, [P, 3, MB, P], f32r)
        a_bc = at("a_bc", QT, [P, 2 * D])
        a_junk = at("a_junk", QT + 2 * D, [P, D])
        h_hi = at("h_hi", BIG, [P, NT, D], f32r)
        h_lo = at("h_lo", BIG + 10240, [P, NT, D], f32r)
        cnt = at("cnt", RING, [P, NT, NW], i16)
        al_bc = at("al_bc", RING + 6400, [P, NT * P])
        hot_s = at("hot_s", QT, [P, CK, NW], f16)
        hot_d = at("hot_d", QT + 2560, [P, CK, P], f16)
        iota128 = at("iota128", QT + 2816, [P, P], f16)
        nodes16 = at("nodes16", RAW, [P, NT * P], f16)
        gcnt = at("gcnt", RAW + 640, [P, 2, NW], f16)
        R1 = RING + 8192
        src_i = at("src_i", R1, [P, EC], i32)
        dst_i = at("dst_i", R1 + 160, [P, EC], i32)
        tile_i = at("tile_i", R1 + 320, [P, EC], i32)
        pos_i = at("pos_i", R1 + 480, [P, EC], i32)
        tile_f = at("tile_f", R1 + 640, [P, EC])
        pos_f = at("pos_f", R1 + 800, [P, EC])
        in_tile = at("in_tile", R1 + 960, [P, NT, EC], f16)
        run = at("run", R1 + 1760, [P, NT, EC], f16)
        place = at("place", R1 + 2560, [P, NT, EC])
        tri = at("tri", R1 + 4160, [P, P])
        tiles10 = at("tiles10", R1 + 4288, [P, NT])
        groups = at("groups", R1 + 4304, [P, NG])
        ends = at("ends", R1 + 4368, [P, NT + 1])
        tot = at("tot", R1 + 4384, [P, NT])
        gb_i = at("gb_i", R1 + 4400, [P, NT], i32)
        gb_f = at("gb_f", R1 + 4416, [P, NT])
        gb_cum = at("gb_cum", R1 + 4432, [P, NT])
        place0 = at("place0", R1 + 4448, [P, NT])
        ge_m = at("ge_m", R1 + 4464, [P, NG, NT])
        gt_f = at("gt_f", R1 + 4976, [P, NG])
        HS = 8
        hot_r = at("hot_r", QT, [P, HS, P], f16)
        hot_c = at("hot_c", QT + 512, [P, HS, 2, NC], f16)
        QE = QT + 512 + HS * NC
        pos_lo = at("pos_lo", QE, [P, EC])
        pos_hi = at("pos_hi", QE + 160, [P, EC])
        src1 = at("src1", QE + 320, [P, EC])
        dlo = at("dlo", QE + 480, [P, EC])
        iota16 = at("iota16", QE + 640, [P, NC], f16)
        assert QE + 640 + NC // 2 <= SMALL and NC >= P
        att = at("att", ACC, [P, 2, NT, P])
        att_hi = at("att_hi", ACC + 2560, [P, 2, NT, P], f32r)
        att_lo = at("att_lo", ACC + 5120, [P, 2, NT, P], f32r)
        hp = at("hp", ACC + 7680, [P, 2, D])
        mix_in = at("mix_in", RAW, [P, 2, D])
        x_in = at("x_in", QT, [P, 2, D])
        hneg = at("hneg", QT + 2 * D, [P, D])
        xn2 = at("xn2", RING + 7680, [P, 2, D])
        xg_hi = at("xg_hi", RING + 9728, [P, KB, P], f32r)
        xg_lo = at("xg_lo", RING + 10752, [P, KB, P], f32r)
        gw = at("gw", RING + 11776, [P, KB, NE])
        gw_hi = at("gw_hi", RING + 11840, [P, KB, NE], f32r)
        gw_lo = at("gw_lo", RING + 11904, [P, KB, NE], f32r)
        e_hi = [at("e_hi0", RING, [P, KB, D], f32r), at("e_hi1", BIG, [P, KB, D], f32r)]
        e_lo = [at("e_lo0", RING + KB * D, [P, KB, D], f32r), at("e_lo1", BIG + KB * D, [P, KB, D], f32r)]
        e_raw = at("e_raw", BIG + 2 * KB * D, [P, KB, D])
        EX = BIG + 3 * KB * D
        gx = at("gx", EX, [P, D])
        lt_hi = at("lt_hi", EX + D, [P, KB, P], f32r)
        lt_lo = at("lt_lo", EX + 2 * D, [P, KB, P], f32r)
        y = at("y", EX + 3 * D, [P, D])
        bias = at("bias", EX + 4 * D, [P, 2, D])
        assert EX + 6 * D <= RAW
        x2 = at("x2", RING, [P, NT, D])
        y12 = at("y12", BIG, [P, NT, 2, D])
        G = RAW
        def gate(name, shape, dt=f32):
            nonlocal G
            words = 1
            for d in shape[1:]:
                words *= d
            t = at(name, G, shape, dt)
            G += (words + 7) // 8 * 8
            assert G <= SMALL
            return t

        g_p = gate("g_p", [P, NT, NE])
        g_key = gate("g_key", [P, NT, NE])
        g_s2 = gate("g_s2", [P, NT, NE])
        g_one = gate("g_one", [P, NT, NE])
        g_two = gate("g_two", [P, NT, NE])
        g_mask = gate("g_mask", [P, NT, NE])
        g_in = gate("g_in", [P, NE, NT])
        g_run = gate("g_run", [P, NE, NT])
        g_pos = gate("g_pos", [P, NT, NE])
        sc = gate("sc", [P, NT, NE])
        g_m = gate("g_m", [P, NT])
        g_t = gate("g_t", [P, NT])
        g_ends = gate("g_ends", [P, NE + 1])
        g_tot = gate("g_tot", [P, NE])
        g_nb = gate("g_nb", [P, NE])
        g_nbi = gate("g_nbi", [P, NE], i32)
        g_cum = gate("g_cum", [P, NE])
        g_place = gate("g_place", [P, NE])
        p_f = gate("p_f", [P, 2, NT])
        p_lo = gate("p_lo", [P, 2, NT])
        p_hi = gate("p_hi", [P, 2, NT])
        p_a = gate("p_a", [P, 2, NT], i32)
        tok = gate("tok", [P, NT])
        valid = gate("valid", [P, NT])
        tokv = gate("tokv", [P, NT])
        tri2 = gate("tri2", [P, P])
        io16 = gate("io16", [P, P], f16)
        tok_r = gate("tok_r", [P, 2 * NT, P], f16)
        tok_c = gate("tok_c", [P, 2 * NT, NSLOT], f16)

        ident = small("ident", [P, P])
        ones = small("ones", [P, P])
        ones_r = small("ones_r", [P, 2], f32r)
        stats = small("stats", [P, 2, 6])
        mv = small("mv", [P, 2])
        mean = small("mean", [P, NT])
        rstd = small("rstd", [P, NT])
        nt1 = small("nt1", [P, 1])
        nt2 = small("nt2", [P, 1])
        al = small("al", [P, NT])
        ar = small("ar", [P, NT])
        rsum = small("rsum", [P, NT])
        half_ = small("half_", [P, 1])
        s_tab = small("s_tab", [P, NC], f16)
        d_tab = small("d_tab", [P, NC], f16)
        g_tile = small("g_tile", [P, NG], i32)
        gb = small("gb", [P, NE])
        w12 = small("w12", [P, 2, NT])
        pos12 = small("pos12", [P, 2, NT], i32)
        bounds = small("bounds", [P, NE + 1], i32)
        tok_of = small("tok_of", [P, NSLOT], i32)
        tok_now = small("tok_now", [P, 1], i32)
        hexp = small("hexp", [P, 1])
        rank = small("rank", [P, NE])

        ps = ctx.enter_context(nc.psum_tensor("ps", [P, 8, HALF], f32))

        kv_d = nc.dram_tensor("kv_d", (D, D), f32).ap()
        mix_d = nc.dram_tensor("mix_d", (N, D), f32).ap()
        x2_d = nc.dram_tensor("x2_d", (N, D), f32).ap()
        xn2_d = nc.dram_tensor("xn2_d", (N, D), f32).ap()
        y_d = nc.dram_tensor("y_d", ((NBLK + 1) * P, D), f32).ap()

        def half(w, h):
            return w.rearrange("(k p) n -> p k n", p=P)[:, :, h * HALF:(h + 1) * HALF]

        CH = [half(w_value, 0), half(w_key, 0), half(w_key, 1), half(w_value, 1), half(w_key, 0), half(w_key, 1),
              half(w_ql, 0), half(w_qr, 0), half(w_ql, 1), half(w_qr, 1), half(kv_d, 0), half(kv_d, 1),
              half(gnn_W, 0), half(gnn_W, 1)]
        C_KV, C_W, C_EXP = 10, 12, 14
        UNITS = 4

        owner, first = [], {}

        def phase(name, owners):
            first[name] = len(owner)
            owner.extend(owners)

        G_PIECES = []
        for m in range(KB):
            lo, width = m * P, D - m * P
            cut = [width] if width <= HALF else [HALF, width - HALF]
            for w in cut:
                G_PIECES.append((m, lo, w))
                lo += w
        phase("G", ["dve"] * len(G_PIECES))
        LOW_KEYS = list(LOWER)
        LOW_BANKS = [LOW_KEYS[i:i + 4] for i in range(0, len(LOW_KEYS), 4)]
        phase("LOW", ["act", "dve"] * len(LOW_BANKS))
        phase("T0", ["dve"] * KB)
        phase("KV0", ["dve"] * KB)
        phase("T1", ["dve"] * KB)
        phase("KV1", ["dve"] * KB)
        phase("XT", ["dve"] * (2 * NT))
        for h in range(NH):
            phase(f"QL{h}", ["act"] * NT)
            phase(f"QR{h}", ["dve"] * NT)
        phase("QTMIX", ["dve"] * (4 * NT))
        phase("H0", ["act"] * NT)
        phase("H1", ["act"] * NT)
        phase("AL", ["act"] * len(SCOLS))
        first["GNN"] = len(owner)
        gnn_job, tr_job = {}, {}
        for t in range(NT + 3):
            if t < NT:
                gnn_job[t] = len(owner)
                owner.extend(["dve", "act", "act"])
            if 2 <= t < NT + 2:
                tr_job[t - 2] = len(owner)
                owner.extend(["dve"] * 2)

        def released(n):
            return (s_free_act if owner[n] == "act" else s_free_dve), owner[:n + 1].count(owner[n])

        def qt_job(t, i):
            return first["QTMIX"] + (0 if t == 0 else 4 * t - 2) + i

        def mix_job(t, h):
            return first["QTMIX"] + (4 + 4 * t if t < NT - 1 else 4 * NT - 2) + h

        s_x = [sem(f"s_xt{t}") for t in range(NT)]
        s_raw = [sem(f"s_raw{i}") for i in range(2)]
        s_const, s_edges, s_a, s_gw, s_eb = (sem(n) for n in ("s_const", "s_edges", "s_a", "s_gw", "s_eb"))
        s_xn, s_xhi, s_xlo = sem("s_xn"), sem("s_xhi"), sem("s_xlo")
        s_whi, s_wlo = sem("s_whi"), sem("s_wlo")
        s_full, s_free_act, s_free_dve = sem("s_full"), sem("s_free_act"), sem("s_free_dve")
        s_hi = sem("s_hi")
        s_kvs = [sem(f"s_kvs{i}") for i in range(4)]
        s_xn2 = sem("s_xn2")
        s_mixs = sem("s_mixs")
        s_hhi, s_hlo = sem("s_hhi"), sem("s_hlo")
        s_diag = sem("s_diag")
        s_hot, s_hot_used, s_gcnt, s_add = sem("s_hot"), sem("s_hot_used"), sem("s_gcnt"), sem("s_add")
        s_tri, s_tot, s_totp, s_pos = sem("s_tri"), sem("s_tot"), sem("s_totp"), sem("s_pos")
        s_ph, s_ph_used, s_tab_done, s_zero, s_nodes = sem("s_ph"), sem("s_ph_used"), sem("s_tab_done"), sem("s_zero"), sem("s_nodes")
        s_z, s_e, s_att, s_atthi, s_attlo = sem("s_z"), sem("s_e"), sem("s_att"), sem("s_atthi"), sem("s_attlo")
        s_mx = [sem(f"s_mx{i}") for i in range(2)]
        s_rsum, s_neg, s_eneg, s_x2 = sem("s_rsum"), sem("s_neg"), sem("s_eneg"), sem("s_x2")
        s_x2s = [sem(f"s_x2s{i}") for i in range(2)]
        s_var, s_sd, s_gwhi, s_gwlo = sem("s_var"), sem("s_sd"), sem("s_gwhi"), sem("s_gwlo")
        s_xn2d = [sem(f"s_xn2d{i}") for i in range(2)]
        s_xg, s_gate_used, s_scores, s_gate, s_gexp = sem("s_xg"), sem("s_gate_used"), sem("s_scores"), sem("s_gate"), sem("s_gexp")
        s_tri2, s_gtot, s_gtotp, s_gpos, s_toks, s_tokp, s_route = (sem(n) for n in (
            "s_tri2", "s_gtot", "s_gtotp", "s_gpos", "s_toks", "s_tokp", "s_route"))
        s_er = [sem(f"s_er{k}") for k in range(KB)]
        s_bias = [sem(f"s_bias{i}") for i in range(2)]
        s_ehi, s_elo = sem("s_ehi"), sem("s_elo")
        s_gx, s_tok, s_tok_in, s_tr, s_lhi, s_llo, s_mm, s_ye, s_ys, s_rest = (sem(n) for n in (
            "s_gx", "s_tok", "s_tok_in", "s_tr", "s_lhi", "s_llo", "s_mm", "s_ye", "s_ys", "s_rest"))
        s_x2r, s_fin, s_finw = sem("s_x2r"), sem("s_fin"), sem("s_finw")
        s_y12 = [sem(f"s_y12_{t}") for t in range(NT)]
        s_out = sem("s_out")
        s_chain = sem("s_chain")
        s_pool = sem("s_pool")

        block = ctx.enter_context(nc.Block())

        ring_free = {2: first["T0"] + KB, 3: first["KV0"] + 4, 4: first["KV0"] + KB, 5: first["T1"] + KB,
                     6: first["KV1"] + 4, 7: first["KV1"] + KB}
        for i in range(4):
            name = ["QL0", "QR0", "QL1", "QR1"][i]
            ring_free[8 + i] = first[name] + NT
        ring_free[12] = ring_free[13] = first["QTMIX"] + 4 * NT
        GNN_END = gnn_job[NT - 1] + 3

        def place_chunks(phase_no, m):
            i, total = phase_no * KB + m, 2 * NH * KB
            return range(EC * i // total, EC * (i + 1) // total)

        @block.sync
        def _(sp):
            def load_unit(u):
                c, r = divmod(u, UNITS)
                if u >= 2:
                    sp.wait_ge(s_wlo, u - 1)
                sp.dma_start(w_raw[:, u % 2], CH[c][:, 2 * r:2 * r + 2, :]).then_inc(s_raw[u % 2], 16)

            for t in range(NT):
                sp.dma_start(acc[0:ROWS[t], t, :], x[t * P:t * P + ROWS[t], :]).then_inc(s_x[t], 16)
            sp.dma_start(src_i[0:EP, :], src.rearrange("(p c) -> p c", c=EC)).then_inc(s_edges, 16)
            sp.dma_start(dst_i[0:EP, :], dst.rearrange("(p c) -> p c", c=EC)).then_inc(s_edges, 16)
            u = 0
            while u < 2 * UNITS + 2:
                load_unit(u)
                u += 1
            for h in range(NH):
                for m in range(KB):
                    sp.wait_ge(s_free_dve, released(first[f"KV{h}"] + m)[1])
                    sp.dma_start(kv_d[m * P:(m + 1) * P, h * HALF:(h + 1) * HALF], kv_out[:, m % 4]).then_inc(s_kvs[m % 4], 16)
                    load_unit(u)
                    u += 1
                if h == 0:
                    for _ in range(UNITS):
                        load_unit(u)
                        u += 1
                    sp.wait_ge(s_full, first["T1"] + KB)
                    for t in range(NT):
                        sp.dma_start(acc[0:ROWS[t], t, :], x[t * P:t * P + ROWS[t], :]).then_inc(s_x[t], 16)
            while u < UNITS * C_KV:
                load_unit(u)
                u += 1
            for s in s_kvs:
                sp.wait_ge(s, 16 * 2 * NH)
            while u < UNITS * C_W + 2:
                load_unit(u)
                u += 1
            for t in range(NT):
                sp.wait_ge(s_free_dve, released(mix_job(t, 1))[1])
                sp.dma_start(mix_d[t * P:t * P + ROWS[t], :], acc[0:ROWS[t], t, :]).then_inc(s_mixs, 16)
            sp.wait_ge(s_full, first["H0"])
            sp.wait_ge(s_tab_done, 1)
            sp.dma_start(a_bc[:, :], gnn_a.partition_broadcast(P)).then_inc(s_a, 16)
            while u < UNITS * C_EXP:
                load_unit(u)
                u += 1
            sp.wait_ge(s_mixs, 16 * NT)
            sp.wait_ge(s_add, NG)
            for t in range(NT + 1):
                if t < NT:
                    if t >= 2:
                        sp.wait_ge(s_x2s[t % 2], 16 * (t // 2))
                    sp.dma_start(mix_in[0:ROWS[t], t % 2, :], mix_d[t * P:t * P + ROWS[t], :]).then_inc(s_mx[t % 2], 16)
                    sp.dma_start(x_in[0:ROWS[t], t % 2, :], x[t * P:t * P + ROWS[t], :]).then_inc(s_mx[t % 2], 16)
                if t == 0:
                    sp.wait_ge(s_full, first["H1"] + NT)
                    sp.dma_start(gw[:, :, :], gate_W.rearrange("(k p) e -> p k e", p=P)).then_inc(s_gw, 16)
                    sp.dma_start(gb[:, :], gate_b.rearrange("(o e) -> o e", o=1).partition_broadcast(P)).then_inc(s_gw, 16)
                if t >= 1:
                    i = t - 1
                    sp.wait_ge(s_xn2, NT + i + 1)
                    sp.dma_start(xn2_d[i * P:i * P + ROWS[i], :], xn2[0:ROWS[i], i % 2, :]).then_inc(s_xn2d[i % 2], 16)
                    sp.dma_start(x2_d[i * P:i * P + ROWS[i], :], x_in[0:ROWS[i], i % 2, :]).then_inc(s_x2s[i % 2], 16)
            def load_expert(e):
                for k in range(KB):
                    if e >= 1:
                        sp.wait_ge(s_elo, KB * (e - 1) + k + 1)
                    sp.dma_start(e_raw[:, k, :], expert_W[e, k * P:(k + 1) * P, :]).then_inc(s_er[k], 16)

            def load_bias(e):
                sp.dma_start(bias[:, e % 2, :], expert_b[e:e + 1, :].partition_broadcast(P)).then_inc(s_bias[e % 2], 16)

            sp.wait_ge(s_x2, NT)
            sp.wait_ge(s_full, GNN_END)
            load_expert(0)
            load_bias(0)
            load_bias(1)
            load_expert(1)
            sp.sem_inc(s_ys, 16)
            sp.wait_ge(s_route, 1)
            first_block = [sp.value_load(bounds[0:1, e:e + 1], min_val=0, max_val=NBLK) for e in range(NE + 1)]
            for i in range(2):
                sp.wait_ge(s_xn2d[i], 16 * (NT // 2))
            with sp.Fori(first_block[NE], NBLK + 1) as i:
                sp.dma_start(y_d[bass.ds(i * P, P), :], xn2_d[0:P, :]).then_inc(s_rest, 16)
            for e in range(NE):
                if e + 2 < NE:
                    load_expert(e + 2)
                if 1 <= e < NE - 1:
                    load_bias(e + 1)
                with sp.Fori(first_block[e], first_block[e + 1]) as i:
                    sp.wait_ge(s_ye, i * 2 + 4)
                    sp.dma_start(y_d[bass.ds(i * P, P), :], y[:, :]).then_inc(s_ys, 16)
                    sp.sem_inc(s_rest, 16)
                if e == NE - 2:
                    for i in range(2):
                        sp.wait_ge(s_x2s[i], 16 * (NT // 2))
                    for t in range(NT):
                        sp.dma_start(x2[0:ROWS[t], t, :], x2_d[t * P:t * P + ROWS[t], :]).then_inc(s_x2r, 16)
            for t in range(NT):
                sp.wait_ge(s_finw, t + 1)
                sp.dma_start(out[t * P:t * P + ROWS[t], :], x2[0:ROWS[t], t, :]).then_inc(s_out, 16)
            sp.wait_ge(s_out, 16 * NT)

        @block.gpsimd
        def _(pool):
            nc.gpsimd.memset(ident[:, :], 0.0).then_inc(s_pool, 1)
            nc.gpsimd.memset(ones[:, :], 1.0).then_inc(s_const, 1)
            pool.wait_ge(s_pool, 1)
            nc.gpsimd.affine_select(out=ident[:, :], in_=ident[:, :], compare_op=ALU.not_equal, fill=1.0,
                                    base=0, pattern=[[-1, P]], channel_multiplier=1).then_inc(s_const, 1)
            nc.gpsimd.iota(rank[:, :], [[-1, NE]], base=NE, channel_multiplier=0,
                           allow_small_or_imprecise_dtypes=True).then_inc(s_const, 1)
            nc.gpsimd.memset(tri[:, :], 0.0).then_inc(s_pool, 1)
            pool.wait_ge(s_pool, 2)
            nc.gpsimd.affine_select(out=tri[:, :], in_=tri[:, :], compare_op=ALU.is_ge, fill=1.0,
                                    base=0, pattern=[[-1, P]], channel_multiplier=1).then_inc(s_tri, 1)
            nc.gpsimd.iota(tiles10[:, :], [[1, NT]], base=0, channel_multiplier=0,
                           allow_small_or_imprecise_dtypes=True).then_inc(s_tri, 1)
            nc.gpsimd.iota(groups[:, :], [[1, NG]], base=0, channel_multiplier=0,
                           allow_small_or_imprecise_dtypes=True).then_inc(s_tri, 1)
            nc.gpsimd.iota(iota16[:, :], [[1, NC]], base=0, channel_multiplier=0,
                           allow_small_or_imprecise_dtypes=True).then_inc(s_tri, 1)
            pool.wait_ge(s_wlo, UNITS * C_EXP)
            nc.gpsimd.iota(nodes16[:, :], [[1, NT * P]], base=1, channel_multiplier=0,
                           allow_small_or_imprecise_dtypes=True)
            pool.wait_ge(s_hlo, 1)
            nc.gpsimd.iota(iota128[:, :], [[1, P]], base=0, channel_multiplier=0,
                           allow_small_or_imprecise_dtypes=True).then_inc(s_nodes, 1)
            pool.wait_ge(s_full, first["H1"] + NT)
            nc.gpsimd.memset(cnt[:, :, :].bitcast(i32), 0).then_inc(s_zero, 1)
            nc.gpsimd.memset(hexp[:, :], -0.5).then_inc(s_pool, 1)
            pool.wait_ge(s_pool, 3)
            for t in range(NT):
                pool.wait_ge(s_var, NT + t + 1)
                nc.gpsimd.tensor_tensor(nt2[:, :], mv[:, 1:2], hexp[:, :], ALU.pow).then_inc(s_sd, 1)
            pool.wait_ge(s_x2, NT)
            for i in range(2):
                pool.wait_ge(s_x2s[i], 16 * (NT // 2))
            nc.gpsimd.memset(tri2[:, :], 0.0).then_inc(s_pool, 1)
            pool.wait_ge(s_pool, 4)
            nc.gpsimd.affine_select(out=tri2[:, :], in_=tri2[:, :], compare_op=ALU.is_ge, fill=1.0,
                                    base=0, pattern=[[-1, P]], channel_multiplier=1).then_inc(s_tri2, 1)
            nc.gpsimd.iota(tok[:, :], [[P, NT]], base=0, channel_multiplier=1,
                           allow_small_or_imprecise_dtypes=True).then_inc(s_tri2, 1)
            nc.gpsimd.iota(io16[:, :], [[1, P]], base=0, channel_multiplier=0,
                           allow_small_or_imprecise_dtypes=True).then_inc(s_tri2, 1)
            pool.wait_ge(s_route, 1)
            for i in range(2):
                pool.wait_ge(s_xn2d[i], 16 * (NT // 2))
            n_blocks = pool.value_load(bounds[0:1, NE:NE + 1], min_val=NE, max_val=NBLK)

            def gather(i):
                nc.gpsimd.tensor_copy(tok_now[:, :], tok_of[:, bass.ds(i, 1)]).then_inc(s_tok, 1)
                pool.wait_ge(s_tok, i + 1)
                pool.sem_inc(s_tok_in, 1)
                nc.gpsimd.indirect_dma_start(out=gx[:, :], out_offset=None, in_=xn2_d,
                                             in_offset=bass.IndirectOffsetOnAxis(ap=tok_now[:, :], axis=0)).then_inc(s_gx, 16)

            gather(0)
            with pool.Fori(1, n_blocks + 1) as i:
                pool.wait_ge(s_tr, i * 2)
                gather(i)
            pool.wait_ge(s_ys, n_blocks * 16 + 16)
            pool.wait_ge(s_rest, (NBLK + 1) * 16)
            pool.wait_ge(s_mm, n_blocks * 3)
            pool.sem_inc(s_tok_in, 1)
            pool.wait_ge(s_elo, KB * NE)
            for t in range(NT):
                for c in range(2):
                    nc.gpsimd.indirect_dma_start(out=y12[0:ROWS[t], t, c, :], out_offset=None, in_=y_d,
                                                 in_offset=bass.IndirectOffsetOnAxis(ap=pos12[0:ROWS[t], c, t:t + 1], axis=0)
                                                 ).then_inc(s_y12[t], 16)

        @block.scalar
        def _(act):
            def split_hi(u):
                c, r = divmod(u, UNITS)
                act.wait_ge(s_raw[u % 2], 16 * (u // 2 + 1))
                if u == UNITS:
                    act.wait_ge(s_pos, 1)
                if c >= 2 and r == 0 and c in ring_free:
                    act.wait_ge(s_full, ring_free[c])
                nc.scalar.copy(w_hi[c % 2][:, 2 * r:2 * r + 2, :], w_raw[:, u % 2]).then_inc(s_whi, 1)

            def evac(n, dst_ap, rows=P, cols=HALF):
                act.wait_ge(s_full, n + 1)
                i = nc.scalar.copy(dst_ap, ps[0:rows, n % NB, 0:cols])
                if owner[n] == "act":
                    i.then_inc(s_free_act, 1)
                else:
                    i.then_inc(s_hi, 1)

            act.wait_ge(s_const, 3)
            nc.scalar.copy(ones_r[:, :], ones[:, 0:2])
            for t in range(NT):
                act.wait_ge(s_var, t + 1)
                nc.scalar.activation(nt1[0:ROWS[t], :], mv[0:ROWS[t], 1:2], ACT.Sqrt).then_inc(s_sd, 1)
                act.wait_ge(s_xn, t + 1)
                nc.scalar.copy(xn_hi[0:ROWS[t], t, :], acc[0:ROWS[t], t, :]).then_inc(s_xhi, 1)
            u = 0
            for u in range(UNITS):
                split_hi(u)
            u = UNITS
            for i, (m, lo, w) in enumerate(G_PIECES):
                off = UPPER[m] + lo - m * P
                evac(first["G"] + i, gu_hi[:, off:off + w], cols=w)
                if i >= len(G_PIECES) - UNITS:
                    split_hi(u)
                    u += 1
            for i, keys in enumerate(LOW_BANKS):
                evac(first["LOW"] + 2 * i, gl_hi[:, LOWER[keys[0]]:LOWER[keys[0]] + len(keys) * P], cols=len(keys) * P)
            for h in range(NH):
                for m in range(KB):
                    if h == 1 and m == 0:
                        act.wait_ge(s_full, first["KV0"] + KB)
                    evac(first[f"T{h}"] + m, t_hi[:, m, :])
                    if h == 1 and 1 <= m <= UNITS:
                        split_hi(u)
                        u += 1
                for m in range(KB):
                    n = first[f"KV{h}"] + m
                    act.wait_ge(s_full, n + 1)
                    split_hi(u)
                    u += 1
            for m in range(4):
                act.wait_ge(s_kvs[m], 16 * 2 * NH)
            for t in range(NT):
                for g in range(2):
                    w = ROWS[t]
                    n = first["XT"] + 2 * t + g
                    act.wait_ge(s_full, n + 1)
                    nc.scalar.copy(xt_hi[:, MB * g:MB * g + MB, t * P:t * P + w],
                                   ps[:, n % NB, :].rearrange("p (b c) -> p b c", c=P)[:, :, 0:w]).then_inc(s_hi, 1)
            for h in range(NH):
                for t in range(NT):
                    evac(first[f"QL{h}"] + t, acc[0:ROWS[t], t, h * HALF:(h + 1) * HALF], rows=ROWS[t])
                    if t < UNITS:
                        split_hi(u)
                        u += 1
                for t in range(NT):
                    if t < UNITS:
                        act.wait_ge(s_full, first[f"QR{h}"] + t + 1)
                        split_hi(u)
                        u += 1
            for t in range(NT):
                for g in range(2):
                    n, q = qt_job(t, g), 2 * t + g
                    if q >= 3:
                        act.wait_ge(s_full, mix_job((q - 3) // 2, 1) + 1)
                    act.wait_ge(s_full, n + 1)
                    w = ROWS[t]
                    nc.scalar.copy(qt_hi[:, q % 3, :, 0:w],
                                   ps[:, n % NB, :].rearrange("p (b c) -> p b c", c=P)[:, :, 0:w]).then_inc(s_hi, 1)
                if t == 0:
                    for _ in range(UNITS):
                        split_hi(u)
                        u += 1
            for _ in range(UNITS):
                split_hi(u)
                u += 1
            for h in range(NH):
                for t in range(NT):
                    act.wait_ge(s_mixs, 16 * NT)
                    evac(first[f"H{h}"] + t, acc[0:ROWS[t], t, h * HALF:(h + 1) * HALF], rows=ROWS[t])
                    if h == 0 and t < UNITS:
                        split_hi(u)
                        u += 1
            for t in range(NT):
                act.wait_ge(s_free_act, released(first["H1"] + t)[1])
                nc.scalar.copy(h_hi[0:ROWS[t], t, :], acc[0:ROWS[t], t, :]).then_inc(s_hhi, 1)
            for i, (c, w) in enumerate(SCOLS):
                w = min(HALF, NT * P - c)
                evac(first["AL"] + i, al_bc[:, c:c + w], cols=w)
            def group_counts(a, g):
                act.wait_ge(s_hot_used, g * CK + CK)
                if not (isinstance(g, int) and g < 2):
                    act.wait_ge(s_add, g + (-1))
                nc.scalar.copy(gcnt[:, a, :], ps[:, 3 * a:3 * a + 3, :].rearrange("p b c -> p (b c)")[:, 0:NW]).then_inc(s_gcnt, 1)

            act.wait_ge(s_nodes, 1)
            group_counts(0, 0)
            group_counts(1, 1)
            with act.Fori(1, NG // 2) as q:
                for a in range(2):
                    group_counts(a, q * 2 + a)
            act.wait_ge(s_gw, 32)
            nc.scalar.copy(gw_hi[:, :, :], gw[:, :, :]).then_inc(s_gwhi, 1)
            for t in range(NT + 3):
                if t < NT:
                    act.wait_ge(s_z, t + 1)
                    nc.scalar.activation(att[:, t % 2], att[:, t % 2], ACT.Exp, scale=-1.0).then_inc(s_e, 1)
                    act.wait_ge(s_att, t + 1)
                    if t >= 2:
                        act.wait_ge(s_full, gnn_job[t - 2] + 3)
                    nc.scalar.copy(att_hi[:, t % 2], att[:, t % 2]).then_inc(s_atthi, 1)
                if 1 <= t <= NT:
                    i = t - 1
                    w = ROWS[i]
                    act.wait_ge(s_rsum, i + 1)
                    if i >= 1:
                        act.wait_ge(s_x2, i)
                    for h in range(NH):
                        n = gnn_job[i] + 1 + h
                        act.wait_ge(s_full, n + 1)
                        c = slice(h * HALF, (h + 1) * HALF)
                        nc.scalar.activation(hneg[0:w, c], ps[0:w, n % NB, :], ACT.Exp, scale=rsum[0:w, i:i + 1])
                        nc.scalar.activation(hp[0:w, i % 2, c], ps[0:w, n % NB, :], ACT.Copy, bias=1.0,
                                             scale=rsum[0:w, i:i + 1]).then_inc(s_free_act, 1)
                if t >= 3:
                    i = t - 3
                    w = ROWS[i]
                    if i >= 1:
                        act.wait_ge(s_gate_used, i)
                    for g in range(2):
                        n = tr_job[i] + g
                        act.wait_ge(s_full, n + 1)
                        nc.scalar.copy(xg_hi[:, MB * g:MB * g + MB, 0:w],
                                       ps[:, n % NB, :].rearrange("p (b c) -> p b c", c=P)[:, :, 0:w]).then_inc(s_hi, 1)
            act.wait_ge(s_gate, 1)
            nc.scalar.activation(g_p[:, :, :], g_p[:, :, :], ACT.Exp).then_inc(s_gexp, 1)

            def expert_hi(e):
                for k in range(KB):
                    act.wait_ge(s_er[k], 16 * (e + 1))
                    nc.scalar.copy(e_hi[e % 2][:, k, :], e_raw[:, k, :]).then_inc(s_ehi, 1)

            def block_hi(i, g):
                act.wait_ge(s_tr, i * 2 + (g + 1))
                nc.scalar.copy(lt_hi[:, MB * g:MB * g + MB, :],
                               ps[:, 4 + g, :].rearrange("p (b c) -> p b c", c=P)).then_inc(s_lhi, 1)

            act.wait_ge(s_gate_used, NT)
            expert_hi(0)
            act.wait_ge(s_route, 1)
            first_block = [act.value_load(bounds[0:1, e:e + 1], min_val=0, max_val=NBLK) for e in range(NE + 1)]
            for g in range(2):
                block_hi(0, g)
            for e in range(NE):
                if e + 1 < NE:
                    if e >= 1:
                        act.wait_ge(s_mm, first_block[e] * 3)
                    expert_hi(e + 1)
                with act.Fori(first_block[e], first_block[e + 1]) as i:
                    act.wait_ge(s_mm, i * 3 + 1)
                    block_hi(i + 1, 0)
                    act.wait_ge(s_mm, i * 3 + 3)
                    block_hi(i + 1, 1)

        @block.vector
        def _(dve):
            chained = [0]

            def link(i):
                chained[0] += 1
                i.then_inc(s_chain, 1)
                dve.wait_ge(s_chain, chained[0])

            def split_lo(u):
                c, r = divmod(u, UNITS)
                dve.wait_ge(s_whi, u + 1)
                nc.vector.tensor_tensor(w_lo[c % 2][:, 2 * r:2 * r + 2, :], w_raw[:, u % 2],
                                        w_hi[c % 2][:, 2 * r:2 * r + 2, :].bitcast(f32), ALU.subtract).then_inc(s_wlo, 1)

            hi_count = [0]

            def evac_lo(n, dst_ap, src_ap, hi_ap):
                hi_count[0] += 1
                dve.wait_ge(s_hi, hi_count[0])
                nc.vector.tensor_tensor(dst_ap, src_ap, hi_ap.bitcast(f32), ALU.subtract).then_inc(s_free_dve, 1)

            var_count = [0]

            def norm_stats(t):
                w = ROWS[t]
                for g in range(2):
                    i = nc.vector.bn_stats(stats[0:w, g, :], acc[0:w, t, g * HALF:(g + 1) * HALF])
                link(i)
                link(nc.vector.bn_aggr(mv[0:w, :], stats[0:w, :, :].rearrange("p a b -> p (a b)")))
                link(nc.vector.tensor_copy(mean[0:w, t:t + 1], mv[0:w, 0:1]))
                nc.vector.tensor_scalar(mv[0:w, 1:2], mv[0:w, 1:2], LN_EPS, None, ALU.add).then_inc(s_var, 1)
                var_count[0] += 1
                dve.wait_ge(s_sd, var_count[0])
                link(nc.vector.reciprocal(nt2[0:w, :], nt1[0:w, :]))
                link(nc.vector.tensor_tensor(nt1[0:w, :], nt2[0:w, :], nt2[0:w, :], ALU.mult))
                link(nc.vector.tensor_tensor(nt1[0:w, :], nt1[0:w, :], mv[0:w, 1:2], ALU.mult))
                link(nc.vector.tensor_scalar(nt1[0:w, :], nt1[0:w, :], -0.5, 1.5, ALU.mult, ALU.add))
                link(nc.vector.tensor_tensor(rstd[0:w, t:t + 1], nt1[0:w, :], nt2[0:w, :], ALU.mult))

            for t in range(NT):
                w = ROWS[t]
                dve.wait_ge(s_x[t], 16)
                norm_stats(t)
                nc.vector.tensor_scalar(acc[0:w, t, :], acc[0:w, t, :], mean[0:w, t:t + 1], rstd[0:w, t:t + 1],
                                        ALU.subtract, ALU.mult).then_inc(s_xn, 1)
                dve.wait_ge(s_xhi, t + 1)
                nc.vector.tensor_tensor(xn_lo[0:w, t, :], acc[0:w, t, :], xn_hi[0:w, t, :].bitcast(f32),
                                        ALU.subtract).then_inc(s_xlo, 1)
            for u in range(UNITS):
                split_lo(u)
            u = UNITS

            V = nc.vector
            dve.wait_ge(s_edges, 32)
            dve.wait_ge(s_tri, 4)
            e_ = slice(0, EP)
            V.tensor_scalar(tile_i[e_, :], dst_i[e_, :], 7, None, ALU.logical_shift_right)
            V.tensor_scalar(src1[e_, :], src_i[e_, :], 1.0, None, ALU.add)
            link(V.tensor_scalar(pos_i[e_, :], dst_i[e_, :], P - 1, None, ALU.bitwise_and))
            V.tensor_copy(dlo[e_, :], pos_i[e_, :])
            link(V.tensor_copy(tile_f[e_, :], tile_i[e_, :]))
            link(V.tensor_tensor(in_tile[e_, :, :], tile_f[e_, :].unsqueeze(1).to_broadcast([EP, NT, EC]),
                                 tiles10[e_, :].unsqueeze(2).to_broadcast([EP, NT, EC]), ALU.is_equal))
            flat = in_tile[e_, :, :].rearrange("p a b -> p (a b)")
            link(V.tensor_tensor_scan(run[e_, :, :].rearrange("p a b -> p (a b)"), flat, flat, 0.0, ALU.add, ALU.max))
            link(V.memset(ends[:, :], 0.0))
            link(V.tensor_copy(ends[e_, 1:NT + 1], run[e_, :, EC - 1]))
            V.tensor_tensor(tot[e_, :], ends[e_, 1:NT + 1], ends[e_, 0:NT], ALU.subtract).then_inc(s_tot, 1)
            dve.wait_ge(s_totp, 1)
            link(V.tensor_scalar(gb_i[:, :], ps[:, 7, NT:2 * NT], float(GE - 1), None, ALU.add))
            link(V.tensor_scalar(gb_i[:, :], gb_i[:, :], GE.bit_length() - 1, None, ALU.logical_shift_right))
            link(V.tensor_copy(gb_f[:, :], gb_i[:, :]))
            link(V.tensor_tensor_scan(gb_cum[:, :], gb_f[:, :], gb_f[:, :], 0.0, ALU.add, ALU.max))
            link(V.tensor_tensor(ge_m[:, :, :], groups[:, :].unsqueeze(2).to_broadcast([P, NG, NT]),
                                 gb_cum[:, :].unsqueeze(1).to_broadcast([P, NG, NT]), ALU.is_ge))
            link(V.tensor_reduce(gt_f[:, :], ge_m[:, :, :], AX.X, ALU.add))
            V.tensor_scalar(g_tile[:, :], gt_f[:, :], float(NT - 1), None, ALU.min)
            link(V.tensor_tensor(place0[:, :], gb_cum[:, :], gb_f[:, :], ALU.subtract))
            link(V.scalar_tensor_tensor(place0[:, :], place0[:, :], float(GE), ps[:, 7, 0:NT], ALU.mult, ALU.add))
            link(V.scalar_tensor_tensor(place0[:, :], place0[:, :], -1.0, ends[:, 0:NT], ALU.add, ALU.subtract))
            link(V.tensor_tensor(place[e_, :, :], run[e_, :, :], place0[e_, :].unsqueeze(2).to_broadcast([EP, NT, EC]), ALU.add))
            link(V.tensor_tensor(place[e_, :, :], place[e_, :, :], in_tile[e_, :, :], ALU.mult))
            link(V.tensor_reduce(pos_f[e_, :], place[e_, :, :].rearrange("p a b -> p b a"), AX.X, ALU.add))
            link(V.tensor_copy(pos_i[e_, :], pos_f[e_, :]))
            link(V.tensor_scalar(tile_i[e_, :], pos_i[e_, :], P - 1, None, ALU.bitwise_and))
            link(V.tensor_copy(pos_lo[e_, :], tile_i[e_, :]))
            link(V.tensor_scalar(tile_i[e_, :], pos_i[e_, :], P.bit_length() - 1, None, ALU.logical_shift_right))
            link(V.tensor_copy(pos_hi[e_, :], tile_i[e_, :]))
            V.tensor_copy(gt_f[:, 0:1], gb_f[:, 0:1]).then_inc(s_pos, 1)

            def place_hot(j):
                if j >= HS:
                    dve.wait_ge(s_ph_used, j - HS + 1)
                s = j % HS
                V.tensor_scalar(hot_r[e_, s, :], iota16[e_, 0:P], pos_lo[e_, j:j + 1], None, ALU.is_equal)
                for i, v in enumerate((src1, dlo)):
                    last = V.tensor_scalar(hot_c[e_, s, i, :], iota16[e_, :], pos_hi[e_, j:j + 1], v[e_, j:j + 1],
                                           ALU.is_equal, ALU.mult)
                last.then_inc(s_ph, 1)

            for i, (m, lo, w) in enumerate(G_PIECES):
                off, n = UPPER[m] + lo - m * P, first["G"] + i
                evac_lo(n, gu_lo[:, off:off + w], ps[:, n % NB, 0:w], gu_hi[:, off:off + w])
                if i >= len(G_PIECES) - UNITS:
                    split_lo(u)
                    u += 1
            for i, keys in enumerate(LOW_BANKS):
                n, w = first["LOW"] + 2 * i + 1, len(keys) * P
                dve.wait_ge(s_full, n + 1)
                nc.vector.tensor_copy(gl_lo[:, LOWER[keys[0]]:LOWER[keys[0]] + w], ps[:, n % NB, 0:w]).then_inc(s_free_dve, 1)
            for h in range(NH):
                for m in range(KB):
                    n = first[f"T{h}"] + m
                    for j in place_chunks(2 * h, m):
                        place_hot(j)
                    evac_lo(n, t_lo[:, m, :], ps[:, n % NB, :], t_hi[:, m, :])
                    if h == 1 and 1 <= m <= UNITS:
                        split_lo(u)
                        u += 1
                for m in range(KB):
                    n = first[f"KV{h}"] + m
                    for j in place_chunks(2 * h + 1, m):
                        place_hot(j)
                    dve.wait_ge(s_full, n + 1)
                    k = 2 * h + m // 4
                    if k >= 1:
                        dve.wait_ge(s_kvs[m % 4], 16 * k)
                    nc.vector.tensor_copy(kv_out[:, m % 4], ps[:, n % NB, :]).then_inc(s_free_dve, 1)
                    split_lo(u)
                    u += 1
                    if h == 1:
                        for t in ([m] if m < KB - 1 else range(m, NT)):
                            w = ROWS[t]
                            dve.wait_ge(s_x[t], 32)
                            nc.vector.tensor_scalar(acc[0:w, t, :], acc[0:w, t, :], mean[0:w, t:t + 1], rstd[0:w, t:t + 1],
                                                    ALU.subtract, ALU.mult).then_inc(s_xn2, 1)
            dve.wait_ge(s_ph_used, EC)
            V.tensor_copy(s_tab[:, :], ps[:, 7, 0:NC])
            V.tensor_copy(d_tab[:, :], ps[:, 7, NC:2 * NC]).then_inc(s_tab_done, 1)
            for m in range(4):
                dve.wait_ge(s_kvs[m], 16 * 2 * NH)
            for t in range(NT):
                for g in range(2):
                    w = ROWS[t]
                    n = first["XT"] + 2 * t + g
                    evac_lo(n, xt_lo[:, MB * g:MB * g + MB, t * P:t * P + w],
                            ps[:, n % NB, :].rearrange("p (b c) -> p b c", c=P)[:, :, 0:w],
                            xt_hi[:, MB * g:MB * g + MB, t * P:t * P + w])
            for h in range(NH):
                for t in range(NT):
                    if t < UNITS:
                        split_lo(u)
                        u += 1
                for t in range(NT):
                    n, w = first[f"QR{h}"] + t, ROWS[t]
                    dve.wait_ge(s_free_act, released(first[f"QL{h}"] + t)[1])
                    dve.wait_ge(s_full, n + 1)
                    a = acc[0:w, t, h * HALF:(h + 1) * HALF]
                    nc.vector.tensor_tensor(a, ps[0:w, n % NB, :], a, ALU.mult).then_inc(s_free_dve, 1)
                    if t < UNITS:
                        split_lo(u)
                        u += 1

            def mix_out(t):
                w = ROWS[t]
                for h in range(NH):
                    n = mix_job(t, h)
                    dve.wait_ge(s_full, n + 1)
                    nc.vector.tensor_copy(acc[0:w, t, h * HALF:(h + 1) * HALF], ps[0:w, n % NB, :]).then_inc(s_free_dve, 1)

            for t in range(NT):
                if t >= 2:
                    mix_out(t - 2)
                for g in range(2):
                    n, q, w = qt_job(t, g), 2 * t + g, ROWS[t]
                    evac_lo(n, qt_lo[:, q % 3, :, 0:w],
                            ps[:, n % NB, :].rearrange("p (b c) -> p b c", c=P)[:, :, 0:w], qt_hi[:, q % 3, :, 0:w])
                if t == 0:
                    for _ in range(UNITS):
                        split_lo(u)
                        u += 1
            mix_out(NT - 2)
            mix_out(NT - 1)
            for _ in range(UNITS):
                split_lo(u)
                u += 1
            for _ in range(UNITS):
                split_lo(u)
                u += 1
            i = nc.vector.memset(al[:, :], 0.0)
            link(nc.vector.memset(ar[:, :], 0.0))
            dve.wait_ge(s_a, 16)
            for t in range(NT):
                w = ROWS[t]
                dve.wait_ge(s_free_act, released(first["H1"] + t)[1])
                for v, a in ((al, a_bc[0:w, 0:D]), (ar, a_bc[0:w, D:2 * D])):
                    link(nc.vector.tensor_tensor_reduce(out=a_junk[0:w, :], in0=acc[0:w, t, :], in1=a, scale=1.0, scalar=0.0,
                                                        op0=ALU.mult, op1=ALU.add, accum_out=v[0:w, t:t + 1]))
            for t in range(NT):
                w = ROWS[t]
                dve.wait_ge(s_hhi, t + 1)
                i = nc.vector.tensor_tensor(h_lo[0:w, t, :], acc[0:w, t, :], h_hi[0:w, t, :].bitcast(f32), ALU.subtract)
                i.then_inc(s_hlo, 1)
            dve.wait_ge(s_hlo, NT)
            for t in range(NT):
                nc.vector.tensor_scalar(acc[:, 0, t * P:(t + 1) * P] if t < 8 else acc[:, 1, (t - 8) * P:(t - 7) * P],
                                        ident[:, :], al[:, t:t + 1], None, ALU.mult).then_inc(s_diag, 1)
            dve.wait_ge(s_nodes, 1)
            dve.wait_ge(s_tab_done, 1)
            dve.wait_ge(s_zero, 1)

            def group_hots(g):
                for j in range(CK):
                    if not (isinstance(g, int) and g == 0):
                        dve.wait_ge(s_hot_used, g * CK + (j - CK + 1))
                    V.tensor_scalar(hot_s[:, j, :], nodes16[:, 0:NW], s_tab[:, bass.ds(g * CK + j, 1)], None, ALU.is_equal)
                    V.tensor_scalar(hot_d[:, j, :], iota128[:, :], d_tab[:, bass.ds(g * CK + j, 1)], None,
                                    ALU.is_equal).then_inc(s_hot, 1)

            def group_add(a, g):
                dve.wait_ge(s_gcnt, g + 1)
                if not (isinstance(g, int) and g == 0):
                    dve.wait_ge(s_add, g)
                tile = dve.value_load(g_tile[0:1, bass.ds(g, 1)], min_val=0, max_val=NT - 1)
                c = cnt[:, bass.ds(tile, 1), :].rearrange("p a b -> p (a b)")
                V.tensor_tensor(c, c, gcnt[:, a, :], ALU.add).then_inc(s_add, 1)

            group_hots(0)
            group_hots(1)
            group_add(0, 0)
            with dve.Fori(1, NG // 2) as q:
                group_hots(q * 2)
                group_add(1, q * 2 + (-1))
                group_hots(q * 2 + 1)
                group_add(0, q * 2)
            group_add(1, NG - 1)
            dve.wait_ge(s_add, NG)
            for t in range(NT + 3):
                if t < NT:
                    w = ROWS[t]
                    if t == 0:
                        dve.wait_ge(s_free_act, released(first["AL"] + len(SCOLS) - 1)[1])
                    z = att[:, t % 2]
                    if t >= 2:
                        dve.wait_ge(s_atthi, t - 1)
                    link(nc.vector.tensor_tensor(z, al_bc[:, t * P:(t + 1) * P].unsqueeze(1).to_broadcast([P, NT, P]),
                                                 ar[:, :].unsqueeze(2).to_broadcast([P, NT, P]), ALU.add))
                    nc.vector.scalar_tensor_tensor(z, z, NEG_SLOPE, z, ALU.mult, ALU.max).then_inc(s_z, 1)
                    dve.wait_ge(s_e, t + 1)
                    nc.vector.scalar_tensor_tensor(z[:, :, 0:w], z[:, :, 0:w], F32_MAX, cnt[:, :, t * P:t * P + w],
                                                   ALU.min, ALU.mult).then_inc(s_att, 1)
                    dve.wait_ge(s_atthi, t + 1)
                    nc.vector.tensor_tensor(att_lo[:, t % 2], z, att_hi[:, t % 2].bitcast(f32), ALU.subtract).then_inc(s_attlo, 1)
                if t == 0:
                    dve.wait_ge(s_gwhi, 1)
                    nc.vector.tensor_tensor(gw_lo[:, :, :], gw[:, :, :], gw_hi[:, :, :].bitcast(f32), ALU.subtract).then_inc(s_gwlo, 1)
                if 1 <= t <= NT:
                    i = t - 1
                    w = ROWS[i]
                    n = gnn_job[i]
                    dve.wait_ge(s_full, n + 1)
                    rs = rsum[0:w, i:i + 1]
                    nc.vector.tensor_scalar(rs, ps[0:w, n % NB, 0:1], GNN_EPS, None, ALU.add).then_inc(s_free_dve, 1)
                    dve.wait_ge(s_free_dve, released(n)[1])
                    nc.vector.reciprocal(rs, rs).then_inc(s_rsum, 1)
                    hv = hp[0:w, i % 2, :]
                    dve.wait_ge(s_free_act, released(n + 2)[1])
                    link(nc.vector.scalar_tensor_tensor(hv, hneg[0:w, :], 1.0, hv, ALU.min, ALU.max))
                    dve.wait_ge(s_mx[i % 2], 32 * (i // 2 + 1))
                    link(nc.vector.scalar_tensor_tensor(hv, hv, -1.0, mix_in[0:w, i % 2, :], ALU.add, ALU.add))
                    x2v = x_in[0:w, i % 2, :]
                    nc.vector.tensor_tensor(x2v, x2v, hv, ALU.add).then_inc(s_x2, 1)
                    dve.wait_ge(s_x2, i + 1)
                    for g in range(2):
                        last = nc.vector.bn_stats(stats[0:w, g, :], x2v[:, g * HALF:(g + 1) * HALF])
                    link(last)
                    link(nc.vector.bn_aggr(mv[0:w, :], stats[0:w, :, :].rearrange("p a b -> p (a b)")))
                    nc.vector.tensor_scalar(mv[0:w, 1:2], mv[0:w, 1:2], LN_EPS, None, ALU.add).then_inc(s_var, 1)
                    dve.wait_ge(s_sd, NT + i + 1)
                    link(nc.vector.tensor_tensor(nt1[0:w, :], nt2[0:w, :], nt2[0:w, :], ALU.mult))
                    link(nc.vector.tensor_tensor(nt1[0:w, :], nt1[0:w, :], mv[0:w, 1:2], ALU.mult))
                    link(nc.vector.tensor_scalar(nt1[0:w, :], nt1[0:w, :], -0.5, 1.5, ALU.mult, ALU.add))
                    link(nc.vector.tensor_tensor(nt1[0:w, :], nt1[0:w, :], nt2[0:w, :], ALU.mult))
                    if i >= 2:
                        dve.wait_ge(s_full, tr_job[i - 2] + 2)
                        dve.wait_ge(s_xn2d[i % 2], 16 * (i // 2))
                    nc.vector.tensor_scalar(xn2[0:w, i % 2, :], x2v, mv[0:w, 0:1], nt1[0:w, :],
                                            ALU.subtract, ALU.mult).then_inc(s_xn2, 1)
                if t >= 3:
                    i = t - 3
                    w = ROWS[i]
                    for g in range(2):
                        n = tr_job[i] + g
                        evac_lo(n, xg_lo[:, MB * g:MB * g + MB, 0:w],
                                ps[:, n % NB, :].rearrange("p (b c) -> p b c", c=P)[:, :, 0:w],
                                xg_hi[:, MB * g:MB * g + MB, 0:w])

            dve.wait_ge(s_tri2, 3)
            link(V.memset(sc[:, :, :], 0.0))
            dve.wait_ge(s_gate_used, NT)
            gps = ps[:, 7, 0:NT * NE].rearrange("p (t e) -> p t e", e=NE)

            def over_experts(v):
                return v.unsqueeze(2).to_broadcast([P, NT, NE])

            def over_tiles(v):
                return v.unsqueeze(1).to_broadcast([P, NT, NE])

            if ROWS[-1] == P:
                link(V.tensor_copy(sc[:, :, :], gps))
            else:
                V.tensor_copy(sc[:, 0:NT - 1, :], gps[:, 0:NT - 1, :])
                link(V.tensor_copy(sc[0:ROWS[-1], NT - 1, :], gps[0:ROWS[-1], NT - 1, :]))
            S = sc[:, :, :]
            link(V.tensor_tensor(S, S, over_tiles(gb[:, :]), ALU.add))
            link(V.tensor_scalar(S, S, GATE_EPS, None, ALU.max))
            link(V.tensor_reduce(g_m[:, :], S, AX.X, ALU.max))
            V.tensor_tensor(g_p[:, :, :], S, over_experts(g_m[:, :]), ALU.subtract).then_inc(s_gate, 1)

            def choose(pick, scores):
                link(V.tensor_tensor(g_key[:, :, :], scores, over_experts(g_m[:, :]), ALU.is_ge))
                link(V.tensor_tensor(g_key[:, :, :], g_key[:, :, :], over_tiles(rank[:, :]), ALU.mult))
                link(V.tensor_reduce(g_t[:, :], g_key[:, :, :], AX.X, ALU.max))
                link(V.tensor_tensor(pick, g_key[:, :, :], over_experts(g_t[:, :]), ALU.is_equal))

            choose(g_one[:, :, :], S)
            link(V.scalar_tensor_tensor(g_s2[:, :, :], g_one[:, :, :], -1e30, S, ALU.mult, ALU.add))
            link(V.tensor_reduce(g_m[:, :], g_s2[:, :, :], AX.X, ALU.max))
            choose(g_two[:, :, :], g_s2[:, :, :])
            V.tensor_scalar(valid[:, :], tok[:, :], float(N), None, ALU.is_lt)
            link(V.tensor_tensor(g_mask[:, :, :], g_one[:, :, :], g_two[:, :, :], ALU.add))
            V.tensor_tensor(tokv[:, :], tok[:, :], valid[:, :], ALU.mult)
            link(V.tensor_tensor(g_in[:, :, :], g_mask[:, :, :].rearrange("p t e -> p e t"),
                                 valid[:, :].unsqueeze(1).to_broadcast([P, NE, NT]), ALU.mult))
            flat2 = g_in[:, :, :].rearrange("p a b -> p (a b)")
            link(V.tensor_tensor_scan(g_run[:, :, :].rearrange("p a b -> p (a b)"), flat2, flat2, 0.0, ALU.add, ALU.max))
            link(V.memset(g_ends[:, :], 0.0))
            link(V.tensor_copy(g_ends[:, 1:NE + 1], g_run[:, :, NT - 1]))
            V.tensor_tensor(g_tot[:, :], g_ends[:, 1:NE + 1], g_ends[:, 0:NE], ALU.subtract).then_inc(s_gtot, 1)
            dve.wait_ge(s_gtotp, 1)
            link(V.tensor_scalar(g_nbi[:, :], ps[:, 7, NE:2 * NE], float(P - 1), None, ALU.add))
            link(V.tensor_scalar(g_nbi[:, :], g_nbi[:, :], P.bit_length() - 1, None, ALU.logical_shift_right))
            link(V.tensor_copy(g_nb[:, :], g_nbi[:, :]))
            link(V.tensor_scalar(g_nb[:, :], g_nb[:, :], 1.0, None, ALU.max))
            link(V.tensor_tensor_scan(g_cum[:, :], g_nb[:, :], g_nb[:, :], 0.0, ALU.add, ALU.max))
            V.memset(bounds[:, 0:1], 0)
            V.tensor_copy(bounds[:, 1:NE + 1], g_cum[:, :])
            link(V.tensor_tensor(g_place[:, :], g_cum[:, :], g_nb[:, :], ALU.subtract))
            link(V.scalar_tensor_tensor(g_place[:, :], g_place[:, :], float(P), ps[:, 7, 0:NE], ALU.mult, ALU.add))
            link(V.scalar_tensor_tensor(g_place[:, :], g_place[:, :], -1.0, g_ends[:, 0:NE], ALU.add, ALU.subtract))
            link(V.tensor_tensor(g_pos[:, :, :], g_run[:, :, :].rearrange("p e t -> p t e"), over_tiles(g_place[:, :]), ALU.add))
            for c, pick in enumerate((g_one, g_two)):
                link(V.tensor_tensor(g_key[:, :, :], g_pos[:, :, :], pick[:, :, :], ALU.mult))
                link(V.tensor_reduce(p_f[:, c, :], g_key[:, :, :], AX.X, ALU.add))
            link(V.tensor_copy(pos12[:, :, :], p_f[:, :, :]))
            link(V.tensor_scalar(p_a[:, :, :], pos12[:, :, :], P - 1, None, ALU.bitwise_and))
            link(V.tensor_copy(p_lo[:, :, :], p_a[:, :, :]))
            link(V.tensor_scalar(p_a[:, :, :], pos12[:, :, :], P.bit_length() - 1, None, ALU.logical_shift_right))
            link(V.tensor_copy(p_hi[:, :, :], p_a[:, :, :]))
            for t in range(NT):
                for c in range(2):
                    V.tensor_scalar(tok_r[:, 2 * t + c, :], io16[:, :], p_lo[:, c, t:t + 1], None, ALU.is_equal)
                    last = V.tensor_scalar(tok_c[:, 2 * t + c, :], io16[:, 0:NSLOT], p_hi[:, c, t:t + 1], tokv[:, t:t + 1],
                                           ALU.is_equal, ALU.mult)
                last.then_inc(s_toks, 1)
            dve.wait_ge(s_tokp, 1)
            V.tensor_copy(tok_of[:, :], ps[:, 7, 0:NSLOT]).then_inc(s_route, 1)
            dve.sem_inc(s_ye, 2)

            def expert_lo(e):
                for k in range(KB):
                    dve.wait_ge(s_ehi, KB * e + k + 1)
                    V.tensor_tensor(e_lo[e % 2][:, k, :], e_raw[:, k, :], e_hi[e % 2][:, k, :].bitcast(f32),
                                    ALU.subtract).then_inc(s_elo, 1)

            def block_lo(i, g):
                dve.wait_ge(s_lhi, i * 2 + (g + 1))
                V.tensor_tensor(lt_lo[:, MB * g:MB * g + MB, :], ps[:, 4 + g, :].rearrange("p (b c) -> p b c", c=P),
                                lt_hi[:, MB * g:MB * g + MB, :].bitcast(f32), ALU.subtract).then_inc(s_llo, 1)

            expert_lo(0)
            for g in range(2):
                block_lo(0, g)
            dve.wait_ge(s_gexp, 1)
            link(V.tensor_reduce(g_t[:, :], g_p[:, :, :], AX.X, ALU.add))
            link(V.reciprocal(g_t[:, :], g_t[:, :]))
            link(V.tensor_tensor(g_p[:, :, :], g_p[:, :, :], over_experts(g_t[:, :]), ALU.mult))
            link(V.tensor_scalar(g_p[:, :, :], g_p[:, :, :], W_THRES, None, ALU.max))
            for c, pick in enumerate((g_one, g_two)):
                link(V.tensor_tensor(g_key[:, :, :], g_p[:, :, :], pick[:, :, :], ALU.mult))
                link(V.tensor_reduce(w12[:, c, :], g_key[:, :, :], AX.X, ALU.add))
            link(V.tensor_tensor(g_t[:, :], w12[:, 0, :], w12[:, 1, :], ALU.add))
            link(V.reciprocal(g_t[:, :], g_t[:, :]))
            link(V.tensor_scalar(g_t[:, :], g_t[:, :], 1.0 / TOPK, None, ALU.mult))
            link(V.tensor_tensor(w12[:, :, :], w12[:, :, :], g_t[:, :].unsqueeze(1).to_broadcast([P, 2, NT]), ALU.mult))

            first_block = [dve.value_load(bounds[0:1, e:e + 1], min_val=0, max_val=NBLK) for e in range(NE + 1)]
            for e in range(NE):
                if e + 1 < NE:
                    expert_lo(e + 1)
                dve.wait_ge(s_bias[e % 2], 16 * (e // 2 + 1))
                with dve.Fori(first_block[e], first_block[e + 1]) as i:
                    block_lo(i + 1, 0)
                    dve.wait_ge(s_ys, i * 16 + 16)
                    for h in range(NH):
                        c = slice(h * HALF, (h + 1) * HALF)
                        dve.wait_ge(s_mm, i * 3 + (2 + h))
                        V.tensor_tensor(y[:, c], ps[:, h, :], bias[:, e % 2, c], ALU.add).then_inc(s_ye, 1)
                    block_lo(i + 1, 1)
            dve.wait_ge(s_x2r, 16 * NT)
            for t in range(NT):
                w = ROWS[t]
                dve.wait_ge(s_y12[t], 32)
                v = x2[0:w, t, :]
                link(V.scalar_tensor_tensor(v, y12[0:w, t, 0, :], w12[0:w, 0, t:t + 1], v, ALU.mult, ALU.add))
                V.scalar_tensor_tensor(v, y12[0:w, t, 1, :], w12[0:w, 1, t:t + 1], v, ALU.mult, ALU.add).then_inc(s_finw, 1)

        @block.tensor
        def _(pe):
            def bank_free(n):
                if n >= NB:
                    pe.wait_ge(*released(n - NB))

            def chunk_ready(c):
                pe.wait_ge(s_wlo, UNITS * (c + 1))

            def three(o, lh, ll, rh, rl, k, last_k):
                nc.tensor.matmul(o, lh, rh, start=(k == 0), stop=False)
                nc.tensor.matmul(o, lh, rl, start=False, stop=False)
                return nc.tensor.matmul(o, ll, rh, start=False, stop=(k == last_k))

            for i, (m, lo, w) in enumerate(G_PIECES):
                n = first["G"] + i
                bank_free(n)
                for t in range(NT):
                    if i == 0:
                        pe.wait_ge(s_xlo, t + 1)
                    r = ROWS[t]
                    a, b = (v[0:r, t, m * P:(m + 1) * P] for v in (xn_hi, xn_lo))
                    c, d = (v[0:r, t, lo:lo + w] for v in (xn_hi, xn_lo))
                    last = three(ps[:, n % NB, 0:w], a, b, c, d, t, NT - 1)
                last.then_inc(s_full, 1)
                if i == len(G_PIECES) // 2:
                    pe.wait_ge(s_tot, 1)
                    nc.tensor.matmul(ps[:, 7, 0:NT], tri[0:EP, :], tot[0:EP, :], start=True, stop=True)
                    nc.tensor.matmul(ps[:, 7, NT:2 * NT], ones[0:EP, :], tot[0:EP, :], start=True, stop=True).then_inc(s_totp, 1)
            pe.wait_ge(s_const, 3)
            for i, keys in enumerate(LOW_BANKS):
                for part, (g, n) in enumerate(((gu_hi, first["LOW"] + 2 * i), (gu_lo, first["LOW"] + 2 * i + 1))):
                    bank_free(n)
                    if i == 0:
                        pe.wait_ge(s_free_dve, released(first["G"] + len(G_PIECES) - 1)[1])
                    for j, (row, col) in enumerate(keys):
                        off = UPPER[col] + (row - col) * P
                        last = nc.tensor.transpose(ps[:, n % NB, j * P:(j + 1) * P], g[:, off:off + P].bitcast(f32), ident[:, :])
                    last.then_inc(s_full, 1)

            def place_edges(j):
                pe.wait_ge(s_ph, j + 1)
                if j == 0:
                    pe.wait_ge(s_pos, 1)
                s = j % HS
                nc.tensor.matmul(ps[:, 7, 0:2 * NC], hot_r[0:EP, s, :], hot_c[0:EP, s, :, :].rearrange("p a b -> p (a b)"),
                                 start=(j == 0), stop=(j == EC - 1)).then_inc(s_ph_used, 1)

            def gram(k, m, part):
                if k <= m:
                    off = UPPER[k] + (m - k) * P
                    return (gu_hi, gu_lo)[part][:, off:off + P]
                off = LOWER[(k, m)]
                return (gl_hi, gl_lo)[part][:, off:off + P]

            for h in range(NH):
                c = 3 * h
                chunk_ready(c)
                if h == 0:
                    pe.wait_ge(*released(first["T0"] - 1))
                    pe.wait_ge(*released(first["T0"] - 2))
                for m in range(KB):
                    n = first[f"T{h}"] + m
                    bank_free(n)
                    for k in range(KB):
                        last = three(ps[:, n % NB, :], gram(k, m, 0), gram(k, m, 1), w_hi[c % 2][:, k, :], w_lo[c % 2][:, k, :], k, KB - 1)
                    last.then_inc(s_full, 1)
                    for j in place_chunks(2 * h, m):
                        place_edges(j)
                for m in range(KB):
                    c = 3 * h + 1 + m // MB
                    if m % MB == 0:
                        chunk_ready(c)
                    n = first[f"KV{h}"] + m
                    bank_free(n)
                    col = (m % MB) * P
                    for k in range(KB):
                        if m == 0:
                            pe.wait_ge(*released(first[f"T{h}"] + k))
                        last = three(ps[:, n % NB, :], w_hi[c % 2][:, k, col:col + P], w_lo[c % 2][:, k, col:col + P],
                                     t_hi[:, k, :], t_lo[:, k, :], k, KB - 1)
                    last.then_inc(s_full, 1)
                    for j in place_chunks(2 * h + 1, m):
                        place_edges(j)

            def transposes(n, tile, g, w):
                for b in range(MB):
                    last = nc.tensor.transpose(ps[:, n % NB, b * P:b * P + w], tile[0:w, (MB * g + b) * P:(MB * g + b + 1) * P],
                                               ident[0:w, 0:w])
                last.then_inc(s_full, 1)

            for t in range(NT):
                pe.wait_ge(s_xn2, t + 1)
                for g in range(2):
                    n = first["XT"] + 2 * t + g
                    bank_free(n)
                    transposes(n, acc[:, t, :], g, ROWS[t])

            def nodes_times_chunk(c, name, start_job):
                chunk_ready(c)
                for t in range(NT):
                    n, w = start_job + t, ROWS[t]
                    bank_free(n)
                    for k in range(KB):
                        last = three(ps[0:w, n % NB, :], xt_hi[:, k, t * P:t * P + w], xt_lo[:, k, t * P:t * P + w],
                                     w_hi[c % 2][:, k, :], w_lo[c % 2][:, k, :], k, KB - 1)
                    last.then_inc(s_full, 1)

            pe.wait_ge(*released(first["XT"] + 2 * NT - 1))
            for h in range(NH):
                nodes_times_chunk(6 + 2 * h, "ql", first[f"QL{h}"])
                nodes_times_chunk(7 + 2 * h, "qr", first[f"QR{h}"])

            def q_transposes(t):
                pe.wait_ge(*released(first["QR1"] + t))
                for g in range(2):
                    n = qt_job(t, g)
                    bank_free(n)
                    transposes(n, acc[:, t, :], g, ROWS[t])

            q_transposes(0)
            for t in range(NT):
                if t + 1 < NT:
                    q_transposes(t + 1)
                w = ROWS[t]
                for h in range(NH):
                    n = mix_job(t, h)
                    bank_free(n)
                    if t == 0:
                        chunk_ready(C_KV + h)
                    pe.wait_ge(*released(qt_job(t, 1)))
                    for k in range(KB):
                        s = (2 * t + k // MB) % 3
                        last = three(ps[0:w, n % NB, :], qt_hi[:, s, k % MB, 0:w], qt_lo[:, s, k % MB, 0:w],
                                     w_hi[h][:, k, :], w_lo[h][:, k, :], k, KB - 1)
                    last.then_inc(s_full, 1)
            for h in range(NH):
                nodes_times_chunk(C_W + h, "h", first[f"H{h}"])
            for i in range(len(SCOLS)):
                n = first["AL"] + i
                bank_free(n)
                tiles = range(4 * i, min(NT, 4 * i + 4))
                for t in tiles:
                    pe.wait_ge(s_diag, t + 1)
                    d = acc[:, 0, t * P:(t + 1) * P] if t < 8 else acc[:, 1, (t - 8) * P:(t - 7) * P]
                    last = nc.tensor.matmul(ps[:, n % NB, (t % 4) * P:(t % 4 + 1) * P], ones[:, :], d, start=True, stop=True)
                last.then_inc(s_full, 1)
            for n in range(first["AL"] - 4, first["AL"] + len(SCOLS)):
                pe.wait_ge(*released(n))

            def count_group(a, g):
                if not (isinstance(g, int) and g < 2):
                    pe.wait_ge(s_gcnt, g + (-1))
                for j in range(CK):
                    pe.wait_ge(s_hot, g * CK + (j + 1))
                    for b, (c, w) in enumerate(SCOLS):
                        last = nc.tensor.matmul(ps[:, 3 * a + b, 0:w], hot_d[:, j, :], hot_s[:, j, c:c + w],
                                                start=(j == 0), stop=(j == CK - 1))
                    last.then_inc(s_hot_used, 1)

            count_group(0, 0)
            count_group(1, 1)
            with pe.Fori(1, NG // 2) as q:
                for a in range(2):
                    count_group(a, q * 2 + a)
            pe.wait_ge(s_gcnt, NG)
            for t in range(NT + 3):
                if t < NT:
                    w = ROWS[t]
                    pe.wait_ge(s_attlo, t + 1)
                    if t == 0:
                        pe.wait_ge(s_hlo, NT)
                    n = gnn_job[t]
                    bank_free(n)
                    for d in range(NT):
                        r = ROWS[d]
                        nc.tensor.matmul(ps[0:w, n % NB, 0:2], att_hi[0:r, t % 2, d, 0:w], ones_r[0:r, :], start=(d == 0), stop=False)
                        last = nc.tensor.matmul(ps[0:w, n % NB, 0:2], att_lo[0:r, t % 2, d, 0:w], ones_r[0:r, :], start=False, stop=(d == NT - 1))
                    last.then_inc(s_full, 1)
                    for h in range(NH):
                        n = gnn_job[t] + 1 + h
                        bank_free(n)
                        for d in range(NT):
                            r = ROWS[d]
                            last = three(ps[0:w, n % NB, :], att_hi[0:r, t % 2, d, 0:w], att_lo[0:r, t % 2, d, 0:w],
                                         h_hi[0:r, d, h * HALF:(h + 1) * HALF], h_lo[0:r, d, h * HALF:(h + 1) * HALF], d, NT - 1)
                        last.then_inc(s_full, 1)
                if t >= 3:
                    i = t - 3
                    w = ROWS[i]
                    if i == 0:
                        pe.wait_ge(s_gwlo, 1)
                        pe.wait_ge(s_tab_done, 1)
                    pe.wait_ge(*released(tr_job[i] + 1))
                    for k in range(KB):
                        last = three(ps[0:w, 7, i * NE:(i + 1) * NE], xg_hi[:, k, 0:w], xg_lo[:, k, 0:w],
                                     gw_hi[:, k, :], gw_lo[:, k, :], k, KB - 1)
                    last.then_inc(s_gate_used, 1)
                if 2 <= t < NT + 2:
                    i = t - 2
                    pe.wait_ge(s_xn2, NT + i + 1)
                    for g in range(2):
                        n = tr_job[i] + g
                        bank_free(n)
                        transposes(n, xn2[:, i % 2, :], g, ROWS[i])
            pe.wait_ge(s_gtot, 1)
            nc.tensor.matmul(ps[:, 7, 0:NE], tri2[:, :], g_tot[:, :], start=True, stop=True)
            nc.tensor.matmul(ps[:, 7, NE:2 * NE], ones[:, :], g_tot[:, :], start=True, stop=True).then_inc(s_gtotp, 1)
            for t in range(NT):
                pe.wait_ge(s_toks, t + 1)
                for c in range(2):
                    last = nc.tensor.matmul(ps[:, 7, 0:NSLOT], tok_r[:, 2 * t + c, :], tok_c[:, 2 * t + c, :],
                                            start=(t + c == 0), stop=(t == NT - 1 and c == 1))
            last.then_inc(s_tokp, 1)

            def block_transposes(g):
                for b in range(MB):
                    k = MB * g + b
                    last = nc.tensor.transpose(ps[:, 4 + g, b * P:(b + 1) * P], gx[:, k * P:(k + 1) * P], ident[:, :])
                last.then_inc(s_tr, 1)

            pe.wait_ge(s_gx, 16)
            for g in range(2):
                block_transposes(g)
            first_block = [pe.value_load(bounds[0:1, e:e + 1], min_val=0, max_val=NBLK) for e in range(NE + 1)]
            for e in range(NE):
                pe.wait_ge(s_elo, KB * (e + 1))
                with pe.Fori(first_block[e], first_block[e + 1]) as i:
                    for g in range(2):
                        pe.wait_ge(s_llo, i * 2 + (g + 1))
                        for h in range(NH):
                            c = slice(h * HALF, (h + 1) * HALF)
                            if g == 0:
                                pe.wait_ge(s_ye, i * 2 + (1 + h))
                            for k in range(MB * g, MB * g + MB):
                                last = three(ps[:, h, :], lt_hi[:, k, :], lt_lo[:, k, :], e_hi[e % 2][:, k, c], e_lo[e % 2][:, k, c],
                                             k, KB - 1)
                            if g == 1 or h == 1:
                                last.then_inc(s_mm, 1)
                        if g == 0:
                            pe.wait_ge(s_gx, i * 16 + 32)
                        block_transposes(g)


_INS = ["x", "src", "dst", "L0_gnn_W", "L0_gnn_a", "L0_mix_w_query_left", "L0_mix_w_query_right", "L0_mix_w_key",
        "L0_mix_w_value", "L0_ffn_gate_W", "L0_ffn_gate_b", "L0_ffn_expert_W", "L0_ffn_expert_b"]


def kernel(**inputs):
    import numpy as np
    import concourse.bacc as bacc
    from concourse.bass_utils import run_bass_kernel_spmd

    nc = bacc.Bacc("TRN2", target_bir_lowering=False, num_devices=1)
    arrays, args = {}, []
    for name in _INS:
        a = np.ascontiguousarray(inputs[name])
        arrays["in_" + name] = a
        args.append(nc.dram_tensor("in_" + name, a.shape, mybir.dt.from_np(a.dtype), kind="ExternalInput").ap())
    y = nc.dram_tensor("out_0", inputs["x"].shape, mybir.dt.float32, kind="ExternalOutput").ap()
    gps_layer(nc, *args, y)
    r = run_bass_kernel_spmd(nc, [arrays], core_ids=[0])
    return r.results[0]["out_0"]
```

```python
from contextlib import ExitStack

import concourse.bass as bass
from concourse import mybir


def gps_layer(nc, x, src, dst, gnn_W, gnn_a, w_ql, w_qr, w_key, w_value, gate_W, gate_b, expert_W, expert_b, out):
    f32, f32r = mybir.dt.float32, mybir.dt.float32r
    f16, i32, i16 = mybir.dt.float16, mybir.dt.int32, mybir.dt.int16
    ALU, ACT, AX = mybir.AluOpType, mybir.ActivationFunctionType, mybir.AxisListType

    P = 128
    N, D = x.shape
    E = src.shape[0]
    NE = expert_b.shape[0]
    NT = (N + P - 1) // P
    KB = D // P
    HALF = 512
    NH = D // HALF
    MB = HALF // P
    ROWS = [min(P, N - t * P) for t in range(NT)]
    EP = 125
    EC = E // EP
    assert EP * EC == E
    NB = 7
    CK = 4
    GE = CK * P
    NG = (E + NT * GE) // GE
    NG += NG % 2
    NC = NG * CK
    NW = (N + 3) // 4 * 4
    NEG_SLOPE, GNN_EPS, LN_EPS, GATE_EPS, W_THRES, TOPK = 0.1, 1e-5, 1e-5, 1e-4, 0.1, 2
    NBLK = (TOPK * N + NE * P) // P
    NSLOT = NBLK + 1
    AT_ONCE = 3
    F32_MAX = 3.4028234e38
    SCOLS = [(c, min(HALF, NW - c)) for c in range(0, NW, HALF)]

    base = (nc.sbuf_base + 31) // 32 * 32
    RING, BIG, ACC, RAW, QT, SMALL = 0, 16384, 36864, 47104, 49152, 52224

    ctx = ExitStack()
    with ctx:
        def at(name, word, shape, dt=f32):
            return nc.alloc_sbuf_tensor_at(name, shape, dt, offset=base + 4 * word)

        small_at = [SMALL]

        def small(name, shape, dt=f32):
            words = 1
            for s in shape[1:]:
                words *= s
            t = at(name, small_at[0], shape, dt)
            small_at[0] += (words + 7) // 8 * 8
            assert base + 4 * small_at[0] <= nc.sbuf_usable_end
            return t

        def sem(name):
            return ctx.enter_context(nc.semaphore(name))

        w_hi = [at(f"w_hi{s}", RING + 8192 * s, [P, KB, HALF], f32r) for s in range(2)]
        w_lo = [at(f"w_lo{s}", RING + 8192 * s + 4096, [P, KB, HALF], f32r) for s in range(2)]
        w_raw = at("w_raw", RAW, [P, 2, 2, HALF])
        acc = at("acc", ACC, [P, NT, D])
        xn_hi = at("xn_hi", BIG, [P, NT, D], f32r)
        xn_lo = at("xn_lo", BIG + 10240, [P, NT, D], f32r)
        UPPER = [sum(KB - i for i in range(m)) * P for m in range(KB)]
        NUP = UPPER[-1] + P
        LOWER = {}
        for m in range(KB):
            for n in range(m + 1, KB):
                LOWER[(n, m)] = len(LOWER) * P
        NLOW = len(LOWER) * P
        gu_hi = at("gu_hi", ACC, [P, NUP], f32r)
        gu_lo = at("gu_lo", ACC + NUP, [P, NUP], f32r)
        gl_hi = at("gl_hi", BIG, [P, NLOW], f32r)
        gl_lo = at("gl_lo", BIG + NLOW, [P, NLOW], f32r)
        T0 = BIG + 2 * NLOW
        t_hi = at("t_hi", T0, [P, KB, HALF], f32r)
        t_lo = at("t_lo", T0 + 4096, [P, KB, HALF], f32r)
        kv_out = at("kv_out", T0 + 8192, [P, 4, HALF])
        xt_hi = at("xt_hi", BIG, [P, KB, N], f32r)
        xt_lo = at("xt_lo", BIG + KB * N, [P, KB, N], f32r)
        qt_hi = at("qt_hi", QT, [P, 3, MB, P], f32r)
        qt_lo = at("qt_lo", QT + 1536, [P, 3, MB, P], f32r)
        a_bc = at("a_bc", QT, [P, 2 * D])
        a_junk = at("a_junk", QT + 2 * D, [P, D])
        h_hi = at("h_hi", BIG, [P, NT, D], f32r)
        h_lo = at("h_lo", BIG + 10240, [P, NT, D], f32r)
        cnt = at("cnt", RING, [P, NT, NW], i16)
        al_bc = at("al_bc", RING + 6400, [P, NT * P])
        hot_s = at("hot_s", QT, [P, CK, NW], f16)
        hot_d = at("hot_d", QT + 2560, [P, CK, P], f16)
        iota128 = at("iota128", QT + 2816, [P, P], f16)
        nodes16 = at("nodes16", RAW, [P, NT * P], f16)
        zeros16 = at("zeros16", QT + 2880, [P, P], f16)
        diag = at("diag", RAW + 640, [P, NT, P])
        R1 = RING + 8192
        src_i = at("src_i", R1, [P, EC], i32)
        dst_i = at("dst_i", R1 + 160, [P, EC], i32)
        tile_i = at("tile_i", R1 + 320, [P, EC], i32)
        pos_i = at("pos_i", R1 + 480, [P, EC], i32)
        tile_f = at("tile_f", R1 + 640, [P, EC])
        pos_f = at("pos_f", R1 + 800, [P, EC])
        in_tile = at("in_tile", R1 + 960, [P, NT, EC], f16)
        run = at("run", R1 + 1760, [P, NT, EC], f16)
        place = at("place", R1 + 2560, [P, NT, EC])
        tri = at("tri", R1 + 4160, [P, P])
        tiles10 = at("tiles10", R1 + 4288, [P, NT])
        ends = at("ends", R1 + 4368, [P, NT + 1])
        tot = at("tot", R1 + 4384, [P, NT])
        gb_i = at("gb_i", R1 + 4400, [P, NT], i32)
        gb_f = at("gb_f", R1 + 4416, [P, NT])
        gb_cum = at("gb_cum", R1 + 4432, [P, NT])
        place0 = at("place0", R1 + 4448, [P, NT])
        HS = 8
        hot_r = at("hot_r", QT, [P, HS, P], f16)
        hot_c = at("hot_c", QT + 512, [P, HS, 2, NC], f16)
        QE = QT + 512 + HS * NC
        pos_lo = at("pos_lo", QE, [P, EC])
        pos_hi = at("pos_hi", QE + 160, [P, EC])
        src1 = at("src1", QE + 320, [P, EC])
        dlo = at("dlo", QE + 480, [P, EC])
        iota16 = at("iota16", QE + 640, [P, NC], f16)
        assert QE + 640 + NC // 2 <= SMALL and NC >= P
        att = at("att", ACC, [P, 2, NT, P])
        att_hi = at("att_hi", ACC + 2560, [P, 2, NT, P], f32r)
        att_lo = at("att_lo", ACC + 5120, [P, 2, NT, P], f32r)
        hp = at("hp", ACC + 7680, [P, 2, D])
        mix_in = at("mix_in", RAW, [P, 2, D])
        x_in = at("x_in", QT, [P, 2, D])
        hneg = at("hneg", QT + 2 * D, [P, D])
        xn2 = at("xn2", RING + 7680, [P, 2, D])
        xg = at("xg", RING + 9728, [P, 2, KB, P])
        gw = at("gw", RING + 11776, [P, KB, NE])
        att_sum = at("att_sum", RING + 12000, [P, 2, P])
        att_part = at("att_part", RING + 12256, [P, NT // 2, P])
        assert NT == 10
        e_hi = [at("e_hi0", RING, [P, KB, D], f32r), at("e_hi1", BIG, [P, KB, D], f32r)]
        e_lo = [at("e_lo0", RING + KB * D, [P, KB, D], f32r), at("e_lo1", BIG + KB * D, [P, KB, D], f32r)]
        e_raw = [at(f"e_raw{k}", BIG + 2 * KB * D + k * D, [P, D]) for k in range(KB)]
        EX = BIG + 3 * KB * D
        gx = at("gx", EX, [P, D])
        lt_hi = at("lt_hi", EX + D, [P, KB, P], f32r)
        lt_lo = at("lt_lo", EX + 2 * D, [P, KB, P], f32r)
        y = at("y", EX + 3 * D, [P, D])
        bias = at("bias", EX + 4 * D, [P, 2, D])
        assert EX + 6 * D <= RAW
        EARLY = (SMALL - RAW) // D
        x2 = [at(f"x2_{t}", RAW + t * D if t < EARLY else RING + (t - EARLY) * D, [P, D]) for t in range(NT)]
        y_lower = [at(f"y_lower{t}", RING + (NT - EARLY + t) * D, [P, D]) for t in range(NT)]
        y_higher = [at(f"y_higher{t}", BIG + t * D, [P, D]) for t in range(NT)]
        G = RAW
        def gate(name, shape, dt=f32):
            nonlocal G
            words = 1
            for d in shape[1:]:
                words *= d
            t = at(name, G, shape, dt)
            G += (words + 7) // 8 * 8
            assert G <= SMALL
            return t

        g_p = gate("g_p", [P, NT, NE])
        g_key = gate("g_key", [P, NT, NE])
        g_s2 = gate("g_s2", [P, NT, NE])
        g_one = gate("g_one", [P, NT, NE])
        g_two = gate("g_two", [P, NT, NE])
        g_mask = gate("g_mask", [P, NT, NE])
        g_in = gate("g_in", [P, NE, NT])
        g_run = gate("g_run", [P, NE, NT])
        g_pos = gate("g_pos", [P, NT, NE])
        sc = gate("sc", [P, NT, NE])
        g_m = gate("g_m", [P, NT])
        g_t = gate("g_t", [P, NT])
        g_ends = gate("g_ends", [P, NE + 1])
        g_tot = gate("g_tot", [P, NE])
        g_nb = gate("g_nb", [P, NE])
        g_nbi = gate("g_nbi", [P, NE], i32)
        g_cum = gate("g_cum", [P, NE])
        g_place = gate("g_place", [P, NE])
        p_f = gate("p_f", [P, 2, NT])
        p_lo = gate("p_lo", [P, 2, NT])
        p_hi = gate("p_hi", [P, 2, NT])
        p_a = gate("p_a", [P, 2, NT], i32)
        tok = gate("tok", [P, NT])
        valid = gate("valid", [P, NT])
        tokv = gate("tokv", [P, NT])
        tri2 = gate("tri2", [P, P])
        io16 = gate("io16", [P, P], f16)
        tok_r = gate("tok_r", [P, 2 * NT, P], f16)
        tok_c = gate("tok_c", [P, 2 * NT, NSLOT], f16)

        ident = small("ident", [P, P])
        ones = small("ones", [P, P])
        stats = small("stats", [P, 2, 6])
        mvx = small("mvx", [P, 2, 2])
        sdx = small("sdx", [P, 2])
        mv = small("mv", [P, 2])
        mean = small("mean", [P, NT])
        rstd = small("rstd", [P, NT])
        nt1 = small("nt1", [P, 1])
        nt2 = small("nt2", [P, 1])
        al = small("al", [P, NT])
        ar = small("ar", [P, NT])
        rsum = small("rsum", [P, NT])
        s_tab = small("s_tab", [P, NC], f16)
        d_tab = small("d_tab", [P, NC], f16)
        g_first = small("g_first", [P, NT + 1], i32)
        gb = small("gb", [P, NE])
        w12 = small("w12", [P, 2, NT])
        pos12 = small("pos12", [P, 2, NT], i32)
        bounds = small("bounds", [P, NE + 1], i32)
        tok_of = small("tok_of", [P, NSLOT], i32)
        tok_now = small("tok_now", [P, 1], i32)
        hexp = small("hexp", [P, 1])
        rank = small("rank", [P, NE])

        ps = ctx.enter_context(nc.psum_tensor("ps", [P, 8, HALF], f32))

        kv_d = nc.dram_tensor("kv_d", (D, D), f32).ap()
        mix_d = nc.dram_tensor("mix_d", (N, D), f32).ap()
        x2_d = nc.dram_tensor("x2_d", (N, D), f32).ap()
        xn2_d = nc.dram_tensor("xn2_d", (N, D), f32).ap()
        y_d = nc.dram_tensor("y_d", ((NBLK + 1) * P, D), f32).ap()

        def half(w, h):
            return w.rearrange("(k p) n -> p k n", p=P)[:, :, h * HALF:(h + 1) * HALF]

        CH = [half(w_value, 0), half(w_key, 0), half(w_key, 1), half(w_value, 1), half(w_key, 0), half(w_key, 1),
              half(w_ql, 0), half(w_qr, 0), half(w_ql, 1), half(w_qr, 1), half(kv_d, 0), half(kv_d, 1),
              half(gnn_W, 0), half(gnn_W, 1)]
        C_KV, C_W, C_EXP = 10, 12, 14
        UNITS = 4

        owner, first = [], {}

        def phase(name, owners):
            first[name] = len(owner)
            owner.extend(owners)

        G_PIECES = []
        for m in range(KB):
            lo, width = m * P, D - m * P
            cut = [width] if width <= HALF else [HALF, width - HALF]
            for w in cut:
                G_PIECES.append((m, lo, w))
                lo += w
        phase("G", ["dve"] * len(G_PIECES))
        LOW_KEYS = list(LOWER)
        LOW_BANKS = [LOW_KEYS[i:i + 4] for i in range(0, len(LOW_KEYS), 4)]
        phase("LOW", ["act", "dve"] * len(LOW_BANKS))
        phase("T0", ["dve"] * KB)
        phase("KV0", ["dve"] * KB)
        phase("T1", ["dve"] * KB)
        phase("KV1", ["dve"] * KB)
        phase("XT", ["dve"] * (2 * NT))
        for h in range(NH):
            phase(f"QL{h}", ["act"] * NT)
            phase(f"QR{h}", ["dve"] * NT)
        phase("QTMIX", ["dve"] * (4 * NT))
        phase("H0", ["act"] * NT)
        phase("H1", ["act"] * NT)
        phase("AL", ["act"] * len(SCOLS))
        first["GNN"] = len(owner)
        gnn_job, tr_job = {}, {}
        for t in range(NT + 3):
            if t < NT:
                gnn_job[t] = len(owner)
                owner.extend(["dve", "act", "act"])
            if 2 <= t < NT + 2:
                tr_job[t - 2] = len(owner)
                owner.extend(["act"] * 2)

        def released(n):
            return (s_free_act if owner[n] == "act" else s_free_dve), owner[:n + 1].count(owner[n])

        def qt_job(t, i):
            return first["QTMIX"] + (0 if t == 0 else 4 * t - 2) + i

        def mix_job(t, h):
            return first["QTMIX"] + (4 + 4 * t if t < NT - 1 else 4 * NT - 2) + h

        s_x = [sem(f"s_xt{t}") for t in range(NT)]
        s_raw = [sem(f"s_raw{i}") for i in range(2)]
        s_const, s_edges, s_a, s_gw = (sem(n) for n in ("s_const", "s_edges", "s_a", "s_gw"))
        s_xn, s_xhi, s_xlo = sem("s_xn"), sem("s_xhi"), sem("s_xlo")
        s_whi, s_wlo = sem("s_whi"), sem("s_wlo")
        s_full, s_free_act, s_free_dve = sem("s_full"), sem("s_free_act"), sem("s_free_dve")
        s_hi = sem("s_hi")
        s_kvs = [sem(f"s_kvs{i}") for i in range(4)]
        s_xn2 = sem("s_xn2")
        s_mixs = sem("s_mixs")
        s_hhi, s_hlo = sem("s_hhi"), sem("s_hlo")
        s_diag = sem("s_diag")
        s_hot, s_hot_used, s_counted, s_cnt = sem("s_hot"), sem("s_hot_used"), sem("s_counted"), sem("s_cnt")
        s_tri, s_tot, s_totp, s_pos = sem("s_tri"), sem("s_tot"), sem("s_totp"), sem("s_pos")
        s_ph, s_ph_used, s_tab_done, s_nodes = sem("s_ph"), sem("s_ph_used"), sem("s_tab_done"), sem("s_nodes")
        s_z, s_e, s_att, s_atthi, s_attlo = sem("s_z"), sem("s_e"), sem("s_att"), sem("s_atthi"), sem("s_attlo")
        s_mx = [sem(f"s_mx{i}") for i in range(2)]
        s_part, s_sum = sem("s_part"), sem("s_sum")
        s_rsum, s_x2, s_xm = sem("s_rsum"), sem("s_x2"), sem("s_xm")
        s_x2s = [sem(f"s_x2s{i}") for i in range(2)]
        s_var, s_sd = sem("s_var"), sem("s_sd")
        s_xn2d = [sem(f"s_xn2d{i}") for i in range(2)]
        s_gate_used, s_gate, s_gexp = sem("s_gate_used"), sem("s_gate"), sem("s_gexp")
        s_tri2, s_gtot, s_gtotp, s_toks, s_tokp, s_route = (sem(n) for n in (
            "s_tri2", "s_gtot", "s_gtotp", "s_toks", "s_tokp", "s_route"))
        s_er = [sem(f"s_er{k}") for k in range(KB)]
        s_w12 = sem("s_w12")
        s_bias = [sem(f"s_bias{i}") for i in range(2)]
        s_ehi, s_elo = sem("s_ehi"), sem("s_elo")
        s_gx, s_tok, s_tok_in, s_tr, s_lhi, s_llo, s_mm, s_ye, s_ys, s_rest = (sem(n) for n in (
            "s_gx", "s_tok", "s_tok_in", "s_tr", "s_lhi", "s_llo", "s_mm", "s_ye", "s_ys", "s_rest"))
        s_x2r, s_fin, s_finw = sem("s_x2r"), sem("s_fin"), sem("s_finw")
        s_y12 = [[sem(f"s_y12_{c}_{t}") for t in range(NT)] for c in range(2)]
        s_out = sem("s_out")
        s_chain = sem("s_chain")
        s_pool = sem("s_pool")

        block = ctx.enter_context(nc.Block())

        ring_free = {2: first["T0"] + KB, 3: first["KV0"] + 4, 4: first["KV0"] + KB, 5: first["T1"] + KB,
                     6: first["KV1"] + 4, 7: first["KV1"] + KB}
        for i in range(4):
            name = ["QL0", "QR0", "QL1", "QR1"][i]
            ring_free[8 + i] = first[name] + NT
        ring_free[12] = ring_free[13] = first["QTMIX"] + 4 * NT
        GNN_END = gnn_job[NT - 1] + 3

        def place_chunks(phase_no, m):
            i, total = phase_no * KB + m - MB, 2 * NH * KB - MB
            if i < 0:
                return range(0)
            return range(EC * i // total, EC * (i + 1) // total)

        @block.sync
        def _(sp):
            def load_unit(u):
                c, r = divmod(u, UNITS)
                if u >= 2:
                    sp.wait_ge(s_wlo, u - 1)
                sp.dma_start(w_raw[:, u % 2], CH[c][:, 2 * r:2 * r + 2, :]).then_inc(s_raw[u % 2], 16)

            for t in range(NT):
                sp.dma_start(acc[0:ROWS[t], t, :], x[t * P:t * P + ROWS[t], :]).then_inc(s_x[t], 16)
            sp.dma_start(src_i[0:EP, :], src.rearrange("(p c) -> p c", c=EC)).then_inc(s_edges, 16)
            sp.dma_start(dst_i[0:EP, :], dst.rearrange("(p c) -> p c", c=EC)).then_inc(s_edges, 16)
            u = 0
            while u < 2 * UNITS + 2:
                load_unit(u)
                u += 1
            for h in range(NH):
                for m in range(KB):
                    sp.wait_ge(s_free_dve, released(first[f"KV{h}"] + m)[1])
                    sp.dma_start(kv_d[m * P:(m + 1) * P, h * HALF:(h + 1) * HALF], kv_out[:, m % 4]).then_inc(s_kvs[m % 4], 16)
                    load_unit(u)
                    u += 1
                if h == 0:
                    for _ in range(UNITS):
                        load_unit(u)
                        u += 1
                    sp.wait_ge(s_full, first["T1"] + KB)
                    for t in range(NT):
                        sp.dma_start(acc[0:ROWS[t], t, :], x[t * P:t * P + ROWS[t], :]).then_inc(s_x[t], 16)
            while u < UNITS * C_KV:
                load_unit(u)
                u += 1
            for s in s_kvs:
                sp.wait_ge(s, 16 * 2 * NH)
            while u < UNITS * C_W + 2:
                load_unit(u)
                u += 1
            for t in range(NT):
                sp.wait_ge(s_free_dve, released(mix_job(t, 1))[1])
                sp.dma_start(mix_d[t * P:t * P + ROWS[t], :], acc[0:ROWS[t], t, :]).then_inc(s_mixs, 16)
            sp.wait_ge(s_full, first["H0"])
            sp.wait_ge(s_tab_done, 1)
            sp.dma_start(a_bc[:, :], gnn_a.partition_broadcast(P)).then_inc(s_a, 16)
            while u < UNITS * C_EXP:
                load_unit(u)
                u += 1
            sp.wait_ge(s_mixs, 16 * NT)
            sp.wait_ge(s_cnt, NT)
            for t in range(NT + 1):
                if t < NT:
                    if t >= 2:
                        sp.wait_ge(s_x2s[t % 2], 16 * (t // 2))
                    sp.dma_start(mix_in[0:ROWS[t], t % 2, :], mix_d[t * P:t * P + ROWS[t], :]).then_inc(s_mx[t % 2], 16)
                    sp.dma_start(x_in[0:ROWS[t], t % 2, :], x[t * P:t * P + ROWS[t], :]).then_inc(s_mx[t % 2], 16)
                if t == 0:
                    sp.wait_ge(s_full, first["H1"] + NT)
                    sp.dma_start(gw[:, :, :], gate_W.rearrange("(k p) e -> p k e", p=P)).then_inc(s_gw, 16)
                    sp.dma_start(gb[:, :], gate_b.rearrange("(o e) -> o e", o=1).partition_broadcast(P)).then_inc(s_gw, 16)
                if t >= 1:
                    i = t - 1
                    sp.wait_ge(s_xn2, NT + i + 1)
                    sp.dma_start(xn2_d[i * P:i * P + ROWS[i], :], xn2[0:ROWS[i], i % 2, :]).then_inc(s_xn2d[i % 2], 16)
                    sp.dma_start(x2_d[i * P:i * P + ROWS[i], :], x_in[0:ROWS[i], i % 2, :]).then_inc(s_x2s[i % 2], 16)
            def load_expert(e, running=None):
                for k in range(KB):
                    if running is not None and k == AT_ONCE:
                        sp.wait_ge(s_gx, first_block[running] * 16 + 32)
                    if e >= 1:
                        sp.wait_ge(s_elo, KB * (e - 1) + k + 1)
                    sp.dma_start(e_raw[k][:, :], expert_W[e, k * P:(k + 1) * P, :]).then_inc(s_er[k], 16)

            def load_x2(tiles):
                for t in tiles:
                    sp.dma_start(x2[t][0:ROWS[t], :], x2_d[t * P:t * P + ROWS[t], :]).then_inc(s_x2r, 16)

            def load_bias(e):
                sp.dma_start(bias[:, e % 2, :], expert_b[e:e + 1, :].partition_broadcast(P)).then_inc(s_bias[e % 2], 16)

            sp.wait_ge(s_x2, NT)
            sp.wait_ge(s_full, GNN_END)
            load_expert(0)
            load_bias(0)
            load_bias(1)
            load_expert(1)
            sp.sem_inc(s_ys, 16)
            sp.wait_ge(s_route, 1)
            first_block = [sp.value_load(bounds[0:1, e:e + 1], min_val=0, max_val=NBLK) for e in range(NE + 1)]
            for e in range(NE):
                if e + 2 < NE:
                    load_expert(e + 2, running=e)
                if 1 <= e < NE - 1:
                    load_bias(e + 1)
                if e == NE - 1:
                    sp.wait_ge(s_rest, (NBLK + 1) * 16)
                with sp.Fori(first_block[e], first_block[e + 1]) as i:
                    sp.wait_ge(s_ye, i * 2 + 4)
                    sp.dma_start(y_d[bass.ds(i * P, P), :], y[:, :]).then_inc(s_ys, 16)
                    if e < NE - 1:
                        sp.sem_inc(s_rest, 16)
                if e == 2:
                    for i in range(2):
                        sp.wait_ge(s_xn2d[i], 16 * (NT // 2))
                    with sp.Fori(first_block[NE - 1], NBLK + 1) as i:
                        sp.dma_start(y_d[bass.ds(i * P, P), :], xn2_d[0:P, :]).then_inc(s_rest, 16)
                if e == NE - 3:
                    sp.wait_ge(s_w12, 1)
                    for i in range(2):
                        sp.wait_ge(s_x2s[i], 16 * (NT // 2))
                    load_x2(range(EARLY))
                if e == NE - 2:
                    load_x2(range(EARLY, NT))
            for t in range(NT):
                sp.wait_ge(s_finw, t + 1)
                sp.dma_start(out[t * P:t * P + ROWS[t], :], x2[t][0:ROWS[t], :]).then_inc(s_out, 16)
            sp.wait_ge(s_out, 16 * NT)

        @block.gpsimd
        def _(pool):
            nc.gpsimd.memset(ident[:, :], 0.0).then_inc(s_pool, 1)
            nc.gpsimd.memset(ones[:, :], 1.0).then_inc(s_const, 1)
            pool.wait_ge(s_pool, 1)
            nc.gpsimd.affine_select(out=ident[:, :], in_=ident[:, :], compare_op=ALU.not_equal, fill=1.0,
                                    base=0, pattern=[[-1, P]], channel_multiplier=1).then_inc(s_const, 1)
            nc.gpsimd.iota(rank[:, :], [[-1, NE]], base=NE, channel_multiplier=0,
                           allow_small_or_imprecise_dtypes=True).then_inc(s_const, 1)
            nc.gpsimd.memset(tri[:, :], 0.0).then_inc(s_pool, 1)
            pool.wait_ge(s_pool, 2)
            nc.gpsimd.affine_select(out=tri[:, :], in_=tri[:, :], compare_op=ALU.is_ge, fill=1.0,
                                    base=0, pattern=[[-1, P]], channel_multiplier=1).then_inc(s_tri, 1)
            nc.gpsimd.iota(tiles10[:, :], [[1, NT]], base=0, channel_multiplier=0,
                           allow_small_or_imprecise_dtypes=True).then_inc(s_tri, 1)
            nc.gpsimd.iota(iota16[:, :], [[1, NC]], base=0, channel_multiplier=0,
                           allow_small_or_imprecise_dtypes=True).then_inc(s_tri, 1)
            pool.wait_ge(s_wlo, UNITS * C_EXP)
            nc.gpsimd.iota(nodes16[:, :], [[1, NT * P]], base=1, channel_multiplier=0,
                           allow_small_or_imprecise_dtypes=True)
            pool.wait_ge(s_diag, NT)
            nc.gpsimd.memset(zeros16[:, :], 0.0)
            nc.gpsimd.iota(iota128[:, :], [[1, P]], base=0, channel_multiplier=0,
                           allow_small_or_imprecise_dtypes=True).then_inc(s_nodes, 1)
            nc.gpsimd.memset(hexp[:, :], -0.5).then_inc(s_pool, 1)
            pool.wait_ge(s_pool, 3)
            def sum_tiles(t):
                pool.wait_ge(s_att, t + 1)
                if t >= 2:
                    pool.wait_ge(s_full, gnn_job[t - 2] + 1)
                if t >= 1:
                    pool.wait_ge(s_sum, t)
                z, o, half_t = att[:, t % 2], att_sum[:, t % 2, :], NT // 2
                nc.gpsimd.tensor_tensor(att_part[:, :, :], z[:, 0:half_t, :], z[:, half_t:NT, :], ALU.add).then_inc(s_part, 1)
                pool.wait_ge(s_part, 3 * t + 1)
                nc.gpsimd.tensor_tensor(att_part[:, 0:2, :], att_part[:, 0:2, :], att_part[:, 2:4, :], ALU.add).then_inc(s_part, 1)
                pool.wait_ge(s_part, 3 * t + 2)
                nc.gpsimd.tensor_tensor(att_part[:, 0, :], att_part[:, 0, :], att_part[:, 1, :], ALU.add).then_inc(s_part, 1)
                pool.wait_ge(s_part, 3 * t + 3)
                nc.gpsimd.tensor_tensor(o, att_part[:, 0, :], att_part[:, 4, :], ALU.add).then_inc(s_sum, 1)

            sum_tiles(0)
            for t in range(NT + 2):
                if t >= 2:
                    pool.wait_ge(s_var, NT + t - 1)
                    nc.gpsimd.tensor_tensor(nt2[:, :], mv[:, 1:2], hexp[:, :], ALU.pow).then_inc(s_sd, 1)
                if t + 1 < NT:
                    sum_tiles(t + 1)
                if 1 <= t <= NT:
                    i = t - 1
                    pool.wait_ge(s_mx[i % 2], 32 * (i // 2 + 1))
                    v = x_in[0:ROWS[i], i % 2, :]
                    nc.gpsimd.tensor_tensor(v, v, mix_in[0:ROWS[i], i % 2, :], ALU.add).then_inc(s_xm, 1)
            pool.wait_ge(s_x2, NT)
            for i in range(2):
                pool.wait_ge(s_x2s[i], 16 * (NT // 2))
            nc.gpsimd.memset(tri2[:, :], 0.0).then_inc(s_pool, 1)
            pool.wait_ge(s_pool, 4)
            nc.gpsimd.affine_select(out=tri2[:, :], in_=tri2[:, :], compare_op=ALU.is_ge, fill=1.0,
                                    base=0, pattern=[[-1, P]], channel_multiplier=1).then_inc(s_tri2, 1)
            nc.gpsimd.iota(tok[:, :], [[P, NT]], base=0, channel_multiplier=1,
                           allow_small_or_imprecise_dtypes=True).then_inc(s_tri2, 1)
            nc.gpsimd.iota(io16[:, :], [[1, P]], base=0, channel_multiplier=0,
                           allow_small_or_imprecise_dtypes=True).then_inc(s_tri2, 1)
            pool.wait_ge(s_gate_used, NT)
            for k in range(KB):
                pool.wait_ge(s_ehi, k + 1)
                nc.gpsimd.tensor_tensor(e_lo[0][:, k, :], e_raw[k][:, :], e_hi[0][:, k, :].bitcast(f32),
                                        ALU.subtract).then_inc(s_elo, 1)
            pool.wait_ge(s_route, 1)
            for i in range(2):
                pool.wait_ge(s_xn2d[i], 16 * (NT // 2))
            n_blocks = pool.value_load(bounds[0:1, NE:NE + 1], min_val=NE, max_val=NBLK)

            def gather(i):
                nc.gpsimd.tensor_copy(tok_now[:, :], tok_of[:, bass.ds(i, 1)]).then_inc(s_tok, 1)
                pool.wait_ge(s_tok, i + 1)
                pool.sem_inc(s_tok_in, 1)
                nc.gpsimd.indirect_dma_start(out=gx[:, :], out_offset=None, in_=xn2_d,
                                             in_offset=bass.IndirectOffsetOnAxis(ap=tok_now[:, :], axis=0)).then_inc(s_gx, 16)

            def gather_y(c, rows):
                for t in range(NT):
                    nc.gpsimd.indirect_dma_start(out=rows[t][0:ROWS[t], :], out_offset=None, in_=y_d,
                                                 in_offset=bass.IndirectOffsetOnAxis(ap=pos12[0:ROWS[t], c, t:t + 1], axis=0)
                                                 ).then_inc(s_y12[c][t], 16)

            gather(0)
            with pool.Fori(1, n_blocks + 1) as i:
                pool.wait_ge(s_tr, i * 2)
                gather(i)
            last_expert = pool.value_load(bounds[0:1, NE - 1:NE], min_val=NE - 1, max_val=NBLK - 1)
            pool.wait_ge(s_ys, last_expert * 16 + 16)
            pool.sem_inc(s_tok_in, 1)
            pool.wait_ge(s_mm, last_expert * 3)
            pool.sem_inc(s_tok_in, 1)
            pool.wait_ge(s_rest, (NBLK + 1) * 16)
            gather_y(0, y_lower)
            pool.wait_ge(s_ys, n_blocks * 16 + 16)
            pool.wait_ge(s_mm, n_blocks * 3)
            pool.sem_inc(s_tok_in, 1)
            gather_y(1, y_higher)

        @block.scalar
        def _(act):
            def split_hi(u):
                c, r = divmod(u, UNITS)
                act.wait_ge(s_raw[u % 2], 16 * (u // 2 + 1))
                if u == UNITS:
                    act.wait_ge(s_pos, 1)
                if c >= 2 and r == 0 and c in ring_free:
                    act.wait_ge(s_full, ring_free[c])
                nc.scalar.copy(w_hi[c % 2][:, 2 * r:2 * r + 2, :], w_raw[:, u % 2]).then_inc(s_whi, 1)

            def evac(n, dst_ap, rows=P, cols=HALF):
                act.wait_ge(s_full, n + 1)
                i = nc.scalar.copy(dst_ap, ps[0:rows, n % NB, 0:cols])
                if owner[n] == "act":
                    i.then_inc(s_free_act, 1)
                else:
                    i.then_inc(s_hi, 1)

            act.wait_ge(s_const, 3)
            for t in range(NT + 1):
                if t < NT:
                    act.wait_ge(s_var, t + 1)
                    nc.scalar.activation(sdx[0:ROWS[t], t % 2:t % 2 + 1], mvx[0:ROWS[t], t % 2, 1:2], ACT.Sqrt).then_inc(s_sd, 1)
                if t >= 1:
                    act.wait_ge(s_xn, t)
                    nc.scalar.copy(xn_hi[0:ROWS[t - 1], t - 1, :], acc[0:ROWS[t - 1], t - 1, :]).then_inc(s_xhi, 1)
            u = 0
            for i, (m, lo, w) in enumerate(G_PIECES):
                off = UPPER[m] + lo - m * P
                evac(first["G"] + i, gu_hi[:, off:off + w], cols=w)
                if i == NB - 1:
                    for _ in range(UNITS):
                        split_hi(u)
                        u += 1
            for i, keys in enumerate(LOW_BANKS):
                evac(first["LOW"] + 2 * i, gl_hi[:, LOWER[keys[0]]:LOWER[keys[0]] + len(keys) * P], cols=len(keys) * P)
            for h in range(NH):
                for m in range(KB):
                    if h == 1 and m == 0:
                        act.wait_ge(s_full, first["KV0"] + KB)
                    evac(first[f"T{h}"] + m, t_hi[:, m, :])
                    if KB - UNITS <= m:
                        split_hi(u)
                        u += 1
                for m in range(KB):
                    n = first[f"KV{h}"] + m
                    act.wait_ge(s_full, n + 1)
                    split_hi(u)
                    u += 1
            for m in range(4):
                act.wait_ge(s_kvs[m], 16 * 2 * NH)
            for t in range(NT):
                for g in range(2):
                    w = ROWS[t]
                    n = first["XT"] + 2 * t + g
                    act.wait_ge(s_full, n + 1)
                    nc.scalar.copy(xt_hi[:, MB * g:MB * g + MB, t * P:t * P + w],
                                   ps[:, n % NB, :].rearrange("p (b c) -> p b c", c=P)[:, :, 0:w]).then_inc(s_hi, 1)
            for h in range(NH):
                for t in range(NT):
                    evac(first[f"QL{h}"] + t, acc[0:ROWS[t], t, h * HALF:(h + 1) * HALF], rows=ROWS[t])
                    if t < UNITS:
                        split_hi(u)
                        u += 1
                for t in range(NT):
                    if t < UNITS:
                        act.wait_ge(s_full, first[f"QR{h}"] + t + 1)
                        split_hi(u)
                        u += 1
            for t in range(NT):
                for g in range(2):
                    n, q = qt_job(t, g), 2 * t + g
                    if q >= 3:
                        act.wait_ge(s_full, mix_job((q - 3) // 2, 1) + 1)
                    act.wait_ge(s_full, n + 1)
                    w = ROWS[t]
                    nc.scalar.copy(qt_hi[:, q % 3, :, 0:w],
                                   ps[:, n % NB, :].rearrange("p (b c) -> p b c", c=P)[:, :, 0:w]).then_inc(s_hi, 1)
                if t == 0:
                    for _ in range(UNITS):
                        split_hi(u)
                        u += 1
            for _ in range(UNITS):
                split_hi(u)
                u += 1
            for h in range(NH):
                for t in range(NT):
                    act.wait_ge(s_mixs, 16 * NT)
                    evac(first[f"H{h}"] + t, acc[0:ROWS[t], t, h * HALF:(h + 1) * HALF], rows=ROWS[t])
                    if h == 0 and t < UNITS:
                        split_hi(u)
                        u += 1
            for i, (c, w) in enumerate(SCOLS):
                w = min(HALF, NT * P - c)
                evac(first["AL"] + i, al_bc[:, c:c + w], cols=w)
            for t in range(NT):
                act.wait_ge(s_free_act, released(first["H1"] + t)[1])
                nc.scalar.copy(h_hi[0:ROWS[t], t, :], acc[0:ROWS[t], t, :]).then_inc(s_hhi, 1)
            for t in range(NT):
                if t == NT - 1:
                    act.wait_ge(s_z, 1)
                    nc.scalar.activation(att[:, 0], att[:, 0], ACT.Exp, scale=-1.0).then_inc(s_e, 1)
                act.wait_ge(s_counted, t + 1)
                nc.scalar.copy(cnt[:, t, :], ps[:, 3 * (t % 2):3 * (t % 2) + 3, :].rearrange("p b c -> p (b c)")[:, 0:NW]).then_inc(s_cnt, 1)
            for t in range(NT + 4):
                if t < NT:
                    act.wait_ge(s_att, t + 1)
                    if t >= 2:
                        act.wait_ge(s_full, gnn_job[t - 2] + 3)
                    nc.scalar.copy(att_hi[:, t % 2], att[:, t % 2]).then_inc(s_atthi, 1)
                if 2 <= t < NT + 2:
                    i = t - 2
                    w = ROWS[i]
                    act.wait_ge(s_rsum, i + 1)
                    if i >= 1:
                        act.wait_ge(s_x2, i)
                    for h in range(NH):
                        n = gnn_job[i] + 1 + h
                        act.wait_ge(s_full, n + 1)
                        c = slice(h * HALF, (h + 1) * HALF)
                        nc.scalar.activation(hneg[0:w, c], ps[0:w, n % NB, :], ACT.Exp, scale=rsum[0:w, i:i + 1])
                        nc.scalar.activation(hp[0:w, i % 2, c], ps[0:w, n % NB, :], ACT.Copy, bias=1.0,
                                             scale=rsum[0:w, i:i + 1]).then_inc(s_free_act, 1)
                if t + 1 < NT:
                    act.wait_ge(s_z, t + 2)
                    v = att[:, (t + 1) % 2]
                    nc.scalar.activation(v, v, ACT.Exp, scale=-1.0).then_inc(s_e, 1)
                if t >= 4:
                    i = t - 4
                    w = ROWS[i]
                    if i >= 2:
                        act.wait_ge(s_gate_used, i - 1)
                    for g in range(2):
                        n = tr_job[i] + g
                        act.wait_ge(s_full, n + 1)
                        nc.scalar.copy(xg[:, i % 2, MB * g:MB * g + MB, 0:w],
                                       ps[:, n % NB, :].rearrange("p (b c) -> p b c", c=P)[:, :, 0:w]).then_inc(s_free_act, 1)
            def expert_hi(e):
                for k in range(KB):
                    act.wait_ge(s_er[k], 16 * (e + 1))
                    nc.scalar.copy(e_hi[e % 2][:, k, :], e_raw[k][:, :]).then_inc(s_ehi, 1)

            def block_hi(i, g):
                act.wait_ge(s_tr, i * 2 + (g + 1))
                nc.scalar.copy(lt_hi[:, MB * g:MB * g + MB, :],
                               ps[:, 4 + g, :].rearrange("p (b c) -> p b c", c=P)).then_inc(s_lhi, 1)

            act.wait_ge(s_gate_used, NT)
            expert_hi(0)
            act.wait_ge(s_gate, 1)
            nc.scalar.activation(g_p[:, :, :], g_p[:, :, :], ACT.Exp).then_inc(s_gexp, 1)
            act.wait_ge(s_route, 1)
            first_block = [act.value_load(bounds[0:1, e:e + 1], min_val=0, max_val=NBLK) for e in range(NE + 1)]
            for g in range(2):
                block_hi(0, g)
            for e in range(NE):
                if e + 1 < NE:
                    if e >= 1:
                        act.wait_ge(s_mm, first_block[e] * 3)
                    expert_hi(e + 1)
                with act.Fori(first_block[e], first_block[e + 1]) as i:
                    act.wait_ge(s_mm, i * 3 + 1)
                    block_hi(i + 1, 0)
                    act.wait_ge(s_mm, i * 3 + 3)
                    block_hi(i + 1, 1)

        @block.vector
        def _(dve):
            chained = [0]

            def link(i):
                chained[0] += 1
                i.then_inc(s_chain, 1)
                dve.wait_ge(s_chain, chained[0])

            def split_lo(u):
                c, r = divmod(u, UNITS)
                dve.wait_ge(s_whi, u + 1)
                nc.vector.tensor_tensor(w_lo[c % 2][:, 2 * r:2 * r + 2, :], w_raw[:, u % 2],
                                        w_hi[c % 2][:, 2 * r:2 * r + 2, :].bitcast(f32), ALU.subtract).then_inc(s_wlo, 1)

            hi_count = [0]

            def evac_lo(n, dst_ap, src_ap, hi_ap):
                hi_count[0] += 1
                dve.wait_ge(s_hi, hi_count[0])
                nc.vector.tensor_tensor(dst_ap, src_ap, hi_ap.bitcast(f32), ALU.subtract).then_inc(s_free_dve, 1)

            def norm_stats(t):
                w, v = ROWS[t], mvx[0:ROWS[t], t % 2, :]
                dve.wait_ge(s_x[t], 16)
                for g in range(2):
                    i = nc.vector.bn_stats(stats[0:w, g, :], acc[0:w, t, g * HALF:(g + 1) * HALF])
                link(i)
                link(nc.vector.bn_aggr(v, stats[0:w, :, :].rearrange("p a b -> p (a b)")))
                nc.vector.tensor_copy(mean[0:w, t:t + 1], v[:, 0:1])
                nc.vector.tensor_scalar(v[:, 1:2], v[:, 1:2], LN_EPS, None, ALU.add).then_inc(s_var, 1)
                dve.wait_ge(s_var, t + 1)

            def normalise(t):
                w = ROWS[t]
                dve.wait_ge(s_sd, t + 1)
                link(nc.vector.reciprocal(nt2[0:w, :], sdx[0:w, t % 2:t % 2 + 1]))
                link(nc.vector.scalar_tensor_tensor(nt1[0:w, :], nt2[0:w, :], nt2[0:w, :], mvx[0:w, t % 2, 1:2], ALU.mult, ALU.mult))
                link(nc.vector.tensor_scalar(nt1[0:w, :], nt1[0:w, :], -0.5, 1.5, ALU.mult, ALU.add))
                link(nc.vector.tensor_tensor(rstd[0:w, t:t + 1], nt1[0:w, :], nt2[0:w, :], ALU.mult))
                nc.vector.tensor_scalar(acc[0:w, t, :], acc[0:w, t, :], mean[0:w, t:t + 1], rstd[0:w, t:t + 1],
                                        ALU.subtract, ALU.mult).then_inc(s_xn, 1)

            norm_stats(0)
            for t in range(NT + 1):
                if t + 1 < NT:
                    norm_stats(t + 1)
                if t < NT:
                    normalise(t)
                if t >= 1:
                    w = ROWS[t - 1]
                    dve.wait_ge(s_xhi, t)
                    nc.vector.tensor_tensor(xn_lo[0:w, t - 1, :], acc[0:w, t - 1, :], xn_hi[0:w, t - 1, :].bitcast(f32),
                                            ALU.subtract).then_inc(s_xlo, 1)
            u = 0
            V = nc.vector

            def gram_lo(i):
                m, lo, w = G_PIECES[i]
                off, n = UPPER[m] + lo - m * P, first["G"] + i
                evac_lo(n, gu_lo[:, off:off + w], ps[:, n % NB, 0:w], gu_hi[:, off:off + w])

            for i in range(NB):
                gram_lo(i)
            for _ in range(UNITS):
                split_lo(u)
                u += 1

            dve.wait_ge(s_edges, 32)
            dve.wait_ge(s_tri, 3)
            e_ = slice(0, EP)
            V.tensor_scalar(tile_i[e_, :], dst_i[e_, :], 7, None, ALU.logical_shift_right)
            V.tensor_scalar(src1[e_, :], src_i[e_, :], 1.0, None, ALU.add)
            link(V.tensor_scalar(pos_i[e_, :], dst_i[e_, :], P - 1, None, ALU.bitwise_and))
            V.tensor_copy(dlo[e_, :], pos_i[e_, :])
            link(V.tensor_copy(tile_f[e_, :], tile_i[e_, :]))
            link(V.tensor_tensor(in_tile[e_, :, :], tile_f[e_, :].unsqueeze(1).to_broadcast([EP, NT, EC]),
                                 tiles10[e_, :].unsqueeze(2).to_broadcast([EP, NT, EC]), ALU.is_equal))
            flat = in_tile[e_, :, :].rearrange("p a b -> p (a b)")
            link(V.tensor_tensor_scan(run[e_, :, :].rearrange("p a b -> p (a b)"), flat, flat, 0.0, ALU.add, ALU.max))
            link(V.memset(ends[:, :], 0.0))
            link(V.tensor_copy(ends[e_, 1:NT + 1], run[e_, :, EC - 1]))
            V.tensor_tensor(tot[e_, :], ends[e_, 1:NT + 1], ends[e_, 0:NT], ALU.subtract).then_inc(s_tot, 1)
            for i in range(NB, len(G_PIECES)):
                gram_lo(i)
            for i, keys in enumerate(LOW_BANKS):
                n, w = first["LOW"] + 2 * i + 1, len(keys) * P
                dve.wait_ge(s_full, n + 1)
                nc.vector.tensor_copy(gl_lo[:, LOWER[keys[0]]:LOWER[keys[0]] + w], ps[:, n % NB, 0:w]).then_inc(s_free_dve, 1)
            dve.wait_ge(s_totp, 1)
            link(V.tensor_scalar(gb_i[:, :], ps[:, 7, NT:2 * NT], float(GE - 1), None, ALU.add))
            link(V.tensor_scalar(gb_i[:, :], gb_i[:, :], GE.bit_length() - 1, None, ALU.logical_shift_right))
            link(V.tensor_copy(gb_f[:, :], gb_i[:, :]))
            link(V.tensor_scalar(gb_f[:, :], gb_f[:, :], 1.0, None, ALU.max))
            link(V.tensor_tensor_scan(gb_cum[:, :], gb_f[:, :], gb_f[:, :], 0.0, ALU.add, ALU.max))
            V.memset(g_first[:, 0:1], 0)
            V.tensor_copy(g_first[:, 1:NT + 1], gb_cum[:, :])
            link(V.tensor_tensor(place0[:, :], gb_cum[:, :], gb_f[:, :], ALU.subtract))
            link(V.scalar_tensor_tensor(place0[:, :], place0[:, :], float(GE), ps[:, 7, 0:NT], ALU.mult, ALU.add))
            link(V.scalar_tensor_tensor(place0[:, :], place0[:, :], -1.0, ends[:, 0:NT], ALU.add, ALU.subtract))
            link(V.tensor_tensor(place[e_, :, :], run[e_, :, :], place0[e_, :].unsqueeze(2).to_broadcast([EP, NT, EC]), ALU.add))
            link(V.tensor_tensor(place[e_, :, :], place[e_, :, :], in_tile[e_, :, :], ALU.mult))
            link(V.tensor_reduce(pos_f[e_, :], place[e_, :, :].rearrange("p a b -> p b a"), AX.X, ALU.add))
            link(V.tensor_copy(pos_i[e_, :], pos_f[e_, :]))
            link(V.tensor_scalar(tile_i[e_, :], pos_i[e_, :], P - 1, None, ALU.bitwise_and))
            link(V.tensor_copy(pos_lo[e_, :], tile_i[e_, :]))
            link(V.tensor_scalar(tile_i[e_, :], pos_i[e_, :], P.bit_length() - 1, None, ALU.logical_shift_right))
            link(V.tensor_copy(pos_hi[e_, :], tile_i[e_, :]))
            V.tensor_copy(ends[:, 0:1], gb_f[:, 0:1]).then_inc(s_pos, 1)

            def place_hot(j):
                if j >= HS:
                    dve.wait_ge(s_ph_used, j - HS + 1)
                s = j % HS
                V.tensor_scalar(hot_r[e_, s, :], iota16[e_, 0:P], pos_lo[e_, j:j + 1], None, ALU.is_equal)
                for i, v in enumerate((src1, dlo)):
                    last = V.tensor_scalar(hot_c[e_, s, i, :], iota16[e_, :], pos_hi[e_, j:j + 1], v[e_, j:j + 1],
                                           ALU.is_equal, ALU.mult)
                last.then_inc(s_ph, 1)

            for h in range(NH):
                for m in range(KB):
                    n = first[f"T{h}"] + m
                    for j in place_chunks(2 * h, m):
                        place_hot(j)
                    evac_lo(n, t_lo[:, m, :], ps[:, n % NB, :], t_hi[:, m, :])
                    if KB - UNITS <= m:
                        split_lo(u)
                        u += 1
                for m in range(KB):
                    n = first[f"KV{h}"] + m
                    for j in place_chunks(2 * h + 1, m):
                        place_hot(j)
                    dve.wait_ge(s_full, n + 1)
                    k = 2 * h + m // 4
                    if k >= 1:
                        dve.wait_ge(s_kvs[m % 4], 16 * k)
                    nc.vector.tensor_copy(kv_out[:, m % 4], ps[:, n % NB, :]).then_inc(s_free_dve, 1)
                    split_lo(u)
                    u += 1
                    if h == 1:
                        for t in ([m] if m < KB - 1 else range(m, NT)):
                            w = ROWS[t]
                            dve.wait_ge(s_x[t], 32)
                            nc.vector.tensor_scalar(acc[0:w, t, :], acc[0:w, t, :], mean[0:w, t:t + 1], rstd[0:w, t:t + 1],
                                                    ALU.subtract, ALU.mult).then_inc(s_xn2, 1)
            dve.wait_ge(s_ph_used, EC)
            V.tensor_copy(s_tab[:, :], ps[:, 7, 0:NC])
            V.tensor_copy(d_tab[:, :], ps[:, 7, NC:2 * NC]).then_inc(s_tab_done, 1)
            for m in range(4):
                dve.wait_ge(s_kvs[m], 16 * 2 * NH)
            for t in range(NT):
                for g in range(2):
                    w = ROWS[t]
                    n = first["XT"] + 2 * t + g
                    evac_lo(n, xt_lo[:, MB * g:MB * g + MB, t * P:t * P + w],
                            ps[:, n % NB, :].rearrange("p (b c) -> p b c", c=P)[:, :, 0:w],
                            xt_hi[:, MB * g:MB * g + MB, t * P:t * P + w])
            for h in range(NH):
                for t in range(NT):
                    if t < UNITS:
                        split_lo(u)
                        u += 1
                for t in range(NT):
                    n, w = first[f"QR{h}"] + t, ROWS[t]
                    dve.wait_ge(s_free_act, released(first[f"QL{h}"] + t)[1])
                    dve.wait_ge(s_full, n + 1)
                    a = acc[0:w, t, h * HALF:(h + 1) * HALF]
                    nc.vector.tensor_tensor(a, ps[0:w, n % NB, :], a, ALU.mult).then_inc(s_free_dve, 1)
                    if t < UNITS:
                        split_lo(u)
                        u += 1

            def mix_out(t):
                w = ROWS[t]
                for h in range(NH):
                    n = mix_job(t, h)
                    dve.wait_ge(s_full, n + 1)
                    nc.vector.tensor_copy(acc[0:w, t, h * HALF:(h + 1) * HALF], ps[0:w, n % NB, :]).then_inc(s_free_dve, 1)

            for t in range(NT):
                if t >= 2:
                    mix_out(t - 2)
                for g in range(2):
                    n, q, w = qt_job(t, g), 2 * t + g, ROWS[t]
                    evac_lo(n, qt_lo[:, q % 3, :, 0:w],
                            ps[:, n % NB, :].rearrange("p (b c) -> p b c", c=P)[:, :, 0:w], qt_hi[:, q % 3, :, 0:w])
                if t == 0:
                    for _ in range(UNITS):
                        split_lo(u)
                        u += 1
            mix_out(NT - 2)
            mix_out(NT - 1)
            for _ in range(UNITS):
                split_lo(u)
                u += 1
            for _ in range(UNITS):
                split_lo(u)
                u += 1
            i = nc.vector.memset(al[:, :], 0.0)
            link(nc.vector.memset(ar[:, :], 0.0))
            dve.wait_ge(s_a, 16)
            for t in range(NT):
                w = ROWS[t]
                dve.wait_ge(s_free_act, released(first["H1"] + t)[1])
                for v, a in ((al, a_bc[0:w, 0:D]), (ar, a_bc[0:w, D:2 * D])):
                    link(nc.vector.tensor_tensor_reduce(out=a_junk[0:w, :], in0=acc[0:w, t, :], in1=a, scale=1.0, scalar=0.0,
                                                        op0=ALU.mult, op1=ALU.add, accum_out=v[0:w, t:t + 1]))
                nc.vector.tensor_scalar(diag[:, t, :], ident[:, :], al[:, t:t + 1], None, ALU.mult).then_inc(s_diag, 1)

            def scores(t):
                z = att[:, t % 2]
                if t == 0:
                    dve.wait_ge(s_free_act, released(first["AL"] + len(SCOLS) - 1)[1])
                if t >= 2:
                    dve.wait_ge(s_atthi, t - 1)
                    dve.wait_ge(s_attlo, t - 1)
                    dve.wait_ge(s_sum, t - 1)
                link(nc.vector.tensor_tensor(z, al_bc[:, t * P:(t + 1) * P].unsqueeze(1).to_broadcast([P, NT, P]),
                                             ar[:, :].unsqueeze(2).to_broadcast([P, NT, P]), ALU.add))
                nc.vector.scalar_tensor_tensor(z, z, NEG_SLOPE, z, ALU.mult, ALU.max).then_inc(s_z, 1)

            dve.wait_ge(s_nodes, 1)
            for t in range(NT):
                first_group, end = (dve.value_load(g_first[0:1, t + i:t + i + 1], min_val=i, max_val=NG) for i in range(2))
                with dve.Fori(first_group, end) as g:
                    for j in range(CK):
                        dve.wait_ge(s_hot_used, g * CK + (j + 1))
                        V.tensor_scalar(hot_s[:, j, :], nodes16[:, 0:NW], s_tab[:, bass.ds(g * CK + j, 1)], None, ALU.is_equal)
                        V.tensor_scalar(hot_d[:, j, :], iota128[:, :], d_tab[:, bass.ds(g * CK + j, 1)], None,
                                        ALU.is_equal).then_inc(s_hot, 1)
                w = ROWS[t]
                dve.wait_ge(s_hhi, t + 1)
                nc.vector.tensor_tensor(h_lo[0:w, t, :], acc[0:w, t, :], h_hi[0:w, t, :].bitcast(f32),
                                        ALU.subtract).then_inc(s_hlo, 1)
                if t == NT - 2:
                    scores(0)
            dve.wait_ge(s_cnt, NT)
            def weights(t):
                w, z = ROWS[t], att[:, t % 2]
                dve.wait_ge(s_e, t + 1)
                nc.vector.scalar_tensor_tensor(z[:, :, 0:w], z[:, :, 0:w], F32_MAX, cnt[:, :, t * P:t * P + w],
                                               ALU.min, ALU.mult).then_inc(s_att, 1)

            weights(0)
            for t in range(NT + 2):
                if t < NT:
                    dve.wait_ge(s_atthi, t + 1)
                    nc.vector.tensor_tensor(att_lo[:, t % 2], att[:, t % 2], att_hi[:, t % 2].bitcast(f32),
                                            ALU.subtract).then_inc(s_attlo, 1)
                if 2 <= t < NT + 2:
                    i = t - 2
                    w = ROWS[i]
                    n = gnn_job[i]
                    dve.wait_ge(s_full, n + 1)
                    rs = rsum[0:w, i:i + 1]
                    nc.vector.tensor_scalar(rs, ps[0:w, n % NB, 0:1], GNN_EPS, None, ALU.add).then_inc(s_free_dve, 1)
                    dve.wait_ge(s_free_dve, released(n)[1])
                    nc.vector.reciprocal(rs, rs).then_inc(s_rsum, 1)
                if t + 1 < NT:
                    scores(t + 1)
                if 2 <= t < NT + 2:
                    hv = hp[0:w, i % 2, :]
                    dve.wait_ge(s_free_act, released(n + 2)[1])
                    link(nc.vector.scalar_tensor_tensor(hv, hneg[0:w, :], 1.0, hv, ALU.min, ALU.max))
                    dve.wait_ge(s_xm, i + 1)
                    x2v = x_in[0:w, i % 2, :]
                    nc.vector.scalar_tensor_tensor(x2v, hv, -1.0, x2v, ALU.add, ALU.add).then_inc(s_x2, 1)
                if t + 1 < NT:
                    weights(t + 1)
                if 2 <= t < NT + 2:
                    dve.wait_ge(s_x2, i + 1)
                    for g in range(2):
                        last = nc.vector.bn_stats(stats[0:w, g, :], x2v[:, g * HALF:(g + 1) * HALF])
                    link(last)
                    link(nc.vector.bn_aggr(mv[0:w, :], stats[0:w, :, :].rearrange("p a b -> p (a b)")))
                    nc.vector.tensor_scalar(mv[0:w, 1:2], mv[0:w, 1:2], LN_EPS, None, ALU.add).then_inc(s_var, 1)
                    dve.wait_ge(s_sd, NT + i + 1)
                    link(nc.vector.tensor_tensor(nt1[0:w, :], nt2[0:w, :], nt2[0:w, :], ALU.mult))
                    link(nc.vector.tensor_tensor(nt1[0:w, :], nt1[0:w, :], mv[0:w, 1:2], ALU.mult))
                    link(nc.vector.tensor_scalar(nt1[0:w, :], nt1[0:w, :], -0.5, 1.5, ALU.mult, ALU.add))
                    link(nc.vector.tensor_tensor(nt1[0:w, :], nt1[0:w, :], nt2[0:w, :], ALU.mult))
                    if i >= 2:
                        dve.wait_ge(s_full, tr_job[i - 2] + 2)
                        dve.wait_ge(s_xn2d[i % 2], 16 * (i // 2))
                    nc.vector.tensor_scalar(xn2[0:w, i % 2, :], x2v, mv[0:w, 0:1], nt1[0:w, :],
                                            ALU.subtract, ALU.mult).then_inc(s_xn2, 1)

            dve.wait_ge(s_tri2, 3)
            link(V.memset(sc[:, :, :], 0.0))
            dve.wait_ge(s_gate_used, NT)
            gps = ps[:, 7, 0:NT * NE].rearrange("p (t e) -> p t e", e=NE)

            def over_experts(v):
                return v.unsqueeze(2).to_broadcast([P, NT, NE])

            def over_tiles(v):
                return v.unsqueeze(1).to_broadcast([P, NT, NE])

            if ROWS[-1] == P:
                link(V.tensor_copy(sc[:, :, :], gps))
            else:
                V.tensor_copy(sc[:, 0:NT - 1, :], gps[:, 0:NT - 1, :])
                link(V.tensor_copy(sc[0:ROWS[-1], NT - 1, :], gps[0:ROWS[-1], NT - 1, :]))
            S = sc[:, :, :]
            link(V.tensor_tensor(S, S, over_tiles(gb[:, :]), ALU.add))
            link(V.tensor_scalar(S, S, GATE_EPS, None, ALU.max))
            link(V.tensor_reduce(g_m[:, :], S, AX.X, ALU.max))
            V.tensor_tensor(g_p[:, :, :], S, over_experts(g_m[:, :]), ALU.subtract).then_inc(s_gate, 1)

            def choose(pick, scores):
                link(V.tensor_tensor(g_key[:, :, :], scores, over_experts(g_m[:, :]), ALU.is_ge))
                link(V.tensor_tensor(g_key[:, :, :], g_key[:, :, :], over_tiles(rank[:, :]), ALU.mult))
                link(V.tensor_reduce(g_t[:, :], g_key[:, :, :], AX.X, ALU.max))
                link(V.tensor_tensor(pick, g_key[:, :, :], over_experts(g_t[:, :]), ALU.is_equal))

            choose(g_one[:, :, :], S)
            link(V.scalar_tensor_tensor(g_s2[:, :, :], g_one[:, :, :], -1e30, S, ALU.mult, ALU.add))
            link(V.tensor_reduce(g_m[:, :], g_s2[:, :, :], AX.X, ALU.max))
            choose(g_two[:, :, :], g_s2[:, :, :])
            V.tensor_scalar(valid[:, :], tok[:, :], float(N), None, ALU.is_lt)
            link(V.tensor_tensor(g_mask[:, :, :], g_one[:, :, :], g_two[:, :, :], ALU.add))
            V.tensor_tensor(tokv[:, :], tok[:, :], valid[:, :], ALU.mult)
            link(V.tensor_tensor(g_in[:, :, :], g_mask[:, :, :].rearrange("p t e -> p e t"),
                                 valid[:, :].unsqueeze(1).to_broadcast([P, NE, NT]), ALU.mult))
            flat2 = g_in[:, :, :].rearrange("p a b -> p (a b)")
            link(V.tensor_tensor_scan(g_run[:, :, :].rearrange("p a b -> p (a b)"), flat2, flat2, 0.0, ALU.add, ALU.max))
            link(V.memset(g_ends[:, :], 0.0))
            link(V.tensor_copy(g_ends[:, 1:NE + 1], g_run[:, :, NT - 1]))
            V.tensor_tensor(g_tot[:, :], g_ends[:, 1:NE + 1], g_ends[:, 0:NE], ALU.subtract).then_inc(s_gtot, 1)
            dve.wait_ge(s_gtotp, 1)
            link(V.tensor_scalar(g_nbi[:, :], ps[:, 7, NE:2 * NE], float(P - 1), None, ALU.add))
            link(V.tensor_scalar(g_nbi[:, :], g_nbi[:, :], P.bit_length() - 1, None, ALU.logical_shift_right))
            link(V.tensor_copy(g_nb[:, :], g_nbi[:, :]))
            link(V.tensor_scalar(g_nb[:, :], g_nb[:, :], 1.0, None, ALU.max))
            link(V.tensor_tensor_scan(g_cum[:, :], g_nb[:, :], g_nb[:, :], 0.0, ALU.add, ALU.max))
            V.memset(bounds[:, 0:1], 0)
            V.tensor_copy(bounds[:, 1:NE + 1], g_cum[:, :])
            link(V.tensor_tensor(g_place[:, :], g_cum[:, :], g_nb[:, :], ALU.subtract))
            link(V.scalar_tensor_tensor(g_place[:, :], g_place[:, :], float(P), ps[:, 7, 0:NE], ALU.mult, ALU.add))
            link(V.scalar_tensor_tensor(g_place[:, :], g_place[:, :], -1.0, g_ends[:, 0:NE], ALU.add, ALU.subtract))
            link(V.tensor_tensor(g_pos[:, :, :], g_run[:, :, :].rearrange("p e t -> p t e"), over_tiles(g_place[:, :]), ALU.add))
            link(V.tensor_tensor(g_key[:, :, :], g_mask[:, :, :], over_tiles(rank[:, :]), ALU.mult))
            link(V.tensor_reduce(g_t[:, :], g_key[:, :, :], AX.X, ALU.max))
            link(V.tensor_tensor(g_one[:, :, :], g_key[:, :, :], over_experts(g_t[:, :]), ALU.is_equal))
            link(V.tensor_tensor(g_two[:, :, :], g_mask[:, :, :], g_one[:, :, :], ALU.subtract))
            for c, pick in enumerate((g_one, g_two)):
                link(V.tensor_tensor(g_key[:, :, :], g_pos[:, :, :], pick[:, :, :], ALU.mult))
                link(V.tensor_reduce(p_f[:, c, :], g_key[:, :, :], AX.X, ALU.add))
            link(V.tensor_copy(pos12[:, :, :], p_f[:, :, :]))
            link(V.tensor_scalar(p_a[:, :, :], pos12[:, :, :], P - 1, None, ALU.bitwise_and))
            link(V.tensor_copy(p_lo[:, :, :], p_a[:, :, :]))
            link(V.tensor_scalar(p_a[:, :, :], pos12[:, :, :], P.bit_length() - 1, None, ALU.logical_shift_right))
            link(V.tensor_copy(p_hi[:, :, :], p_a[:, :, :]))
            for c in range(2):
                C2 = slice(c * NT, (c + 1) * NT)
                V.tensor_tensor(tok_r[:, C2, :], io16[:, :].unsqueeze(1).to_broadcast([P, NT, P]),
                                p_lo[:, c, :].unsqueeze(2).to_broadcast([P, NT, P]), ALU.is_equal)
                link(V.tensor_tensor(tok_c[:, C2, :], io16[:, 0:NSLOT].unsqueeze(1).to_broadcast([P, NT, NSLOT]),
                                     p_hi[:, c, :].unsqueeze(2).to_broadcast([P, NT, NSLOT]), ALU.is_equal))
                V.tensor_tensor(tok_c[:, C2, :], tok_c[:, C2, :], tokv[:, :].unsqueeze(2).to_broadcast([P, NT, NSLOT]),
                                ALU.mult).then_inc(s_toks, 1)
            dve.wait_ge(s_tokp, 1)
            V.tensor_copy(tok_of[:, :], ps[:, 7, 0:NSLOT]).then_inc(s_route, 1)
            dve.sem_inc(s_ye, 2)

            def expert_lo(e):
                for k in range(KB):
                    dve.wait_ge(s_ehi, KB * e + k + 1)
                    V.tensor_tensor(e_lo[e % 2][:, k, :], e_raw[k][:, :], e_hi[e % 2][:, k, :].bitcast(f32),
                                    ALU.subtract).then_inc(s_elo, 1)

            def block_lo(i, g):
                dve.wait_ge(s_lhi, i * 2 + (g + 1))
                V.tensor_tensor(lt_lo[:, MB * g:MB * g + MB, :], ps[:, 4 + g, :].rearrange("p (b c) -> p b c", c=P),
                                lt_hi[:, MB * g:MB * g + MB, :].bitcast(f32), ALU.subtract).then_inc(s_llo, 1)

            for g in range(2):
                block_lo(0, g)
            dve.wait_ge(s_gexp, 1)
            link(V.tensor_reduce(g_t[:, :], g_p[:, :, :], AX.X, ALU.add))
            link(V.reciprocal(g_t[:, :], g_t[:, :]))
            link(V.tensor_tensor(g_p[:, :, :], g_p[:, :, :], over_experts(g_t[:, :]), ALU.mult))
            link(V.tensor_scalar(g_p[:, :, :], g_p[:, :, :], W_THRES, None, ALU.max))
            for c, pick in enumerate((g_one, g_two)):
                link(V.tensor_tensor(g_key[:, :, :], g_p[:, :, :], pick[:, :, :], ALU.mult))
                link(V.tensor_reduce(w12[:, c, :], g_key[:, :, :], AX.X, ALU.add))
            link(V.tensor_tensor(g_t[:, :], w12[:, 0, :], w12[:, 1, :], ALU.add))
            link(V.reciprocal(g_t[:, :], g_t[:, :]))
            link(V.tensor_scalar(g_t[:, :], g_t[:, :], 1.0 / TOPK, None, ALU.mult))
            V.tensor_tensor(w12[:, :, :], w12[:, :, :], g_t[:, :].unsqueeze(1).to_broadcast([P, 2, NT]), ALU.mult).then_inc(s_w12, 1)

            first_block = [dve.value_load(bounds[0:1, e:e + 1], min_val=0, max_val=NBLK) for e in range(NE + 1)]
            for e in range(NE):
                if e + 1 < NE:
                    expert_lo(e + 1)
                dve.wait_ge(s_bias[e % 2], 16 * (e // 2 + 1))
                with dve.Fori(first_block[e], first_block[e + 1]) as i:
                    block_lo(i + 1, 0)
                    dve.wait_ge(s_ys, i * 16 + 16)
                    for h in range(NH):
                        c = slice(h * HALF, (h + 1) * HALF)
                        dve.wait_ge(s_mm, i * 3 + (2 + h))
                        V.tensor_tensor(y[:, c], ps[:, h, :], bias[:, e % 2, c], ALU.add).then_inc(s_ye, 1)
                    block_lo(i + 1, 1)
            dve.wait_ge(s_x2r, 16 * NT)
            for t in range(NT):
                v = x2[t][0:ROWS[t], :]
                dve.wait_ge(s_y12[0][t], 16)
                V.scalar_tensor_tensor(v, y_lower[t][0:ROWS[t], :], w12[0:ROWS[t], 0, t:t + 1], v, ALU.mult, ALU.add).then_inc(s_fin, 1)
            for t in range(NT):
                v = x2[t][0:ROWS[t], :]
                dve.wait_ge(s_fin, t + 1)
                dve.wait_ge(s_y12[1][t], 16)
                V.scalar_tensor_tensor(v, y_higher[t][0:ROWS[t], :], w12[0:ROWS[t], 1, t:t + 1], v, ALU.mult, ALU.add).then_inc(s_finw, 1)

        @block.tensor
        def _(pe):
            def bank_free(n):
                if n >= NB:
                    pe.wait_ge(*released(n - NB))

            def chunk_ready(c):
                pe.wait_ge(s_wlo, UNITS * (c + 1))

            def three(o, lh, ll, rh, rl, k, last_k):
                nc.tensor.matmul(o, lh, rh, start=(k == 0), stop=False)
                nc.tensor.matmul(o, lh, rl, start=False, stop=False)
                return nc.tensor.matmul(o, ll, rh, start=False, stop=(k == last_k))

            def gram_piece(i, t):
                m, lo, w = G_PIECES[i]
                r = ROWS[t]
                a, b = (v[0:r, t, m * P:(m + 1) * P] for v in (xn_hi, xn_lo))
                c, d = (v[0:r, t, lo:lo + w] for v in (xn_hi, xn_lo))
                last = three(ps[:, i % NB, 0:w], a, b, c, d, t, NT - 1)
                if t == NT - 1:
                    last.then_inc(s_full, 1)

            for t in range(NT):
                pe.wait_ge(s_xlo, t + 1)
                for i in range(NB):
                    gram_piece(i, t)
            for i in range(NB, len(G_PIECES)):
                bank_free(i)
                for t in range(NT):
                    gram_piece(i, t)
            pe.wait_ge(s_tot, 1)
            nc.tensor.matmul(ps[:, 7, 0:NT], tri[0:EP, :], tot[0:EP, :], start=True, stop=True)
            nc.tensor.matmul(ps[:, 7, NT:2 * NT], ones[0:EP, :], tot[0:EP, :], start=True, stop=True).then_inc(s_totp, 1)
            pe.wait_ge(s_const, 3)
            for i, keys in enumerate(LOW_BANKS):
                for part, (g, n) in enumerate(((gu_hi, first["LOW"] + 2 * i), (gu_lo, first["LOW"] + 2 * i + 1))):
                    bank_free(n)
                    if i == 0:
                        pe.wait_ge(s_free_dve, released(first["G"] + len(G_PIECES) - 1)[1])
                    for j, (row, col) in enumerate(keys):
                        off = UPPER[col] + (row - col) * P
                        last = nc.tensor.transpose(ps[:, n % NB, j * P:(j + 1) * P], g[:, off:off + P].bitcast(f32), ident[:, :])
                    last.then_inc(s_full, 1)

            def place_edges(j):
                pe.wait_ge(s_ph, j + 1)
                if j == 0:
                    pe.wait_ge(s_pos, 1)
                s = j % HS
                nc.tensor.matmul(ps[:, 7, 0:2 * NC], hot_r[0:EP, s, :], hot_c[0:EP, s, :, :].rearrange("p a b -> p (a b)"),
                                 start=(j == 0), stop=(j == EC - 1)).then_inc(s_ph_used, 1)

            def gram(k, m, part):
                if k <= m:
                    off = UPPER[k] + (m - k) * P
                    return (gu_hi, gu_lo)[part][:, off:off + P]
                off = LOWER[(k, m)]
                return (gl_hi, gl_lo)[part][:, off:off + P]

            for h in range(NH):
                c = 3 * h
                chunk_ready(c)
                if h == 0:
                    pe.wait_ge(*released(first["T0"] - 1))
                    pe.wait_ge(*released(first["T0"] - 2))
                for m in range(KB):
                    n = first[f"T{h}"] + m
                    bank_free(n)
                    for k in range(KB):
                        last = three(ps[:, n % NB, :], gram(k, m, 0), gram(k, m, 1), w_hi[c % 2][:, k, :], w_lo[c % 2][:, k, :], k, KB - 1)
                    last.then_inc(s_full, 1)
                    for j in place_chunks(2 * h, m):
                        place_edges(j)
                for m in range(KB):
                    c = 3 * h + 1 + m // MB
                    if m % MB == 0:
                        chunk_ready(c)
                    n = first[f"KV{h}"] + m
                    bank_free(n)
                    col = (m % MB) * P
                    for k in range(KB):
                        if m == 0:
                            pe.wait_ge(*released(first[f"T{h}"] + k))
                        last = three(ps[:, n % NB, :], w_hi[c % 2][:, k, col:col + P], w_lo[c % 2][:, k, col:col + P],
                                     t_hi[:, k, :], t_lo[:, k, :], k, KB - 1)
                    last.then_inc(s_full, 1)
                    for j in place_chunks(2 * h + 1, m):
                        place_edges(j)

            def transposes(n, tile, g, w):
                for b in range(MB):
                    last = nc.tensor.transpose(ps[:, n % NB, b * P:b * P + w], tile[0:w, (MB * g + b) * P:(MB * g + b + 1) * P],
                                               ident[0:w, 0:w])
                last.then_inc(s_full, 1)

            for t in range(NT):
                pe.wait_ge(s_xn2, t + 1)
                for g in range(2):
                    n = first["XT"] + 2 * t + g
                    bank_free(n)
                    transposes(n, acc[:, t, :], g, ROWS[t])

            def nodes_times_chunk(c, name, start_job):
                for t in range(NT):
                    n, w = start_job + t, ROWS[t]
                    bank_free(n)
                    for k in range(KB):
                        if t == 0 and k % 2 == 0:
                            pe.wait_ge(s_wlo, UNITS * c + k // 2 + 1)
                        last = three(ps[0:w, n % NB, :], xt_hi[:, k, t * P:t * P + w], xt_lo[:, k, t * P:t * P + w],
                                     w_hi[c % 2][:, k, :], w_lo[c % 2][:, k, :], k, KB - 1)
                    last.then_inc(s_full, 1)

            pe.wait_ge(*released(first["XT"] + 2 * NT - 1))
            for h in range(NH):
                nodes_times_chunk(6 + 2 * h, "ql", first[f"QL{h}"])
                nodes_times_chunk(7 + 2 * h, "qr", first[f"QR{h}"])

            def q_transposes(t):
                pe.wait_ge(*released(first["QR1"] + t))
                for g in range(2):
                    n = qt_job(t, g)
                    bank_free(n)
                    transposes(n, acc[:, t, :], g, ROWS[t])

            q_transposes(0)
            for t in range(NT):
                if t + 1 < NT:
                    q_transposes(t + 1)
                w = ROWS[t]
                for h in range(NH):
                    n = mix_job(t, h)
                    bank_free(n)
                    if t == 0:
                        chunk_ready(C_KV + h)
                    pe.wait_ge(*released(qt_job(t, 1)))
                    for k in range(KB):
                        s = (2 * t + k // MB) % 3
                        last = three(ps[0:w, n % NB, :], qt_hi[:, s, k % MB, 0:w], qt_lo[:, s, k % MB, 0:w],
                                     w_hi[h][:, k, :], w_lo[h][:, k, :], k, KB - 1)
                    last.then_inc(s_full, 1)
            for h in range(NH):
                nodes_times_chunk(C_W + h, "h", first[f"H{h}"])
            for i in range(len(SCOLS)):
                n = first["AL"] + i
                bank_free(n)
                tiles = range(4 * i, min(NT, 4 * i + 4))
                for t in tiles:
                    pe.wait_ge(s_diag, t + 1)
                    last = nc.tensor.matmul(ps[:, n % NB, (t % 4) * P:(t % 4 + 1) * P], ones[:, :], diag[:, t, :], start=True, stop=True)
                last.then_inc(s_full, 1)
            for n in range(first["AL"] - 4, first["AL"] + len(SCOLS)):
                pe.wait_ge(*released(n))

            pe.wait_ge(s_nodes, 1)
            pe.sem_inc(s_hot_used, CK)
            for t in range(NT):
                a = 3 * (t % 2)
                if t >= 2:
                    pe.wait_ge(s_cnt, t - 1)
                for b, (c, w) in enumerate(SCOLS):
                    nc.tensor.matmul(ps[:, a + b, 0:w], zeros16[:, :], nodes16[:, c:c + w], start=True, stop=False)
                first_group, end = (pe.value_load(g_first[0:1, t + i:t + i + 1], min_val=i, max_val=NG) for i in range(2))
                with pe.Fori(first_group, end) as g:
                    for j in range(CK):
                        pe.wait_ge(s_hot, g * CK + (j + 1))
                        for b, (c, w) in enumerate(SCOLS):
                            last = nc.tensor.matmul(ps[:, a + b, 0:w], hot_d[:, j, :], hot_s[:, j, c:c + w],
                                                    start=False, stop=False)
                        last.then_inc(s_hot_used, 1)
                for b, (c, w) in enumerate(SCOLS):
                    last = nc.tensor.matmul(ps[:, a + b, 0:w], zeros16[:, :], nodes16[:, c:c + w], start=False, stop=True)
                last.then_inc(s_counted, 1)
            pe.wait_ge(s_cnt, NT)
            for t in range(NT + 3):
                if t < NT:
                    w = ROWS[t]
                    pe.wait_ge(s_attlo, t + 1)
                    if t == 0:
                        pe.wait_ge(s_hlo, NT)
                    n = gnn_job[t]
                    bank_free(n)
                    pe.wait_ge(s_sum, t + 1)
                    nc.tensor.matmul(ps[0:w, n % NB, 0:2], att_sum[:, t % 2, 0:w], ones[:, 0:2], start=True, stop=True).then_inc(s_full, 1)
                    for h in range(NH):
                        n = gnn_job[t] + 1 + h
                        bank_free(n)
                        for d in range(NT):
                            r = ROWS[d]
                            last = three(ps[0:w, n % NB, :], att_hi[0:r, t % 2, d, 0:w], att_lo[0:r, t % 2, d, 0:w],
                                         h_hi[0:r, d, h * HALF:(h + 1) * HALF], h_lo[0:r, d, h * HALF:(h + 1) * HALF], d, NT - 1)
                        last.then_inc(s_full, 1)
                if t >= 3:
                    i = t - 3
                    w = ROWS[i]
                    if i == 0:
                        pe.wait_ge(s_gw, 32)
                        pe.wait_ge(s_tab_done, 1)
                    pe.wait_ge(*released(tr_job[i] + 1))
                    for k in range(KB):
                        last = nc.tensor.matmul(ps[0:w, 7, i * NE:(i + 1) * NE], xg[:, i % 2, k, 0:w], gw[:, k, :],
                                                start=(k == 0), stop=(k == KB - 1))
                    last.then_inc(s_gate_used, 1)
                if 2 <= t < NT + 2:
                    i = t - 2
                    pe.wait_ge(s_xn2, NT + i + 1)
                    for g in range(2):
                        n = tr_job[i] + g
                        bank_free(n)
                        transposes(n, xn2[:, i % 2, :], g, ROWS[i])
            pe.wait_ge(s_gtot, 1)
            nc.tensor.matmul(ps[:, 7, 0:NE], tri2[:, :], g_tot[:, :], start=True, stop=True)
            nc.tensor.matmul(ps[:, 7, NE:2 * NE], ones[:, :], g_tot[:, :], start=True, stop=True).then_inc(s_gtotp, 1)
            for c in range(2):
                pe.wait_ge(s_toks, c + 1)
                for t in range(NT):
                    last = nc.tensor.matmul(ps[:, 7, 0:NSLOT], tok_r[:, c * NT + t, :], tok_c[:, c * NT + t, :],
                                            start=(t + c == 0), stop=(t == NT - 1 and c == 1))
            last.then_inc(s_tokp, 1)

            def block_transposes(g):
                for b in range(MB):
                    k = MB * g + b
                    last = nc.tensor.transpose(ps[:, 4 + g, b * P:(b + 1) * P], gx[:, k * P:(k + 1) * P], ident[:, :])
                last.then_inc(s_tr, 1)

            pe.wait_ge(s_route, 1)
            first_block = [pe.value_load(bounds[0:1, e:e + 1], min_val=0, max_val=NBLK) for e in range(NE + 1)]
            pe.wait_ge(s_gx, 16)
            for g in range(2):
                block_transposes(g)
            for e in range(NE):
                pe.wait_ge(s_elo, KB * (e + 1))
                with pe.Fori(first_block[e], first_block[e + 1]) as i:
                    for g in range(2):
                        pe.wait_ge(s_llo, i * 2 + (g + 1))
                        for h in range(NH):
                            c = slice(h * HALF, (h + 1) * HALF)
                            if g == 0:
                                pe.wait_ge(s_ye, i * 2 + (1 + h))
                            for k in range(MB * g, MB * g + MB):
                                last = three(ps[:, h, :], lt_hi[:, k, :], lt_lo[:, k, :], e_hi[e % 2][:, k, c], e_lo[e % 2][:, k, c],
                                             k, KB - 1)
                            if g == 1 or h == 1:
                                last.then_inc(s_mm, 1)
                        if g == 0:
                            pe.wait_ge(s_gx, i * 16 + 32)
                        block_transposes(g)


_INS = ["x", "src", "dst", "L0_gnn_W", "L0_gnn_a", "L0_mix_w_query_left", "L0_mix_w_query_right", "L0_mix_w_key",
        "L0_mix_w_value", "L0_ffn_gate_W", "L0_ffn_gate_b", "L0_ffn_expert_W", "L0_ffn_expert_b"]


def kernel(**inputs):
    import numpy as np
    import concourse.bacc as bacc
    from concourse.bass_utils import run_bass_kernel_spmd

    nc = bacc.Bacc("TRN2", target_bir_lowering=False, num_devices=1)
    arrays, args = {}, []
    for name in _INS:
        a = np.ascontiguousarray(inputs[name])
        arrays["in_" + name] = a
        args.append(nc.dram_tensor("in_" + name, a.shape, mybir.dt.from_np(a.dtype), kind="ExternalInput").ap())
    y = nc.dram_tensor("out_0", inputs["x"].shape, mybir.dt.float32, kind="ExternalOutput").ap()
    gps_layer(nc, *args, y)
    r = run_bass_kernel_spmd(nc, [arrays], core_ids=[0])
    return r.results[0]["out_0"]
```
